# Optimizing a Trainium2 kernel written in Bass

```python
import numpy as np
import jax
import jax.numpy as jnp

def _softmax(x, axis=-1):
    return jax.nn.softmax(x, axis=axis)

def _gelu(x):
    return jax.nn.gelu(x, approximate=True)

def _silu(x):
    return jax.nn.silu(x)

def _sigmoid(x):
    return jax.nn.sigmoid(x)

def _layernorm(x, axis=-1, eps=1e-05):
    m = jnp.mean(x, axis=axis, keepdims=True)
    v = jnp.var(x, axis=axis, keepdims=True)
    return (x - m) / jnp.sqrt(v + eps)

def _scatter_add(tgt, idx, src, axis=0):
    return tgt.at[idx].add(src)

def _segment_sum(src, seg, n):
    return jax.ops.segment_sum(src, seg, n)
kernel_name = 'mk_vit_tower_d1_tok_img2048_r4_a6f3b7'

def setup_inputs(seed: int=0):
    np.random.seed(seed)
    _w = jnp.asarray

    def _rec_inputs():
        import jax
        import jax.numpy as jnp
        _rk = jax.random.key(seed)
        x = -0.00286756 + 0.998052 * jax.random.normal(jax.random.fold_in(_rk, 1), (16, 192, 64, 2), jnp.float32)
        return x
    x = _rec_inputs()

    def _L0_tok_setup():
        import jax, jax.numpy as jnp
        import numpy as np
        H = 192
        N = 64
        CH = 1
        NSSM = 192
        L_VAL = 512
        key = jax.random.key(seed)
        k_dt, k_C = jax.random.split(key, 2)
        log_dt = np.log(0.001) + jax.random.uniform(k_dt, (H,), dtype=jnp.float32) * (np.log(0.1) - np.log(0.001))
        B_ri = jnp.concatenate([jnp.ones((NSSM, N, 1), jnp.float32), jnp.zeros((NSSM, N, 1), jnp.float32)], axis=-1)
        inv_A_real = jnp.full((NSSM, N), np.log(0.5), dtype=jnp.float32)
        A_imag = jnp.tile(np.pi * jnp.arange(N, dtype=jnp.float32)[None, :], (NSSM, 1))
        C_ri = jax.random.normal(k_C, (CH, H, N, 2), dtype=jnp.float32)
        return {'log_dt': log_dt, 'B_ri': B_ri, 'inv_A_real': inv_A_real, 'A_imag': A_imag, 'C_ri': C_ri, 'L': L_VAL}
    _L0_tok_all = _L0_tok_setup()
    _L0_tok_in = {k: v for k, v in _L0_tok_all.items() if k in ('log_dt', 'B_ri', 'inv_A_real', 'A_imag')}
    del _L0_tok_all

    def _L0_attn_setup():
        import jax, jax.numpy as jnp
        import numpy as np
        B, S, HID = (1, 1024, 512)
        NH, NKV, D = (16, 4, 128)
        QPG = NH // NKV
        GROUP = (QPG + 2) * D
        TOTAL = NKV * GROUP
        key = jax.random.key(seed)
        k0, k1, k2 = jax.random.split(key, 3)
        x = jax.random.normal(k0, (B, S, HID), dtype=jnp.float32)
        weight_qkv = jax.random.normal(k1, (TOTAL, HID), dtype=jnp.float32) * 0.02
        weight_proj = jax.random.normal(k2, (HID, NH * D), dtype=jnp.float32) * 0.02
        return {'x': x, 'weight_qkv': weight_qkv, 'weight_proj': weight_proj}
    _L0_attn_all = _L0_attn_setup()
    _L0_attn_in = {k: v for k, v in _L0_attn_all.items() if k in ('weight_qkv', 'weight_proj')}
    del _L0_attn_all

    def _L0_ffn_setup():
        import jax, jax.numpy as jnp
        import numpy as np
        TOP_K = 8
        key = jax.random.key(seed)
        k1, k2, k3 = jax.random.split(key, 3)
        B, S, H, E = (4, 1024, 512, 64)
        hidden_states = jax.random.normal(k1, (B, S, H), dtype=jnp.float32)
        router_weight = jax.random.normal(k2, (E, H), dtype=jnp.float32)
        router_bias = jnp.zeros((E,), dtype=jnp.float32)
        expert_bias = jax.random.normal(k3, (E, H), dtype=jnp.float32) * 0.1
        return {'hidden_states': hidden_states, 'router_weight': router_weight, 'router_bias': router_bias, 'expert_bias': expert_bias}
    _L0_ffn_all = _L0_ffn_setup()
    _L0_ffn_in = {k: v for k, v in _L0_ffn_all.items() if k in ('router_weight', 'router_bias', 'expert_bias')}
    del _L0_ffn_all
    return {'x': x, 'L0_tok_log_dt': _L0_tok_in['log_dt'], 'L0_tok_B_ri': _L0_tok_in['B_ri'], 'L0_tok_inv_A_real': _L0_tok_in['inv_A_real'], 'L0_tok_A_imag': _L0_tok_in['A_imag'], 'L0_attn_weight_qkv': _L0_attn_in['weight_qkv'], 'L0_attn_weight_proj': _L0_attn_in['weight_proj'], 'L0_ffn_router_weight': _L0_ffn_in['router_weight'], 'L0_ffn_router_bias': _L0_ffn_in['router_bias'], 'L0_ffn_expert_bias': _L0_ffn_in['expert_bias']}

def reference(x, L0_tok_log_dt, L0_tok_B_ri, L0_tok_inv_A_real, L0_tok_A_imag, L0_attn_weight_qkv, L0_attn_weight_proj, L0_ffn_router_weight, L0_ffn_router_bias, L0_ffn_expert_bias):
    import jax
    import jax.numpy as jnp

    def _L0_tok_ref(log_dt, B_ri, inv_A_real, A_imag, C_ri, L):
        import jax, jax.numpy as jnp
        import numpy as np
        H = 192
        N = 64
        CH = 1
        NSSM = 192
        L_VAL = 512
        dt = jnp.exp(log_dt)
        A = -jnp.exp(inv_A_real) + 1j * A_imag
        rep = H // A.shape[0]
        A = jnp.tile(A, (rep, 1))
        B = B_ri[..., 0] + 1j * B_ri[..., 1]
        B = jnp.tile(B, (rep, 1))[None]
        C = C_ri[..., 0] + 1j * C_ri[..., 1]
        C = (B[:, None, :, :] * C).reshape(-1, H, N)
        dtA = A * dt[:, None]
        C = C * (jnp.exp(dtA) - 1.0) / A
        ell = jnp.arange(L, dtype=jnp.float32)
        V = jnp.exp(dtA[:, :, None] * ell)
        K = 2.0 * jnp.einsum('chn,hnl->chl', C, V).real
        return K.astype(jnp.float32)

    def _L0_attn_ref(x, weight_qkv, weight_proj):
        import jax, jax.numpy as jnp
        import numpy as np
        B, S, HID = (1, 1024, 512)
        NH, NKV, D = (16, 4, 128)
        QPG = NH // NKV
        GROUP = (QPG + 2) * D
        TOTAL = NKV * GROUP
        b, s, _ = x.shape
        qkv = jnp.einsum('bsh,ph->bsp', x, weight_qkv).reshape(b, s, NKV, GROUP)
        q = qkv[..., :QPG * D].reshape(b, s, NKV, QPG, D)
        k = qkv[..., QPG * D:(QPG + 1) * D]
        v = qkv[..., (QPG + 1) * D:]
        scale = 1.0 / jnp.sqrt(jnp.float32(D))
        scores = jnp.einsum('bsgqd,btgd->bgqst', q, k) * scale
        causal = jnp.tril(jnp.ones((s, s), dtype=bool))
        scores = jnp.where(causal, scores, jnp.finfo(scores.dtype).min)
        attn = jax.nn.softmax(scores, axis=-1)
        out = jnp.einsum('bgqst,btgd->bsgqd', attn, v)
        out = out.reshape(b, s, NH * D)
        return jnp.einsum('bse,he->bsh', out, weight_proj)

    def _L0_ffn_ref(hidden_states, router_weight, router_bias, expert_bias):
        import jax, jax.numpy as jnp
        import numpy as np
        TOP_K = 8
        B, S, H = hidden_states.shape
        flat = hidden_states.reshape(B * S, H)
        logits = jnp.einsum('th,eh->te', flat, router_weight) + router_bias
        scores = jax.nn.softmax(logits, axis=-1)
        topk_w, topk_idx = jax.lax.top_k(scores, TOP_K)
        gathered_bias = expert_bias[topk_idx]
        out = flat * jnp.sum(topk_w, axis=-1, keepdims=True) + jnp.einsum('tk,tkh->th', topk_w, gathered_bias)
        return out.reshape(B, S, H)
    h = _L0_tok_ref(L0_tok_log_dt, L0_tok_B_ri, L0_tok_inv_A_real, L0_tok_A_imag, x, 512)
    h = h + _L0_attn_ref(_layernorm(h, axis=-1), L0_attn_weight_qkv, L0_attn_weight_proj)
    h = h + _L0_ffn_ref(_layernorm(h, axis=-1), L0_ffn_router_weight, L0_ffn_router_bias, L0_ffn_expert_bias)
    return h

_drawn_inputs = setup_inputs


def setup_inputs(seed=0):
    import zlib

    import numpy as np

    out = dict(_drawn_inputs(seed))
    spreads = {'L0_tok_inv_A_real': (-0.6931471824645996, 0.2), 'L0_ffn_router_bias': (0.0, 2.0)}
    factors = {}
    for name, (base, spread) in spreads.items():
        noise = np.random.default_rng([zlib.crc32(name.encode()), seed]).standard_normal(out[name].shape)
        drawn = base * np.exp(spread * noise) if base else spread * noise
        out[name] = jnp.asarray(drawn.astype(out[name].dtype))
    for name, factor in factors.items():
        out[name] = (out[name] * factor).astype(out[name].dtype)
    return out
```

```python
from contextlib import ExitStack

import numpy as np

import concourse.bass as bass
from concourse import mybir

F32 = mybir.dt.float32
F16 = mybir.dt.float16
I32 = mybir.dt.int32
ALU = mybir.AluOpType
ACT = mybir.ActivationFunctionType
AX_X = mybir.AxisListType.X
RMAX = bass.bass_isa.ReduceOp.max

P = 128
BATCH, SEQ, MODES = 16, 192, 64
HID = 512
NKV, QPG, D = 4, 4, 128
NH = NKV * QPG
GROUP = QPG + 2
KT = HID // P
PAIRS = BATCH // 2
PT = 2 * SEQ
TT = PT // P
S0, S1 = P, SEQ - P
EXPERTS, TOP_K = 64, 8
EPS = 1e-5

NK_, NJ, NA = 16, 8, HID // P
NTAB = NK_ + NJ + NA
HHALF = SEQ // 2

X_SCALE = 2.0 ** 10
W_SCALE = 2.0 ** 14
QKV_STORE = 2.0 ** 9
P_SCALE = 2.0 ** 14
QKV_EVAC = QKV_STORE / (X_SCALE * W_SCALE)
OUT_EVAC = 1.0 / P_SCALE
NORM_FLOOR = 2.0 ** -60

MASKED = -1e30
ROUND = 1.5 * 2.0 ** 23
TWO_PI = 6.283185
LOG2E = 1.4426950408889634
LN2_HI, LN2_LO = 0.693145751953125, 1.4286068203094172e-06
INV_2PI = 0.15915494309189535

C_ID, C_M0, C_M1 = 0, P, 2 * P
C_L = C_M1 + SEQ
C_OFF = C_L + NTAB
C_HALF = C_OFF + NTAB
NCONST = C_HALF + 3


def shape_constants():
    c = np.zeros((P, NCONST), np.float32)
    p, s = np.arange(P)[:, None], np.arange(SEQ)[None, :]
    c[:, C_ID:C_ID + P] = np.eye(P)
    c[:, C_M0:C_M0 + P] = np.where(s[:, :P] <= p, 0.0, MASKED)
    c[:, C_M1:C_M1 + SEQ] = np.where(s <= S0 + p % S1, 0.0, MASKED)
    c[:, C_L:C_L + NTAB] = [*range(NK_), *range(0, P, NK_), *range(0, HID, P)]
    imag = p >= MODES
    c[:, C_OFF:C_OFF + NK_] = np.where(imag, -0.25, 0.0)
    c[:, C_OFF + NK_ + NJ:C_OFF + NTAB] = np.where(imag, 0.25, 0.0)
    c[:, C_HALF:] = -0.5
    return c


RING = 5


def slot_tasks(g, prev, nxt):
    out = [("S", g, b, r) for b in range(2) for r in range(2)]
    if g < NKV - 1 or nxt:
        out += [("A", g + 1, j) for j in range(QPG + 1)]
    if g == 0:
        out += [("V", t) for t in range(TT)]
    out += [("T", g, i) for i in range(4)]
    if g == 2 and prev:
        out += [("Z", j) for j in range(TT)]
    if g == 3 and prev:
        out += [("WT",)]
    out += [("D", g, b, r) for b in range(2) for r in range(2)]
    if g == 1 and nxt:
        out += [("HX", j) for j in range(TT)]
    if g == 2 and prev:
        out += [("LG",)]
    if g == 2 and nxt:
        out += [("XX", j) for j in range(TT)]
    if g == 3 and prev:
        out += [("EB", j) for j in range(TT)]
    return out


def body_tasks(prev, nxt):
    return [t for g in range(NKV) for t in slot_tasks(g, prev, nxt)]


TASKS = {
    "lead": [("HX", j) for j in range(TT)] + [("XX", j) for j in range(TT)] + [("A", 0, j) for j in range(QPG + 1)],
    "first": body_tasks(False, True),
    "mid": body_tasks(True, True),
    "last": body_tasks(True, False),
    "tail": [("Z", j) for j in range(TT)] + [("LG",), ("WT",)] + [("EB", j) for j in range(TT)],
}
SEGMENTS = list(TASKS)
ON_SCALAR = ("A", "V", "T", "D", "HX", "XX")
INDEX = {seg: {t: i for i, t in enumerate(ts)} for seg, ts in TASKS.items()}
SCALAR_INDEX = {seg: {t: i for i, t in enumerate([t for t in ts if t[0] in ON_SCALAR])} for seg, ts in TASKS.items()}


class Where:

    def __init__(self, seg, p):
        self.seg, self.p = seg, p
        self.prev = seg in ("mid", "last")
        self.next = seg in ("first", "mid")


class Signal:

    def __init__(self, sem, lead=0, first=0, mid=0, last=0, tail=0):
        self.sem = sem
        self.n = dict(lead=lead, first=first, mid=mid, last=last, tail=tail)

    def at(self, w, k):
        n, i = self.n, SEGMENTS.index(w.seg)
        before = sum(n[s] * (PAIRS - 2 if s == "mid" else 1) for s in SEGMENTS[:i])
        if w.seg != "mid":
            return before + k
        return w.p * n["mid"] + (before - n["mid"] + k)


def count(f):
    return {seg: f(seg) for seg in SEGMENTS}


def await_(eng, signal, w, k):
    v = signal.at(w, k)
    if not (isinstance(v, int) and v <= 0):
        eng.wait_ge(signal.sem, v)


def await_apart(eng, signal, w, k, spare):
    await_(eng, signal, w, k)
    if not isinstance(w.p, int):
        eng.sem_inc(spare, 1)


def vit_tower(nc, x, log_dt, b_ri, inv_a_real, a_imag, w_qkv, w_proj, r_weight, r_bias, e_bias, const, out):
    with ExitStack() as ctx:
        def sb(name, shape, dt=F32, c=ctx):
            return c.enter_context(nc.sbuf_tensor(name, shape, dt))

        def sem(name):
            return ctx.enter_context(nc.semaphore(name))

        ht_dram = nc.dram_tensor("h_transposed", (P, KT, BATCH * SEQ), F32, kind="Internal").ap()
        h_dram = nc.dram_tensor("h_tokens", (BATCH * SEQ, HID), F32, kind="Internal").ap()
        out_rows = out.rearrange("c s l -> (c s) l")

        bank = [ctx.enter_context(nc.psum_tensor(f"bank{i}", [P, 512], F32)) for i in range(8)]
        ring_bank, acc = bank[:RING], bank[RING:]

        wq = sb("wq", [P, NKV * GROUP, 2, KT, P], F16)
        wp = sb("wp", [P, KT, NH, 2, P], F16)
        cst = sb("cst", [P, NCONST])
        ident = cst[:, C_ID:C_ID + P]
        mask0, mask1 = cst[:, C_M0:C_M0 + P], cst[:, C_M1:C_M1 + SEQ]
        rwT = sb("rwT", [P, KT, EXPERTS])
        eb = sb("eb", [EXPERTS, HID])
        rb = sb("rb", [P, EXPERTS])
        sq = sb("sq", [P, 48])
        wsc = sb("wsc", [P, 24])
        s_q, s_p = wsc[:, 6:7], wsc[:, 7:8]
        alpha, beta = wsc[:, 8:9], wsc[:, 10:11]

        one = ExitStack()
        G = sb("G", [P, 2, BATCH, SEQ], c=one)
        ht = sb("ht", [P, NA, BATCH, 64], c=one)
        x_a = ht[0:HHALF, :, :, :].rearrange("p a c h -> p (a c h)").rearrange("p (c s d m) -> p c s d m", c=BATCH // 2, s=2, d=2)
        tab = sb("tab", [P, 4, 64, NTAB], c=one)
        Tp, Te, Ts, Tc = (tab[:, i] for i in range(4))
        pf = sb("pf", [P, 2, 64, NA], c=one)
        pg = sb("pg", [P, 2, 64, NA], c=one)
        ur = sb("ur", [P, SEQ], c=one)
        re = sb("re", [P, SEQ], c=one)
        fr = sb("fr", [P, SEQ], c=one)
        fi = sb("fi", [P, SEQ], c=one)
        junk = sb("junk", [P, 1024], F16, c=one)
        r_in = sb("r_in", [EXPERTS, HID], c=one)
        par = ExitStack()
        x_b = sb("x_b", [HHALF, BATCH // 2, 2, 2, 2 * MODES], c=par)
        par_in = sb("par_in", [HHALF, 2, 2, 2, MODES], c=par)
        b_in = sb("b_in", [HHALF, 2, 2, 2 * MODES], c=par)
        el = sb("el", [P, 2, SEQ], c=par)
        ev = sb("ev", [P, 4, 2, SEQ], c=par)
        pw = sb("pw", [P, 15, SEQ], c=par)
        par.close()
        Q = sb("Q", [P, 2, 16, NJ, NK_], c=one)
        QB = sb("QB", [P, 16, NJ, NK_], c=one)
        CP = sb("CP", [P, 2, 16, NA, BATCH], c=one)
        CB = sb("CB", [P, 16, NA, BATCH], c=one)
        one.close()

        htin = sb("htin", [P, KT, PT])
        H = sb("H", [P, TT, HID])
        Hr = sb("Hr", [P, TT, HID])
        xn = sb("xn", [P, TT, HID])
        xT = sb("xT", [P, 2, KT, PT], F16)
        stat = sb("stat", [P, 2, TT, 8])
        mv = sb("mv", [P, 2, TT, 2])
        rstd = sb("rstd", [P, 2, 2, TT])
        qT = sb("qT", [P, 2, 2, QPG * SEQ], F16)
        kT = sb("kT", [P, 2, 2, SEQ], F16)
        V = sb("V", [P, 2, TT, NKV * D], F16)
        P0 = sb("P0", [P, 2, QPG, S0])
        P1 = sb("P1", [P, 2, 2, SEQ])
        P2 = sb("P2", [P, 2, 2, S1])
        mx = sb("mx", [P, 2, 6])
        nmx = sb("nmx", [P, 2, 6])
        sums = sb("sums", [P, 2, 6])
        rec = sb("rec", [P, 2, 6])
        PT0 = sb("PT0", [P, 2, 2, QPG, SEQ], F16)
        PT1 = sb("PT1", [P, 2, QPG, S1], F16)
        oT = sb("oT", [P, 2, QPG, PT], F16)
        h2 = sb("h2", [P, TT, HID])
        z = sb("z", [P, TT, HID])
        zT = sb("zT", [P, TT, KT, P])
        lg = sb("lg", [P, 4, TT, EXPERTS])
        small = sb("small", [P, 4, TT])
        top = sb("top", [P, TT, 8])
        wT = sb("wT", [EXPERTS, TT, P])

        const_in, par_loaded, x_loaded = sem("const_in"), sem("par_loaded"), [sem("x_a_loaded"), sem("x_b_loaded")]
        wq_loaded, wp_loaded, r_loaded = sem("wq_loaded"), sem("wp_loaded"), sem("r_loaded")
        a_full, a_free = sem("a_full"), sem("a_free")
        b_full, b_hi, b_free = sem("b_full"), sem("b_hi"), sem("b_free")
        dve1 = sem("dve1")
        pool1 = sem("pool1")
        act1 = sem("act1")
        trig_in, trig = sem("trig_in"), sem("trig")
        squares, norm_max, scales = sem("squares"), sem("norm_max"), sem("scales")
        decay_arg, decay, phase, waves, cosine = (sem(s) for s in ("decay_arg", "decay", "phase", "waves", "cosine"))
        tables, partial, qcp, ht_stored = (sem(s) for s in ("tables", "partial", "qcp", "ht_stored"))
        qcp_used = sem("qcp_used")

        ntask = count(lambda s: len(TASKS[s]))
        nscalar = count(lambda s: len(SCALAR_INDEX[s]))
        units = dict(first=8, mid=8, last=8)
        full = Signal(sem("full"), **ntask)
        free = Signal(sem("free"), **ntask)
        part_hi = Signal(sem("part_hi"), **nscalar)
        row_max = Signal(sem("row_max"), **units)
        neg_max = Signal(sem("neg_max"), **units)
        exps = Signal(sem("exps"), **units)
        recips = Signal(sem("recips"), **units)
        probs = Signal(sem("probs"), **units)
        nx = dict(lead=1, first=1, mid=1)
        pv = dict(mid=1, last=1, tail=1)
        three = lambda d: {k: TT * v for k, v in d.items()}
        x_var, x_rstd = Signal(sem("x_var"), **nx), Signal(sem("x_rstd"), **nx)
        xn_ready = Signal(sem("xn_ready"), **three(nx))
        ht_in = Signal(sem("ht_in"), lead=16, first=16, mid=16)
        h_out = Signal(sem("h_out"), lead=16, first=16, mid=16)
        hr_in = Signal(sem("hr_in"), first=16, mid=16, last=16)
        acc_full = Signal(sem("acc_full"), **three(pv))
        acc_free = Signal(sem("acc_free"), **three(pv))
        f_var, f_rstd = Signal(sem("f_var"), **pv), Signal(sem("f_rstd"), **pv)
        z_ready = Signal(sem("z_ready"), **three(pv))
        lg_in, lg_exp = Signal(sem("lg_in"), **pv), Signal(sem("lg_exp"), **pv)
        w_ready, out_ready = Signal(sem("w_ready"), **pv), Signal(sem("out_ready"), **pv)
        out_stored = Signal(sem("out_stored"), mid=16, last=16, tail=16)
        x_steps, f_steps = 1, 11
        vec = Signal(sem("vec"), lead=x_steps, first=x_steps, mid=x_steps + f_steps, last=f_steps, tail=f_steps)

        pe_passed, dve_passed = sem("pe_passed"), sem("dve_passed")

        block = ctx.enter_context(nc.Block())

        LEAD, FIRST, LAST, TAIL = Where("lead", 0), Where("first", 0), Where("last", PAIRS - 1), Where("tail", PAIRS)

        def bodies(eng, lead, body, tail):
            lead(LEAD)
            body(FIRST)
            with eng.Fori(1, PAIRS - 1) as p:
                body(Where("mid", p))
            body(LAST)
            tail(TAIL)

        CH, NCH, CPG = 16, SEQ // 16, 4
        NG = NCH // CPG
        GT = 2 + 2 * BATCH // 2
        W_TASKS = [("q", j) for j in range(NKV * GROUP)] + [("p", j, e) for j in range(KT) for e in range(0, NH, 4)]
        W_FROM = 2
        def w_tasks(c):
            n = -(-len(W_TASKS) // (NCH - W_FROM))
            return range(min(len(W_TASKS), (c - W_FROM) * n), min(len(W_TASKS), (c - W_FROM + 1) * n)) if c >= W_FROM else range(0)

        def head_pieces(part, j):
            if j < QPG:
                first = qT[:, part, :, j * S0:(j + 1) * S0]
                rest = qT[:, part, :, QPG * S0 + j * S1:QPG * S0 + (j + 1) * S1]
            else:
                first, rest = kT[:, part, :, 0:S0], kT[:, part, :, S0:SEQ]
            return [(first, lambda b: b[:, 0:2 * S0].rearrange("p (b s) -> p b s", b=2)),
                    (rest, lambda b: b[:, 2 * S0:PT].rearrange("p (b s) -> p b s", b=2))]

        def token_pieces(part, j):
            def piece(at, start, n):
                return (xT[:, part, :, at:at + n], lambda b: b[:, :].rearrange("p (k s) -> p k s", k=KT)[:, :, start:start + n])
            if j == 0:
                return [piece(0, 0, P)]
            if j == 1:
                return [piece(2 * S0, 0, S1), piece(S0, S1, P - S1)]
            return [piece(S0 + P - S1, 0, S1), piece(2 * S0 + S1, S1, S1)]

        def probs_out(part, i):
            if i < 2:
                return PT0[:, part, i, :, 0:S0]
            if i == 2:
                return PT0[:, part].rearrange("p b h s -> p (b h) s")[:, :, S0:SEQ]
            return PT1[:, part, :, :]

        def probs_in(b, i):
            if i < 2:
                return b[:, :].rearrange("p (h s) -> p h s", h=QPG)
            if i == 2:
                return b[:, :].rearrange("p (h s) -> p h s", h=2 * QPG)
            return b[:, 0:2 * P].rearrange("p (h s) -> p h s", h=QPG)

        def j_of(t, hs):
            return t[:, hs, NK_:NK_ + NJ].unsqueeze(3).broadcast_to([P, CH, NJ, NK_])

        def k_of(t, hs):
            return t[:, hs, 0:NK_].unsqueeze(2).broadcast_to([P, CH, NJ, NK_])

        def g_of(r, c):
            return G[:, r, :, CH * c:CH * (c + 1)].rearrange("p c h -> p h c").unsqueeze(2).broadcast_to([P, CH, NA, BATCH])

        def a_of(r, hs):
            return pf[:, r, hs, :].unsqueeze(3).broadcast_to([P, CH, NA, BATCH])

        @block.sync
        def _(sp):
            sp.dma_start(cst[:, :], const).then_inc(const_in, 16)
            for d in range(2):
                for i, src in enumerate((a_imag, inv_a_real)):
                    sp.dma_start(par_in[:, :, i, d, :], src.rearrange("(s p) n -> p s n", p=HHALF)).then_inc(par_loaded, 16)
                sp.dma_start(b_in[:, :, d, :], b_ri.rearrange("(s p) n r -> p s (n r)", p=HHALF)).then_inc(par_loaded, 16)
            sp.dma_start(el[:, 0, :], log_dt.rearrange("(o h) -> o h", o=1).broadcast_to([P, SEQ])).then_inc(par_loaded, 16)
            x_rows = x.rearrange("c (s p) n r -> p c s (n r)", p=HHALF)
            for half, dst in enumerate((x_a, x_b)):
                for d in range(2):
                    sp.dma_start(dst[:, :, :, d, :], x_rows[:, half * (BATCH // 2):(half + 1) * (BATCH // 2)]).then_inc(x_loaded[half], 16)
            sp.dma_start(wq[:, :, :, :, :].rearrange("p j a k d -> p j (a k d)").bitcast(F32),
                         w_qkv.rearrange("(j p) l -> p j l", p=P)).then_inc(wq_loaded, 16)
            sp.dma_start(wp[:, :, :, :, :].rearrange("p j h a d -> p j (h a d)").bitcast(F32),
                         w_proj.rearrange("(j p) e -> p j e", p=P)).then_inc(wp_loaded, 16)
            sp.dma_start(r_in[:, :], r_weight).then_inc(r_loaded, 16)
            sp.dma_start(eb[:, :], e_bias).then_inc(r_loaded, 16)
            sp.dma_start(rb[:, :], r_bias.rearrange("(o h) -> o h", o=1).broadcast_to([P, EXPERTS])).then_inc(r_loaded, 16)
            for g in range(NG):
                sp.wait_ge(a_free, GT + 2 * CPG * (g + 1))
                sp.dma_start(ht_dram.rearrange("p a (c h) -> p a c h", c=BATCH)[:, :, :, 64 * g:64 * (g + 1)],
                             ht[:, :, :, :]).then_inc(ht_stored, 16)

            def load_ht(w, q):
                sp.dma_start(htin[:, :, :], ht_dram[:, :, bass.ds(q * PT, PT)]).then_inc(ht_in.sem, 16)

            def store_h(w, q):
                await_(sp, part_hi, w, SCALAR_INDEX[w.seg][("HX", TT - 1)] + 1)
                sp.dma_start(h_dram[bass.ds(q * PT, PT), :].rearrange("(t p) l -> p t l", p=P),
                             H[:, :, :]).then_inc(h_out.sem, 16)

            def lead(w):
                sp.wait_ge(ht_stored, 16 * NG)
                load_ht(w, 0)
                store_h(w, 0)

            def body(w):
                if w.next:
                    if w.seg == "mid":
                        await_(sp, full, w, INDEX["mid"][("HX", TT - 1)] + 1 - len(TASKS["mid"]))
                    else:
                        await_(sp, full, LEAD, INDEX["lead"][("HX", TT - 1)] + 1)
                    load_ht(w, w.p + 1)
                if w.prev:
                    await_(sp, acc_free, w, TT)
                await_(sp, h_out, w, 0)
                sp.dma_start(Hr[:, :, :], h_dram[bass.ds(w.p * PT, PT), :].rearrange("(t p) l -> p t l", p=P)).then_inc(hr_in.sem, 16)
                if w.next:
                    store_h(w, w.p + 1)
                if w.prev:
                    store_out(w, w.p - 1)

            def store_out(w, q):
                await_(sp, out_ready, w, 1)
                sp.dma_start(out_rows[bass.ds(q * PT, PT), :].rearrange("(t p) l -> p t l", p=P),
                             z[:, :, :]).then_inc(out_stored.sem, 16)

            def tail(w):
                store_out(w, PAIRS - 1)
                await_(sp, out_stored, w, 16)
                await_(sp, h_out, w, 0)

            bodies(sp, lead, body, tail)

        @block.tensor
        def _(pe):
            pe.wait_ge(const_in, 16)
            na, nb = [0], [0]

            def bank_a():
                if na[0] >= 4:
                    pe.wait_ge(a_free, na[0] - 3)
                na[0] += 1
                return bank[(na[0] - 1) % 4]

            def bank_b():
                if nb[0] >= 4:
                    pe.wait_ge(b_free, nb[0] - 3)
                nb[0] += 1
                return bank[4 + (nb[0] - 1) % 4]

            pe.wait_ge(par_loaded, 16 * 7)
            for i in range(2):
                b = bank_a()
                for k in range(2):
                    for s in range(2):
                        if i == 0:
                            src = par_in[:, s, k, :, :].rearrange("p d n -> p (d n)")
                        else:
                            src = b_in[:, s, :, :].rearrange("p d n -> p (d n)")[:, k::2]
                        mm = pe.transpose(b[:, (2 * k + s) * HHALF:(2 * k + s + 1) * HHALF], src, ident[0:HHALF, 0:HHALF])
                mm.then_inc(a_full, 1)
            for c in range(0, BATCH, 2):
                xs, c0 = (x_a, 0) if c < BATCH // 2 else (x_b, BATCH // 2)
                if c == c0:
                    pe.wait_ge(x_loaded[bool(c0)], 32)
                for r in range(2):
                    b = bank_a()
                    for k in range(2):
                        for s in range(2):
                            src = xs[:, c - c0 + k, s, :, :].rearrange("p d m -> p (d m)")[:, r::2]
                            mm = pe.transpose(b[:, (2 * k + s) * HHALF:(2 * k + s + 1) * HHALF], src, ident[0:HHALF, 0:HHALF])
                    mm.then_inc(a_full, 1)
            for c in range(NCH):
                pe.wait_ge(qcp, c + 1)
                for half in range(2):
                    b = bank_a()
                    for h in range(8):
                        i = 8 * half + h
                        mm = pe.matmul(b[:, 64 * h:64 * h + 64], Q[:, c % 2, i].rearrange("p j k -> p (j k)"),
                                       CP[:, c % 2, i].rearrange("p a c -> p (a c)"), start=True, stop=True)
                    mm.then_inc(a_full, 1)
                for t in w_tasks(c):
                    task = W_TASKS[t]
                    if t == 0:
                        pe.wait_ge(wq_loaded, 16)
                    if task[0] == "p" and W_TASKS[t - 1][0] == "q":
                        pe.wait_ge(wp_loaded, 16)
                    b = bank_b()
                    if task[0] == "q":
                        src = wq[:, task[1]].rearrange("p a k d -> p (a k d)").bitcast(F32)
                    else:
                        src = wp[:, task[1], task[2]:task[2] + 4].rearrange("p h a d -> p (h a d)").bitcast(F32)
                    for k in range(4):
                        mm = pe.transpose(b[:, k * P:(k + 1) * P], src[:, k * P:(k + 1) * P], ident)
                    mm.then_inc(b_full, 1)
            pe.wait_ge(r_loaded, 48)
            b = bank_b()
            for k in range(KT):
                mm = pe.transpose(b[:, k * EXPERTS:(k + 1) * EXPERTS], r_in[:, k * P:(k + 1) * P], ident[0:EXPERTS, 0:EXPERTS])
            mm.then_inc(b_full, 1)
            pe.wait_ge(a_free, GT + 2 * NCH)
            pe.wait_ge(b_free, len(W_TASKS) + 1)

            def take(w, task):
                i = INDEX[w.seg][task]
                await_(pe, free, w, i + 1 - RING)
                return ring_bank[(ring_start(w) + i) % RING]

            def ready(w, task):
                await_(pe, free, w, INDEX[w.seg][task] + 1)

            def split_product(b, pairs_, rhs_of, lhs_of, last=True):
                n = len(pairs_)
                for i, t in enumerate(pairs_):
                    for c, (l, r) in enumerate(((0, 0), (0, 1), (1, 0))):
                        mm = pe.matmul(b, lhs_of(t, l), rhs_of(t, r), start=(i == 0 and c == 0),
                                       stop=(last and i == n - 1 and c == 2))
                return mm

            def hx(w):
                await_(pe, ht_in, w, 16)
                for j in range(TT):
                    b = take(w, ("HX", j))
                    for k in range(KT):
                        mm = pe.transpose(b[:, k * P:(k + 1) * P], htin[:, k, j * P:(j + 1) * P], ident)
                    mm.then_inc(full.sem, 1)

            def xx(w):
                for j in range(TT):
                    await_(pe, xn_ready, w, j + 1)
                    b = take(w, ("XX", j))
                    for k in range(KT):
                        mm = pe.transpose(b[:, k * P:(k + 1) * P], xn[:, j, k * P:(k + 1) * P], ident)
                    mm.then_inc(full.sem, 1)

            def project(w, u, x_task):
                if x_task is not None:
                    ready(*x_task)
                for j in range(QPG + 1):
                    b = take(w, ("A", u, j))
                    row = GROUP * (u % NKV) + j
                    split_product(b[:, 0:PT], range(KT), lambda t, r: xT[:, r, t, :],
                                  lambda t, l: wq[:, row, l, t, :]).then_inc(full.sem, 1)

            def values(w):
                for t in range(TT):
                    b = take(w, ("V", t))
                    split_product(b[:, :], range(KT), lambda k, r: wq[:, QPG + 1::GROUP, r, k, :],
                                  lambda k, l: xT[:, l, k, t * P:(t + 1) * P]).then_inc(full.sem, 1)

            def turn_probs(w, g):
                for b2 in range(2):
                    await_(pe, probs, w, 2 * g + b2 + 1)
                    b = take(w, ("T", g, b2))
                    for h in range(QPG):
                        mm = pe.transpose(b[:, h * P:(h + 1) * P], P0[:, b2, h, :], ident)
                    mm.then_inc(full.sem, 1)
                b = take(w, ("T", g, 2))
                for b2 in range(2):
                    for r2 in range(2):
                        mm = pe.transpose(b[:, (2 * b2 + r2) * P:(2 * b2 + r2 + 1) * P], P1[:, r2, b2, 0:S0], ident)
                mm.then_inc(full.sem, 1)
                b = take(w, ("T", g, 3))
                for r2 in range(2):
                    mm = pe.transpose(b[:, r2 * P:(r2 + 1) * P], P2[:, r2, :, :].rearrange("p b s -> p (b s)"), ident)
                mm.then_inc(full.sem, 1)

            def attend(w, g):
                ready(w, ("T", g, 3))
                if g == 0:
                    ready(w, ("V", TT - 1))
                for b2 in range(2):
                    for r2 in range(2):
                        b = take(w, ("D", g, b2, r2))
                        split_product(b[:, 0:PT], range(1), lambda t, r: PT0[:, r, b2, 2 * r2:2 * r2 + 2, :],
                                      lambda t, l: V[:, l, b2, g * D:(g + 1) * D], last=False)
                        tail_rows = b[:, 0:PT].rearrange("p (h s) -> p h s", h=2)[:, :, S0:SEQ]
                        half = slice(b2 * S1, (b2 + 1) * S1)
                        for c, (l, r) in enumerate(((0, 0), (0, 1), (1, 0))):
                            mm = pe.matmul(tail_rows, V[half, l, 2, g * D:(g + 1) * D], PT1[half, r, 2 * r2:2 * r2 + 2, :],
                                           start=False, stop=(c == 2))
                        mm.then_inc(full.sem, 1)

            def turn_z(w):
                for j in range(TT):
                    await_(pe, z_ready, w, j + 1)
                    b = take(w, ("Z", j))
                    for k in range(KT):
                        mm = pe.transpose(b[:, k * P:(k + 1) * P], z[:, j, k * P:(k + 1) * P], ident)
                    mm.then_inc(full.sem, 1)

            def logits(w):
                ready(w, ("Z", TT - 1))
                b = take(w, ("LG",))
                for j in range(TT):
                    for k in range(KT):
                        mm = pe.matmul(b[:, j * EXPERTS:(j + 1) * EXPERTS], zT[:, j, k, :], rwT[:, k, :],
                                       start=(k == 0), stop=(k == KT - 1))
                mm.then_inc(full.sem, 1)

            def turn_weights(w):
                b = take(w, ("WT",))
                await_apart(pe, w_ready, w, 1, pe_passed)
                for j in range(TT):
                    mm = pe.transpose(b[0:EXPERTS, j * P:(j + 1) * P], lg[:, 0, j, :], ident)
                mm.then_inc(full.sem, 1)

            def experts(w):
                ready(w, ("WT",))
                for j in range(TT):
                    b = take(w, ("EB", j))
                    pe.matmul(b[:, :], wT[:, j, :], eb[:, :], start=True, stop=True).then_inc(full.sem, 1)

            def lead(w):
                hx(w)
                xx(w)
                project(w, 0, (w, ("XX", TT - 1)))

            def body(w):
                for g in range(NKV):
                    if g == 0:
                        if w.seg == "first":
                            await_(pe, free, LEAD, INDEX["lead"][("A", 0, QPG)] + 1)
                        elif w.seg == "mid":
                            await_(pe, free, w, INDEX["mid"][("A", NKV, QPG)] + 1 - len(TASKS["mid"]))
                        else:
                            await_(pe, free, w, INDEX["mid"][("A", NKV, QPG)] + 1 - len(TASKS["mid"]))
                    else:
                        ready(w, ("A", g, QPG))
                    scores_only(w, g)
                    if g < NKV - 1 or w.next:
                        project(w, g + 1, (w, ("XX", TT - 1)) if g == NKV - 1 else None)
                    if g == 0:
                        values(w)
                    turn_probs(w, g)
                    if g > 0:
                        output_group(w, g - 1)
                    elif w.prev:
                        await_(pe, free, w, INDEX["mid"][("D", NKV - 1, 1, 1)] + 1 - len(TASKS["mid"]))
                        output_group(w, NKV - 1)
                    if g == 2 and w.prev:
                        turn_z(w)
                    if g == 3 and w.prev:
                        turn_weights(w)
                    attend(w, g)
                    if g == 1 and w.next:
                        hx(w)
                    if g == 2 and w.prev:
                        logits(w)
                    if g == 2 and w.next:
                        xx(w)
                    if g == 3 and w.prev:
                        experts(w)

            def scores_only(w, g):
                for b2 in range(2):
                    b = take(w, ("S", g, b2, 0))
                    for h in range(QPG):
                        mm = split_product(b[:, h * S0:(h + 1) * S0], range(1),
                                           lambda t, r: kT[:, r, b2, 0:S0],
                                           lambda t, l: qT[:, l, b2, h * S0:(h + 1) * S0])
                    mm.then_inc(full.sem, 1)
                    b = take(w, ("S", g, b2, 1))
                    for r2 in range(2):
                        mm = split_product(b[:, r2 * SEQ:(r2 + 1) * SEQ], range(1),
                                           lambda t, r: kT[:, r, b2, :],
                                           lambda t, l: qT[:, l, b2, QPG * S0 + r2 * P:QPG * S0 + (r2 + 1) * P])
                    mm.then_inc(full.sem, 1)

            def output_group(w, g):
                if g < NKV - 1:
                    ready(w, ("D", g, 1, 1))
                for j in range(TT):
                    if g == 0 and w.prev:
                        await_(pe, acc_free, w, j + 1)
                    for h in range(QPG):
                        for c, (l, r) in enumerate(((0, 0), (0, 1), (1, 0))):
                            mm = pe.matmul(acc[j][:, :], oT[:, l, h, j * P:(j + 1) * P], wp[:, :, g * QPG + h, r, :],
                                           start=(g == 0 and h == 0 and c == 0), stop=(g == NKV - 1 and h == QPG - 1 and c == 2))
                    if g == NKV - 1:
                        mm.then_inc(acc_full.sem, 1)

            def tail(w):
                await_(pe, free, LAST, INDEX["last"][("D", NKV - 1, 1, 1)] + 1)
                output_group(w, NKV - 1)
                turn_z(w)
                logits(w)
                turn_weights(w)
                experts(w)

            bodies(pe, lead, body, tail)

        @block.scalar
        def _(act):
            na = [0]

            def bank_a():
                na[0] += 1
                act.wait_ge(a_full, na[0])
                return bank[(na[0] - 1) % 4]

            def cp(out_, in_):
                return act.activation(out_, in_, ACT.Copy)

            b = bank_a()
            cp(pw[:, 0, :], b[:, 0:SEQ])
            cp(el[:, 1, :], b[:, SEQ:2 * SEQ]).then_inc(a_free, 1)
            b = bank_a()
            cp(pw[:, 1:3, :], b[:, 0:2 * SEQ].rearrange("p (k h) -> p k h", k=2)).then_inc(a_free, 1)
            for c in range(0, BATCH, 2):
                for r in range(2):
                    b = bank_a()
                    cp(G[:, r, c:c + 2, :], b[:, 0:2 * SEQ].rearrange("p (c h) -> p c h", c=2)).then_inc(a_free, 1)
            act.wait_ge(trig_in, 1)
            act.activation(pw[:, 6, :], re[:, :], ACT.Tanh, scale=0.5).then_inc(trig, 1)
            act.activation(pw[:, 7, :], pw[:, 5, :], ACT.Sin, scale=TWO_PI).then_inc(trig, 1)
            act.activation(pw[:, 8, :], pw[:, 5, :], ACT.Sin, scale=TWO_PI / 2).then_inc(trig, 1)
            act.wait_ge(wq_loaded, 16)
            wq_flat = wq[:, :, :, :, :].rearrange("p j a k d -> p (j a k d)").bitcast(F32)
            wp_flat = wp[:, :, :, :, :].rearrange("p j h a d -> p (j h a d)").bitcast(F32)
            for i in range(20):
                if i == 12:
                    act.wait_ge(wp_loaded, 16)
                src = wq_flat[:, i * 1024:(i + 1) * 1024] if i < 12 else wp_flat[:, (i - 12) * 1024:(i - 11) * 1024]
                if i:
                    act.wait_ge(squares, i)
                act.activation(junk[:, :], src, ACT.Square, scale=2.0 ** -7, accum_out=sq[:, i:i + 1]).then_inc(squares, 1)
            act.wait_ge(norm_max, 1)
            act.activation(wsc[:, 2:4], wsc[:, 0:2], ACT.Sqrt, scale=2.0 ** 14).then_inc(norm_max, 1)

            for c in range(NCH):
                g = c // CPG
                if c % CPG == 0:
                    act.wait_ge(decay_arg, g + 1)
                    act.activation(Te, Te, ACT.Exp).then_inc(decay, 1)
                    act.wait_ge(phase, g + 1)
                    act.activation(Ts, Tp, ACT.Sin, scale=TWO_PI).then_inc(waves, 1)
                    act.activation(Tc, Tp, ACT.Sin, scale=TWO_PI / 2).then_inc(act1, 1)
                    act.wait_ge(act1, g + 1)
                    act.activation(Tc, Tc, ACT.Square).then_inc(waves, 1)
                    if g:
                        pass
                for half in range(2):
                    b = bank_a()
                    if c % CPG == 0 and half == 0 and g:
                        act.wait_ge(ht_stored, 16 * g)
                    h0 = CH * (c % CPG) + 8 * half
                    cp(ht[:, :, :, h0:h0 + 8].rearrange("p a c h -> p h a c"),
                       b[:, :].rearrange("p (h a c) -> p h a c", h=8, a=NA)).then_inc(a_free, 1)
                for t in w_tasks(c):
                    if t == 0:
                        act.wait_ge(scales, 1)
                    act.wait_ge(b_full, t + 1)
                    src = bank[4 + t % 4][:, :].rearrange("p (k d) -> p k d", k=4)
                    if W_TASKS[t][0] == "q":
                        hi = wq[:, W_TASKS[t][1], 0, :, :]
                    else:
                        hi = wp[:, W_TASKS[t][1], W_TASKS[t][2]:W_TASKS[t][2] + 4, 0, :]
                    act.activation(hi, src, ACT.Copy, scale=s_q if W_TASKS[t][0] == "q" else s_p).then_inc(b_hi, 1)

            act.preload_act_table(ACT.Exp)

            def copy_part(w, task, pieces, scale=1.0):
                i = INDEX[w.seg][task]
                await_(act, full, w, i + 1)
                b = ring_bank[(ring_start(w) + i) % RING]
                for out_, in_of in pieces:
                    ins = act.activation(out_, in_of(b), ACT.Copy, scale=scale)
                ins.then_inc(part_hi.sem, 1)

            def project(w, u):
                for j in range(QPG + 1):
                    copy_part(w, ("A", u, j), head_pieces(0, j), QKV_EVAC)

            def hx(w):
                if w.seg != "lead":
                    await_(act, xn_ready, w, 0)
                    await_(act, h_out, w, 0)
                for j in range(TT):
                    copy_part(w, ("HX", j), [(H[:, j, :], lambda b: b[:, :])])

            def xx(w):
                for j in range(TT):
                    copy_part(w, ("XX", j), token_pieces(0, j), X_SCALE)

            def lead(w):
                hx(w)
                xx(w)
                project(w, 0)

            def router_exp(w):
                await_(act, lg_in, w, 1)
                act.activation(lg[:, 1], lg[:, 0], ACT.Exp).then_inc(lg_exp.sem, 1)

            def body(w):
                for g in range(NKV):
                    for b2 in range(2):
                        await_(act, neg_max, w, 2 * g + b2 + 1)
                        for i in range(6):
                            t = P0[:, b2, i, :] if i < QPG else P1[:, i - QPG, b2, :]
                            e = act.activation(t, t, ACT.Exp, bias=nmx[:, b2, i:i + 1], scale=alpha,
                                               accum_out=sums[:, b2, i:i + 1])
                        e.then_inc(exps.sem, 1)
                    if g < NKV - 1 or w.next:
                        project(w, g + 1)
                    if g == 0:
                        for t in range(TT):
                            copy_part(w, ("V", t), [(V[:, 0, t, :], lambda b: b[:, :])], QKV_EVAC)
                    for i in range(4):
                        copy_part(w, ("T", g, i), [(probs_out(0, i), lambda b: probs_in(b, i))], P_SCALE)
                    for b2 in range(2):
                        for r2 in range(2):
                            copy_part(w, ("D", g, b2, r2), [(oT[:, 0, 2 * r2:2 * r2 + 2, b2 * SEQ:(b2 + 1) * SEQ],
                                      lambda b: b[:, 0:PT].rearrange("p (h s) -> p h s", h=2))], OUT_EVAC)
                    if g == 1 and w.next:
                        hx(w)
                    if g == 2 and w.prev:
                        router_exp(w)
                    if g == 2 and w.next:
                        xx(w)

            bodies(act, lead, body, router_exp)

        @block.gpsimd
        def _(pool):
            npool = [0]

            def own(ins):
                npool[0] += 1
                ins.then_inc(pool1, 1)
                pool.wait_ge(pool1, npool[0])

            def wide(v, n):
                return v.unsqueeze(2).broadcast_to([P, v.shape[1], n])

            pool.wait_ge(norm_max, 2)
            pool.partition_all_reduce(wsc[:, 4:6], wsc[:, 2:4], P, RMAX).then_inc(norm_max, 1)
            for g in range(NG):
                hs = slice(64 * g, 64 * (g + 1))
                if g:
                    pool.wait_ge(qcp, CPG * g)
                else:
                    pool.wait_ge(trig_in, 1)
                    pool.wait_ge(const_in, 16)
                pool.tensor_tensor(Te, wide(re[:, hs], NTAB), cst[:, C_L:C_L + NTAB].unsqueeze(1).broadcast_to([P, 64, NTAB]),
                                   ALU.mult).then_inc(decay_arg, 1)
                pool.wait_ge(decay, g + 1)
                pool.wait_ge(waves, 2 * g + 1)
                own(pool.tensor_tensor(Ts, Ts, Te, ALU.mult))
                pool.wait_ge(cosine, g + 1)
                own(pool.tensor_tensor(Tc, Tc, Te, ALU.mult))
                c_, s_ = Tc[:, :, NK_ + NJ:], Ts[:, :, NK_ + NJ:]
                fr_, fi_ = wide(fr[:, hs], NA), wide(fi[:, hs], NA)
                pool.wait_ge(trig_in, 2)
                own(pool.tensor_tensor(pf[:, 0], c_, fr_, ALU.mult))
                own(pool.tensor_tensor(pg[:, 0], s_, fi_, ALU.mult))
                own(pool.tensor_tensor(pf[:, 1], c_, fi_, ALU.mult))
                own(pool.tensor_tensor(pg[:, 1], s_, fr_, ALU.mult))
                own(pool.tensor_tensor(pf[:, 0], pf[:, 0], pg[:, 0], ALU.subtract))
                own(pool.tensor_tensor(pf[:, 1], pf[:, 1], pg[:, 1], ALU.add))
                pool.tensor_tensor(pg[:, 0, 0:1, 0:1], pf[:, 0, 0:1, 0:1], pf[:, 1, 0:1, 0:1], ALU.add).then_inc(tables, 1)
                for c in range(CPG * g, CPG * (g + 1)):
                    k = slice(CH * (c % CPG), CH * (c % CPG + 1))
                    if c:
                        pool.wait_ge(qcp, c)
                    pool.tensor_tensor(QB[:, :, :, :], j_of(Ts, k), k_of(Ts, k), ALU.mult).then_inc(partial, 1)
                    if c == 0:
                        pool.wait_ge(a_free, GT)
                    pool.tensor_tensor(CB[:, :, :, :], g_of(1, c), a_of(1, k), ALU.mult).then_inc(partial, 1)

            def normalise(w, g):
                for b2 in range(2):
                    await_(pool, recips, w, 2 * g + b2 + 1)
                    pool.tensor_tensor(P0[:, b2], P0[:, b2], rec[:, b2, 0:QPG].unsqueeze(2).broadcast_to([P, QPG, S0]), ALU.mult)
                    r1 = rec[:, b2, QPG:6].unsqueeze(2)
                    pool.tensor_tensor(P1[:, :, b2, 0:S0], P1[:, :, b2, 0:S0], r1.broadcast_to([P, 2, S0]), ALU.mult)
                    pool.tensor_tensor(P2[:, :, b2], P1[:, :, b2, S0:SEQ], r1.broadcast_to([P, 2, S1]), ALU.mult).then_inc(probs.sem, 1)

            def root(w, which, var, done):
                await_(pool, var, w, 1)
                pool.tensor_tensor(rstd[:, which, 1], rstd[:, which, 0], cst[:, C_HALF:C_HALF + TT], ALU.pow).then_inc(done.sem, 1)

            def body(w):
                for g in range(NKV):
                    normalise(w, g)
                    if g == 1 and w.prev:
                        root(w, 1, f_var, f_rstd)
                    if g == 1 and w.next:
                        root(w, 0, x_var, x_rstd)

            bodies(pool, lambda w: root(w, 0, x_var, x_rstd), body, lambda w: root(w, 1, f_var, f_rstd))

        @block.vector
        def _(dve):
            nd = [0]

            def own(ins):
                nd[0] += 1
                ins.then_inc(dve1, 1)
                dve.wait_ge(dve1, nd[0])

            def tt(o, a, b, op):
                own(dve.tensor_tensor(o, a, b, op))

            def ts(o, a, s1, s2, op0, op1):
                own(dve.tensor_scalar(o, a, s1, s2, op0, op1))

            def stt(o, a, s, b, op0, op1):
                own(dve.scalar_tensor_tensor(out=o, in0=a, scalar=s, in1=b, op0=op0, op1=op1))

            dve.wait_ge(par_loaded, 16 * 7)
            dve.wait_ge(a_free, 2)
            elf = el[:, :, :].rearrange("p i h -> p (i h)")
            e0, e1, e2, e3 = (ev[:, i].rearrange("p i h -> p (i h)") for i in range(4))
            ts(e0, elf, LOG2E, ROUND, ALU.mult, ALU.add)
            ts(e0, e0, -ROUND, None, ALU.add, ALU.bypass)
            stt(e1, e0, -LN2_HI, elf, ALU.mult, ALU.add)
            stt(e1, e0, -LN2_LO, e1, ALU.mult, ALU.add)
            ts(e2, e1, 1.0 / 5040, None, ALU.mult, ALU.bypass)
            for c in (1.0 / 720, 1.0 / 120, 1.0 / 24, 1.0 / 6, 0.5, 1.0):
                stt(e2, e2, c, e1, ALU.add, ALU.mult)
            ts(e0, e0, 127.0 + 2.0 ** 23, None, ALU.add, ALU.bypass)
            own(dve.tensor_scalar(e3.bitcast(I32), e0.bitcast(I32), 23, None, ALU.logical_shift_left, ALU.bypass))
            stt(e2, e2, 1.0, e3, ALU.add, ALU.mult)
            dt, a = ev[:, 2, 0, :], ev[:, 2, 1, :]
            aim, br, bi = (pw[:, i, :] for i in range(3))
            r = lambda i: pw[:, i, :]
            stt(re[:, :], a, -1.0, dt, ALU.mult, ALU.mult)
            tt(r(3), aim, dt, ALU.mult)
            ts(r(3), r(3), INV_2PI, None, ALU.mult, ALU.bypass)
            ts(r(4), r(3), ROUND, -ROUND, ALU.add, ALU.add)
            tt(ur[:, :], r(3), r(4), ALU.subtract)
            ts(r(5), r(3), 0.5, None, ALU.mult, ALU.bypass)
            ts(r(4), r(5), ROUND, -ROUND, ALU.add, ALU.add)
            own(dve.tensor_tensor(r(5), r(5), r(4), ALU.subtract))
            dve.tensor_copy(r(4), r(5)).then_inc(trig_in, 1)

            def phases(g):
                hs = slice(64 * g, 64 * (g + 1))
                one_row = lambda c0: cst[:, c0:c0 + NTAB].unsqueeze(1).broadcast_to([P, 64, NTAB])
                if g:
                    dve.wait_ge(partial, 2 * CPG * g)
                tt(Tp, ur[:, hs].unsqueeze(2).broadcast_to([P, 64, NTAB]), one_row(C_L), ALU.mult)
                tt(Tp, Tp, one_row(C_OFF), ALU.add)
                ts(Tc, Tp, ROUND, -ROUND, ALU.add, ALU.add)
                dve.tensor_tensor(Tp, Tp, Tc, ALU.subtract).then_inc(phase, 1)

            phases(0)
            dve.wait_ge(trig, 3)
            t_, sy, qy = r(6), r(7), r(8)
            ts(r(9), t_, -1.0, 1.0, ALU.mult, ALU.add)
            own(dve.reciprocal(r(10), r(9)))
            stt(r(9), t_, 2.0, r(10), ALU.mult, ALU.mult)
            tt(r(10), qy, qy, ALU.mult)
            ts(r(10), r(10), -2.0, 1.0, ALU.mult, ALU.add)
            stt(r(11), sy, 2.0, r(10), ALU.mult, ALU.mult)
            stt(r(12), sy, 2.0, sy, ALU.mult, ALU.mult)
            ts(r(13), r(12), -1.0, 1.0, ALU.mult, ALU.add)
            tt(r(13), r(13), r(9), ALU.mult)
            tt(r(13), r(13), r(12), ALU.subtract)
            stt(r(14), r(9), 1.0, r(11), ALU.add, ALU.mult)
            tt(r(9), a, a, ALU.mult)
            tt(r(10), aim, aim, ALU.mult)
            tt(r(9), r(9), r(10), ALU.add)
            own(dve.reciprocal(r(10), r(9)))
            tt(r(9), r(14), aim, ALU.mult)
            tt(r(11), r(13), a, ALU.mult)
            tt(r(9), r(9), r(11), ALU.subtract)
            tt(r(12), r(13), aim, ALU.mult)
            tt(r(11), r(14), a, ALU.mult)
            stt(r(12), r(12), -1.0, r(11), ALU.mult, ALU.subtract)
            stt(r(9), r(9), 2.0, r(10), ALU.mult, ALU.mult)
            stt(r(12), r(12), 2.0, r(10), ALU.mult, ALU.mult)
            tt(r(10), br, r(9), ALU.mult)
            tt(r(11), bi, r(12), ALU.mult)
            tt(fr[:, :], r(10), r(11), ALU.subtract)
            tt(r(10), br, r(12), ALU.mult)
            tt(r(11), bi, r(9), ALU.mult)
            dve.tensor_tensor(fi[:, :], r(10), r(11), ALU.add).then_inc(trig_in, 1)
            dve.wait_ge(squares, 20)
            own(dve.tensor_reduce(wsc[:, 0:1], sq[:, 0:12], AX_X, ALU.add))
            own(dve.tensor_reduce(wsc[:, 1:2], sq[:, 12:20], AX_X, ALU.add))
            dve.tensor_scalar(wsc[:, 0:2], wsc[:, 0:2], NORM_FLOOR, None, ALU.max, ALU.bypass).then_inc(norm_max, 1)
            dve.wait_ge(norm_max, 3)
            own(dve.tensor_scalar(wsc[:, 12:14].bitcast(I32), wsc[:, 4:6].bitcast(I32), 0x7F800000, None,
                                  ALU.bitwise_and, ALU.bypass))
            own(dve.reciprocal(wsc[:, 14:16], wsc[:, 12:14]))
            ts(wsc[:, 6:8], wsc[:, 14:16], W_SCALE, None, ALU.mult, ALU.bypass)
            stt(alpha, wsc[:, 12:13], float(D) ** -0.5 / QKV_STORE ** 2, wsc[:, 12:13], ALU.mult, ALU.mult)
            own(dve.tensor_scalar(wsc[:, 9:10], alpha, -1.0, None, ALU.mult, ALU.bypass))
            dve.scalar_tensor_tensor(out=beta, in0=wsc[:, 12:13], scalar=1.0 / (QKV_STORE * W_SCALE), in1=wsc[:, 13:14],
                                     op0=ALU.mult, op1=ALU.mult).then_inc(scales, 1)

            for c in range(NCH):
                g = c // CPG
                k = slice(CH * (c % CPG), CH * (c % CPG + 1))
                if c % CPG == 0:
                    if g:
                        phases(g)
                    dve.wait_ge(waves, 2 * g + 2)
                    dve.tensor_scalar(Tc, Tc, -2.0, 1.0, ALU.mult, ALU.add).then_inc(cosine, 1)
                    dve.wait_ge(tables, g + 1)
                if c >= 2:
                    dve.wait_ge(a_full, GT + 2 * (c - 1))
                q_, c_ = Q[:, c % 2], CP[:, c % 2]
                dve.tensor_tensor(q_, j_of(Tc, k), k_of(Tc, k), ALU.mult)
                own(dve.tensor_tensor(c_, g_of(0, c), a_of(0, k), ALU.mult))
                dve.wait_ge(partial, 2 * c + 2)
                dve.tensor_tensor(q_, q_, QB[:, :, :, :], ALU.subtract)
                dve.tensor_tensor(c_, c_, CB[:, :, :, :], ALU.subtract).then_inc(qcp, 1)
                for t in w_tasks(c):
                    dve.wait_ge(b_hi, t + 1)
                    task = W_TASKS[t]
                    src = bank[4 + t % 4][:, :].rearrange("p (k d) -> p k d", k=4)
                    if task[0] == "q":
                        hi, lo = wq[:, task[1], 0, :, :], wq[:, task[1], 1, :, :]
                    else:
                        hi, lo = (wp[:, task[1], task[2]:task[2] + 4, i, :] for i in range(2))
                    dve.scalar_tensor_tensor(out=lo, in0=src, scalar=s_q if task[0] == "q" else s_p, in1=hi,
                                             op0=ALU.mult, op1=ALU.subtract).then_inc(b_free, 1)
            t = len(W_TASKS)
            dve.wait_ge(b_full, t + 1)
            dve.tensor_copy(rwT[:, :, :], bank[4 + t % 4][:, 0:KT * EXPERTS].rearrange("p (k e) -> p k e", k=KT)).then_inc(b_free, 1)

            steps = [0]

            def step(w, ins, apart=False):
                steps[0] += 1
                ins.then_inc(vec.sem, 1)
                if apart:
                    await_apart(dve, vec, w, steps[0], dve_passed)
                else:
                    await_(dve, vec, w, steps[0])

            def of(w, task):
                i = INDEX[w.seg][task]
                return ring_bank[(ring_start(w) + i) % RING]

            def low_part(w, task, pieces, hi_pieces, scale):
                await_(dve, part_hi, w, SCALAR_INDEX[w.seg][task] + 1)
                for (lo, in_of), (hi, _) in zip(pieces, hi_pieces):
                    ins = dve.scalar_tensor_tensor(out=lo, in0=in_of(of(w, task)), scalar=scale, in1=hi,
                                                   op0=ALU.mult, op1=ALU.subtract)
                ins.then_inc(free.sem, 1)

            def hx(w):
                for j in range(TT):
                    await_(dve, part_hi, w, SCALAR_INDEX[w.seg][("HX", j)] + 1)
                    dve.bn_stats(stat[:, 0, j, 0:6], of(w, ("HX", j))[:, :]).then_inc(free.sem, 1)
                normal(w, 0, x_var, w and free, INDEX[w.seg][("HX", TT - 1)] + 1)

            def normal(w, which, var, signal, k):
                await_apart(dve, signal, w, k, dve_passed)
                for j in range(TT):
                    ins = dve.bn_aggr(mv[:, which, j, :], stat[:, which, j, 0:6])
                step(w, ins)
                dve.tensor_scalar(rstd[:, which, 0], mv[:, which, :, 1], EPS, None, ALU.add, ALU.bypass).then_inc(var.sem, 1)

            def x_norm(w):
                await_(dve, x_rstd, w, 1)
                for j in range(TT):
                    dve.tensor_scalar(xn[:, j, :], H[:, j, :], mv[:, 0, j, 0:1], rstd[:, 0, 1, j:j + 1],
                                      ALU.subtract, ALU.mult).then_inc(xn_ready.sem, 1)

            def xx(w):
                for j in range(TT):
                    low_part(w, ("XX", j), token_pieces(1, j), token_pieces(0, j), X_SCALE)

            def project(w, u, j):
                low_part(w, ("A", u, j), head_pieces(1, j), head_pieces(0, j), QKV_EVAC)

            def mask_max(w, g, b2):
                for r2 in range(2):
                    await_apart(dve, full, w, INDEX[w.seg][("S", g, b2, r2)] + 1, dve_passed)
                    b = of(w, ("S", g, b2, r2))
                    for i in range(QPG if r2 == 0 else 2):
                        if r2 == 0:
                            o, s, m, c = P0[:, b2, i, :], b[:, i * S0:(i + 1) * S0], mask0, i
                        else:
                            o, s, m, c = P1[:, i, b2, :], b[:, i * SEQ:(i + 1) * SEQ], mask1, QPG + i
                        ins = dve.tensor_tensor_reduce(o, s, m, 1.0, -3e38, ALU.add, ALU.max, mx[:, b2, c:c + 1])
                    ins.then_inc(free.sem, 1)
                await_(dve, free, w, INDEX[w.seg][("S", g, b2, 1)] + 1)
                dve.tensor_scalar(nmx[:, b2, :], mx[:, b2, :], wsc[:, 9:10], None, ALU.mult, ALU.bypass).then_inc(neg_max.sem, 1)

            def reciprocals(w, g, b2):
                await_(dve, exps, w, 2 * g + b2 + 1)
                dve.reciprocal(rec[:, b2, :], sums[:, b2, :]).then_inc(recips.sem, 1)

            def residual(w):
                await_(dve, hr_in, w, 0)
                await_(dve, out_ready, w, 0)
                for j in range(TT):
                    await_(dve, acc_full, w, j + 1)
                    dve.scalar_tensor_tensor(out=h2[:, j, :], in0=acc[j][:, :], scalar=beta, in1=Hr[:, j, :],
                                             op0=ALU.mult, op1=ALU.add).then_inc(acc_free.sem, 1)
                for j in range(TT):
                    await_(dve, acc_free, w, j + 1)
                    ins = dve.bn_stats(stat[:, 1, j, 0:6], h2[:, j, :])
                step(w, ins, apart=True)
                normal(w, 1, f_var, vec, steps[0])

            def z_norm(w):
                await_(dve, f_rstd, w, 1)
                await_(dve, out_stored, w, 0)
                for j in range(TT):
                    dve.tensor_scalar(z[:, j, :], h2[:, j, :], mv[:, 1, j, 0:1], rstd[:, 1, 1, j:j + 1],
                                      ALU.subtract, ALU.mult).then_inc(z_ready.sem, 1)

            def z_turned(w):
                for j in range(TT):
                    await_(dve, full, w, INDEX[w.seg][("Z", j)] + 1)
                    dve.tensor_copy(zT[:, j], of(w, ("Z", j))[:, :].rearrange("p (k s) -> p k s", k=KT)).then_inc(free.sem, 1)

            def router_in(w):
                await_(dve, full, w, INDEX[w.seg][("LG",)] + 1)
                dve.tensor_tensor(lg[:, 0], of(w, ("LG",))[:, 0:TT * EXPERTS].rearrange("p (t e) -> p t e", t=TT),
                                  rb[:, :].unsqueeze(1).broadcast_to([P, TT, EXPERTS]), ALU.add).then_inc(free.sem, 1)
                await_(dve, free, w, INDEX[w.seg][("LG",)] + 1)
                step(w, dve.tensor_reduce(small[:, 0, :], lg[:, 0], AX_X, ALU.max))
                dve.tensor_tensor(lg[:, 0], lg[:, 0], small[:, 0, :].unsqueeze(2).broadcast_to([P, TT, EXPERTS]),
                                  ALU.subtract).then_inc(lg_in.sem, 1)

            def router_out(w):
                await_(dve, lg_exp, w, 1)
                step(w, dve.tensor_reduce(small[:, 1, :], lg[:, 1], AX_X, ALU.add))
                step(w, dve.reciprocal(small[:, 2, :], small[:, 1, :]))
                step(w, dve.tensor_tensor(lg[:, 2], lg[:, 1], small[:, 2, :].unsqueeze(2).broadcast_to([P, TT, EXPERTS]), ALU.mult), apart=True)
                for j in range(TT):
                    ins = dve.max(out=top[:, j, :], in_=lg[:, 2, j, :])
                step(w, ins, apart=True)
                for j in range(TT):
                    ins = dve.match_replace(out=lg[:, 3, j, :], in_to_replace=top[:, j, :], in_values=lg[:, 2, j, :], imm_value=-1.0)
                step(w, ins)
                step(w, dve.tensor_scalar(lg[:, 3], lg[:, 3], 0.0, None, ALU.max, ALU.bypass))
                dve.tensor_tensor(lg[:, 0], lg[:, 2], lg[:, 3], ALU.subtract).then_inc(w_ready.sem, 1)
                await_(dve, w_ready, w, 1)
                step(w, dve.tensor_reduce(small[:, 3, :], lg[:, 0], AX_X, ALU.add))
                for j in range(TT):
                    ins = dve.scalar_tensor_tensor(out=h2[:, j, :], in0=z[:, j, :], scalar=small[:, 3, j:j + 1], in1=h2[:, j, :],
                                                   op0=ALU.mult, op1=ALU.add)
                step(w, ins)

            def weights_turned(w):
                await_(dve, full, w, INDEX[w.seg][("WT",)] + 1)
                dve.tensor_copy(wT[:, :, :], of(w, ("WT",))[0:EXPERTS, 0:TT * P].rearrange("p (t s) -> p t s", t=TT)).then_inc(free.sem, 1)

            def finish(w):
                for j in range(TT):
                    await_(dve, full, w, INDEX[w.seg][("EB", j)] + 1)
                    dve.tensor_tensor(z[:, j, :], of(w, ("EB", j))[:, :], h2[:, j, :], ALU.add).then_inc(free.sem, 1)
                await_(dve, free, w, INDEX[w.seg][("EB", TT - 1)] + 1)
                dve.tensor_copy(small[:, 0, :], small[:, 1, :]).then_inc(out_ready.sem, 1)

            def lead(w):
                steps[0] = 0
                hx(w)
                x_norm(w)
                xx(w)
                for j in range(QPG + 1):
                    project(w, 0, j)
                assert steps[0] == vec.n["lead"]

            def body(w):
                steps[0] = 0
                for g in range(NKV):
                    mask_max(w, g, 0)
                    mask_max(w, g, 1)
                    made = g < NKV - 1 or w.next
                    if made:
                        project(w, g + 1, 0)
                    reciprocals(w, g, 0)
                    if made:
                        project(w, g + 1, 1)
                    reciprocals(w, g, 1)
                    if made:
                        for j in range(2, QPG + 1):
                            project(w, g + 1, j)
                    if g == 1 and w.prev:
                        residual(w)
                    if g == 3 and w.prev:
                        router_out(w)
                    if g == 2 and w.next:
                        x_norm(w)
                    if g == 0:
                        for t in range(TT):
                            low_part(w, ("V", t), [(V[:, 1, t, :], lambda b: b[:, :])], [(V[:, 0, t, :], None)], QKV_EVAC)
                    for i in range(4):
                        low_part(w, ("T", g, i), [(probs_out(1, i), lambda b: probs_in(b, i))], [(probs_out(0, i), None)], P_SCALE)
                    if g == 1 and w.prev:
                        z_norm(w)
                    if g == 2 and w.prev:
                        z_turned(w)
                    if g == 3 and w.prev:
                        weights_turned(w)
                    for b2 in range(2):
                        for r2 in range(2):
                            o = [oT[:, i, 2 * r2:2 * r2 + 2, b2 * SEQ:(b2 + 1) * SEQ] for i in range(2)]
                            low_part(w, ("D", g, b2, r2), [(o[1], lambda b: b[:, 0:PT].rearrange("p (h s) -> p h s", h=2))],
                                     [(o[0], None)], OUT_EVAC)
                    if g == 1 and w.next:
                        hx(w)
                    if g == 2 and w.prev:
                        router_in(w)
                    if g == 2 and w.next:
                        xx(w)
                    if g == 3 and w.prev:
                        finish(w)


            def tail(w):

                steps[0] = 0
                residual(w)
                z_norm(w)
                z_turned(w)
                router_in(w)
                router_out(w)
                weights_turned(w)
                finish(w)


            bodies(dve, lead, body, tail)


def ring_start(w):
    at, n = 0, {}
    for seg in SEGMENTS:
        n[seg] = at
        at = (at + len(TASKS[seg])) % RING
    assert len(TASKS["mid"]) % RING == 0
    return n[w.seg]


_INS = ["x", "L0_tok_log_dt", "L0_tok_B_ri", "L0_tok_inv_A_real", "L0_tok_A_imag", "L0_attn_weight_qkv",
        "L0_attn_weight_proj", "L0_ffn_router_weight", "L0_ffn_router_bias", "L0_ffn_expert_bias"]


def kernel(**inputs):
    import concourse.bacc as _bacc
    from concourse.bass_utils import run_bass_kernel_spmd as _run

    nc = _bacc.Bacc("TRN2", target_bir_lowering=False, num_devices=1)
    arrays, args = {}, []
    for name in _INS:
        a = np.ascontiguousarray(inputs[name])
        arrays[f"in_{name}"] = a
        args.append(nc.dram_tensor(f"in_{name}", a.shape, mybir.dt.from_np(a.dtype), kind="ExternalInput").ap())
    arrays["shape_constants"] = shape_constants()
    args.append(nc.dram_tensor("shape_constants", (P, NCONST), F32, kind="ExternalInput").ap())
    out = nc.dram_tensor("out", (BATCH, SEQ, HID), F32, kind="ExternalOutput").ap()
    vit_tower(nc, *args, out)
    r = _run(nc, [arrays], core_ids=[0])
    return r.results[0]["out"]
```

```python
from contextlib import ExitStack

import numpy as np

import concourse.bass as bass
from concourse import mybir

F32 = mybir.dt.float32
F16 = mybir.dt.float16
I32 = mybir.dt.int32
ALU = mybir.AluOpType
ACT = mybir.ActivationFunctionType
AX_X = mybir.AxisListType.X
RMAX = bass.bass_isa.ReduceOp.max

P = 128
BATCH, SEQ, MODES = 16, 192, 64
HID = 512
NKV, QPG, D = 4, 4, 128
NH = NKV * QPG
GROUP = QPG + 2
KT = HID // P
PAIRS = BATCH // 2
PT = 2 * SEQ
TT = PT // P
S0, S1 = P, SEQ - P
EXPERTS, TOP_K = 64, 8
EPS = 1e-5

NK_, NA, NJ = 16, HID // P, 8
NKA = NK_ + NA
NTAB = NKA + NJ
TAB_H = 32
CH = 8
CPG, NCH = TAB_H // CH, SEQ // CH
STORE_H = 16
BANK_H = 4
HHALF = SEQ // 2

X_SCALE = 2.0 ** 10
W_SCALE = 2.0 ** 14
QKV_STORE = 2.0 ** 9
P_SCALE = 2.0 ** 14
QKV_EVAC = QKV_STORE / (X_SCALE * W_SCALE)
OUT_EVAC = 1.0 / P_SCALE
NORM_FLOOR = 2.0 ** -60

MASKED = -1e30
ROUND = 1.5 * 2.0 ** 23
TWO_PI = 6.283185
LOG2E = 1.4426950408889634
LN2_HI, LN2_LO = 0.693145751953125, 1.4286068203094172e-06
INV_2PI = 0.15915494309189535

C_ID, C_M0, C_M1 = 0, P, 2 * P
C_L = C_M1 + SEQ
C_OFF = C_L + NTAB
C_HALF = C_OFF + NTAB
C_ONE = C_HALF + 3
NCONST = C_ONE + 1


def shape_constants():
    c = np.zeros((P, NCONST), np.float32)
    p, s = np.arange(P)[:, None], np.arange(SEQ)[None, :]
    c[:, C_ID:C_ID + P] = np.eye(P)
    c[:, C_M0:C_M0 + P] = np.where(s[:, :P] <= p, 0.0, MASKED)
    c[:, C_M1:C_M1 + SEQ] = np.where(s <= S0 + p % S1, 0.0, MASKED)
    c[:, C_L:C_L + NTAB] = [*range(NK_), *range(0, HID, P), *range(0, P, NK_)]
    imag = p >= MODES
    c[:, C_OFF:C_OFF + NK_] = np.where(imag, -0.25, 0.0)
    c[:, C_OFF + NK_:C_OFF + NKA] = np.where(imag, 0.25, 0.0)
    c[:, C_HALF:C_HALF + 3] = -0.5
    c[:, C_ONE] = 1.0
    return c


RING = 5


def padded(g, prev, nxt):
    return prev and nxt and g < NKV - 1


def slot_tasks(g, prev, nxt):
    out = [("S", g, b, r) for b in range(2) for r in range(2)]
    if g < NKV - 1 or nxt:
        out += [("A", g + 1, j) for j in range(QPG + 1)]
    if g == 0:
        out += [("V", t) for t in range(TT)]
    out += [("T", g, i) for i in range(4)]
    if g == 2 and prev:
        out += [("Z", j) for j in range(TT)]
    if g == 3 and prev:
        out += [("WT",)]
    out += [("D", g, b, r) for b in range(2) for r in range(2)]
    if padded(g, prev, nxt):
        out += [("PAD", g)]
    if g == 2 and prev:
        out += [("LG",)]
    if g == 2 and nxt:
        out += [("XX", j) for j in range(TT)]
    if g == 3 and prev:
        out += [("EB", j) for j in range(TT)]
    return out


def body_tasks(prev, nxt):
    return [t for g in range(NKV) for t in slot_tasks(g, prev, nxt)]


TASKS = {
    "lead": [("XX", j) for j in range(TT)] + [("A", 0, j) for j in range(QPG + 1)],
    "first": body_tasks(False, True),
    "mid": body_tasks(True, True),
    "last": body_tasks(True, False),
    "tail": [("Z", j) for j in range(TT)] + [("LG",), ("WT",)] + [("EB", j) for j in range(TT)],
}
SEGMENTS = list(TASKS)
ON_SCALAR = ("A", "V", "T", "D", "XX")
INDEX = {seg: {t: i for i, t in enumerate(ts)} for seg, ts in TASKS.items()}
SCALAR_INDEX = {seg: {t: i for i, t in enumerate([t for t in ts if t[0] in ON_SCALAR])} for seg, ts in TASKS.items()}


class Where:

    def __init__(self, seg, p):
        self.seg, self.p = seg, p
        self.prev = seg in ("mid", "last")
        self.next = seg in ("first", "mid")


class Signal:

    def __init__(self, sem, lead=0, first=0, mid=0, last=0, tail=0):
        self.sem = sem
        self.n = dict(lead=lead, first=first, mid=mid, last=last, tail=tail)

    def at(self, w, k):
        n, i = self.n, SEGMENTS.index(w.seg)
        before = sum(n[s] * (PAIRS - 2 if s == "mid" else 1) for s in SEGMENTS[:i])
        if w.seg != "mid":
            return before + k
        return w.p * n["mid"] + (before - n["mid"] + k)


def count(f):
    return {seg: f(seg) for seg in SEGMENTS}


def await_(eng, signal, w, k):
    v = signal.at(w, k)
    if not (isinstance(v, int) and v <= 0):
        eng.wait_ge(signal.sem, v)


def await_apart(eng, signal, w, k, spare):
    await_(eng, signal, w, k)
    if not isinstance(w.p, int):
        eng.sem_inc(spare, 1)


def vit_tower(nc, x, log_dt, b_ri, inv_a_real, a_imag, w_qkv, w_proj, r_weight, r_bias, e_bias, const, out):
    with ExitStack() as ctx:
        def sb(name, shape, dt=F32, c=ctx):
            return c.enter_context(nc.sbuf_tensor(name, shape, dt))

        def sem(name):
            return ctx.enter_context(nc.semaphore(name))

        h_dram = nc.dram_tensor("h_tokens", (BATCH * SEQ, HID), F32, kind="Internal").ap()
        out_rows = out.rearrange("c s l -> (c s) l")

        bank = [ctx.enter_context(nc.psum_tensor(f"bank{i}", [P, 512], F32)) for i in range(8)]
        ring_bank, acc = bank[:RING], bank[RING:]

        wq = sb("wq", [P, NKV * GROUP, 2, KT, P], F16)
        wp = sb("wp", [P, KT, NH, 2, P], F16)
        cst = sb("cst", [P, NCONST])
        ident = cst[:, C_ID:C_ID + P]
        mask0, mask1 = cst[:, C_M0:C_M0 + P], cst[:, C_M1:C_M1 + SEQ]
        rwT = sb("rwT", [P, KT, EXPERTS])
        eb = sb("eb", [EXPERTS, HID])
        rb = sb("rb", [P, EXPERTS])
        sq = sb("sq", [P, 48])
        wsc = sb("wsc", [P, 24])
        s_q, s_p = wsc[:, 6:7], wsc[:, 7:8]
        alpha, beta = wsc[:, 8:9], wsc[:, 10:11]

        one = ExitStack()
        G = sb("G", [P, 2, BATCH, SEQ], c=one)
        ht = sb("ht", [P, 2, STORE_H, P], c=one)
        x_a = ht[0:HHALF, :, :, :].rearrange("p i h b -> p (i h b)").rearrange("p (c s d m) -> p c s d m", c=BATCH // 2, s=2, d=2)
        phase_t = sb("phase_t", [P, TAB_H, NTAB], c=one)
        decay_t = sb("decay_t", [P, TAB_H, NTAB], c=one)
        sin_t = sb("sin_t", [P, 2, TAB_H, NTAB], c=one)
        cos_t = sb("cos_t", [P, 2, TAB_H, NTAB], c=one)
        pf_i = sb("pf_i", [P, 2, TAB_H, NA], c=one)
        pg = sb("pg", [P, 4, TAB_H, NA], c=one)
        ur = sb("ur", [P, SEQ], c=one)
        re = sb("re", [P, SEQ], c=one)
        fr = sb("fr", [P, SEQ], c=one)
        fi = sb("fi", [P, SEQ], c=one)
        junk = sb("junk", [P, 1024], F16, c=one)
        r_in = sb("r_in", [EXPERTS, HID], c=one)
        par = ExitStack()
        x_b = sb("x_b", [HHALF, BATCH // 2, 2, 2, 2 * MODES], c=par)
        par_in = sb("par_in", [HHALF, 2, 2, 2, MODES], c=par)
        b_in = sb("b_in", [HHALF, 2, 2, 2 * MODES], c=par)
        el = sb("el", [P, 2, SEQ], c=par)
        ev = sb("ev", [P, 4, 2, SEQ], c=par)
        pw = sb("pw", [P, 15, SEQ], c=par)
        par.close()
        QA = sb("QA", [P, 2, CH, NJ, NK_], c=one)
        QB = sb("QB", [P, 2, CH, NJ, NK_], c=one)
        CP = sb("CP", [P, 2, CH, NA, BATCH], c=one)
        CB = sb("CB", [P, 2, CH, NA, BATCH], c=one)
        one.close()

        results, weights = bank[0:3], bank[3:5]
        cos_j = bank[5][:, :].rearrange("p (i h j) -> p i h j", i=2, h=TAB_H)
        pf_r = bank[6][:, 0:2 * TAB_H * NA].rearrange("p (i h a) -> p i h a", i=2, h=TAB_H)
        CA = bank[7][:, :].rearrange("p (h a c) -> p h a c", h=CH, a=NA)

        H = sb("H", [P, TT, HID])
        Hr = sb("Hr", [P, TT, HID])
        xn = sb("xn", [P, TT, HID])
        xT = sb("xT", [P, 2, KT, PT], F16)
        stat = sb("stat", [P, 2, TT, 8])
        mv = sb("mv", [P, 2, TT, 2])
        rstd = sb("rstd", [P, 2, 2, TT])
        qT = sb("qT", [P, 2, 2, QPG * SEQ], F16)
        kT = sb("kT", [P, 2, 2, SEQ], F16)
        V = sb("V", [P, 2, TT, NKV * D], F16)
        P0 = sb("P0", [P, 2, QPG, S0])
        P1 = sb("P1", [P, 2, 2, SEQ])
        P2 = sb("P2", [P, 2, 2, S1])
        mx = sb("mx", [P, 2, 6])
        nmx = sb("nmx", [P, 2, 6])
        sums = sb("sums", [P, 2, 6])
        rec = sb("rec", [P, 2, 6])
        PT0 = sb("PT0", [P, 2, 2, QPG, SEQ], F16)
        PT1 = sb("PT1", [P, 2, QPG, S1], F16)
        oT = sb("oT", [P, 2, QPG, PT], F16)
        h2 = sb("h2", [P, TT, HID])
        z = sb("z", [P, TT, HID])
        zT = sb("zT", [P, TT, KT, P])
        lg = sb("lg", [P, 4, TT, EXPERTS])
        small = sb("small", [P, 4, TT])
        top = sb("top", [P, TT, 8])
        wT = sb("wT", [EXPERTS, TT, P])

        const_in, par_loaded, x_loaded = sem("const_in"), sem("par_loaded"), [sem("x_a_loaded"), sem("x_b_loaded")]
        wq_loaded, wp_loaded, r_loaded = sem("wq_loaded"), sem("wp_loaded"), sem("r_loaded")
        a_full, a_free = sem("a_full"), sem("a_free")
        b_full, b_hi, b_free = sem("b_full"), sem("b_hi"), sem("b_free")
        dve1, pool1, act1 = sem("dve1"), sem("pool1"), sem("act1")
        trig_in, trig = sem("trig_in"), sem("trig")
        squares, norms, roots, norm_max, scales = (sem(s) for s in ("squares", "norms", "roots", "norm_max", "scales"))
        b_made = sem("b_made")
        decay_arg, decay, phase = sem("decay_arg"), sem("decay"), sem("phase")
        sines, cosines, sin_made, cos_made = (sem(s) for s in ("sines", "cosines", "sin_made", "cos_made"))
        cb_made, qb_made, cp_made = sem("cb_made"), sem("qb_made"), sem("cp_made")
        ht_stored = [sem("ht_even_stored"), sem("ht_odd_stored")]

        ntask = count(lambda s: len(TASKS[s]))
        nscalar = count(lambda s: len(SCALAR_INDEX[s]))
        units = dict(first=8, mid=8, last=8)
        full = Signal(sem("full"), **ntask)
        free = Signal(sem("free"), **ntask)
        part_hi = Signal(sem("part_hi"), **nscalar)
        row_max = Signal(sem("row_max"), **units)
        neg_max = Signal(sem("neg_max"), **units)
        exps = Signal(sem("exps"), **units)
        recips = Signal(sem("recips"), **units)
        probs = Signal(sem("probs"), **units)
        nx = dict(lead=1, first=1, mid=1)
        pv = dict(mid=1, last=1, tail=1)
        three = lambda d: {k: TT * v for k, v in d.items()}
        x_var, x_rstd = Signal(sem("x_var"), **nx), Signal(sem("x_rstd"), **nx)
        xn_ready = Signal(sem("xn_ready"), **three(nx))
        h_in = Signal(sem("h_in"), lead=16, first=16, mid=16)
        hr_in = Signal(sem("hr_in"), first=16, mid=16, last=16)
        acc_full = Signal(sem("acc_full"), **three(pv))
        acc_free = Signal(sem("acc_free"), **three(pv))
        f_var, f_rstd = Signal(sem("f_var"), **pv), Signal(sem("f_rstd"), **pv)
        z_ready = Signal(sem("z_ready"), **three(pv))
        lg_in, lg_exp = Signal(sem("lg_in"), **pv), Signal(sem("lg_exp"), **pv)
        w_ready, out_ready = Signal(sem("w_ready"), **pv), Signal(sem("out_ready"), **pv)
        out_stored = Signal(sem("out_stored"), mid=16, last=16, tail=16)
        x_steps, f_steps = 2, 11
        vec = Signal(sem("vec"), lead=x_steps, first=x_steps, mid=x_steps + f_steps, last=f_steps, tail=f_steps)

        pe_passed, dve_passed = sem("pe_passed"), sem("dve_passed")

        block = ctx.enter_context(nc.Block())

        LEAD, FIRST, LAST, TAIL = Where("lead", 0), Where("first", 0), Where("last", PAIRS - 1), Where("tail", PAIRS)

        def banks_of(w, g, b2, r2):
            return 1 + (b2 == 1 and r2 == 1 and padded(g, w.prev, w.next))

        def bodies(eng, lead, body, tail):
            lead(LEAD)
            body(FIRST)
            with eng.Fori(1, PAIRS - 1) as p:
                body(Where("mid", p))
            body(LAST)
            tail(TAIL)

        NG = NCH // CPG
        GT = 2 + BATCH
        W_TASKS = [("q", j) for j in range(NKV * GROUP)] + [("p", j, e) for j in range(KT) for e in range(0, NH, 4)]
        W_FROM, W_EACH = 6, 3

        def w_tasks(c):
            n = len(W_TASKS)
            return range(min(n, max(0, c - W_FROM) * W_EACH), min(n, max(0, c + 1 - W_FROM) * W_EACH))

        def head_pieces(part, j):
            if j < QPG:
                first = qT[:, part, :, j * S0:(j + 1) * S0]
                rest = qT[:, part, :, QPG * S0 + j * S1:QPG * S0 + (j + 1) * S1]
            else:
                first, rest = kT[:, part, :, 0:S0], kT[:, part, :, S0:SEQ]
            return [(first, lambda b: b[:, 0:2 * S0].rearrange("p (b s) -> p b s", b=2)),
                    (rest, lambda b: b[:, 2 * S0:PT].rearrange("p (b s) -> p b s", b=2))]

        def token_pieces(part, j):
            def piece(at, start, n):
                return (xT[:, part, :, at:at + n], lambda b: b[:, :].rearrange("p (k s) -> p k s", k=KT)[:, :, start:start + n])
            if j == 0:
                return [piece(0, 0, P)]
            if j == 1:
                return [piece(2 * S0, 0, S1), piece(S0, S1, P - S1)]
            return [piece(S0 + P - S1, 0, S1), piece(2 * S0 + S1, S1, S1)]

        def probs_out(part, i):
            if i < 2:
                return PT0[:, part, i, :, 0:S0]
            if i == 2:
                return PT0[:, part].rearrange("p b h s -> p (b h) s")[:, :, S0:SEQ]
            return PT1[:, part, :, :]

        def probs_in(b, i):
            if i < 2:
                return b[:, :].rearrange("p (h s) -> p h s", h=QPG)
            if i == 2:
                return b[:, :].rearrange("p (h s) -> p h s", h=2 * QPG)
            return b[:, 0:2 * P].rearrange("p (h s) -> p h s", h=QPG)

        def in_table(c):
            return c // CPG % 2, slice(CH * (c % CPG), CH * (c % CPG + 1))

        def j_of(t):
            return t.unsqueeze(3).broadcast_to([P, CH, NJ, NK_])

        def k_of(t):
            return t.unsqueeze(2).broadcast_to([P, CH, NJ, NK_])

        def g_of(r, c):
            return G[:, r, :, CH * c:CH * (c + 1)].rearrange("p c h -> p h c").unsqueeze(2).broadcast_to([P, CH, NA, BATCH])

        def a_of(t):
            return t.unsqueeze(3).broadcast_to([P, CH, NA, BATCH])

        def by_channel(v, g, n):
            return v[:, TAB_H * g:TAB_H * (g + 1)].unsqueeze(2).broadcast_to([P, TAB_H, n])

        def by_column(c0):
            return cst[:, c0:c0 + NTAB].unsqueeze(1).broadcast_to([P, TAB_H, NTAB])

        @block.sync
        def _(sp):
            sp.dma_start(cst[:, :], const).then_inc(const_in, 16)
            for d in range(2):
                for i, src in enumerate((a_imag, inv_a_real)):
                    sp.dma_start(par_in[:, :, i, d, :], src.rearrange("(s p) n -> p s n", p=HHALF)).then_inc(par_loaded, 16)
                sp.dma_start(b_in[:, :, d, :], b_ri.rearrange("(s p) n r -> p s (n r)", p=HHALF)).then_inc(par_loaded, 16)
            sp.dma_start(el[:, 0, :], log_dt.rearrange("(o h) -> o h", o=1).broadcast_to([P, SEQ])).then_inc(par_loaded, 16)
            x_rows = x.rearrange("c (s p) n r -> p c s (n r)", p=HHALF)
            for half, dst in enumerate((x_a, x_b)):
                for d in range(2):
                    sp.dma_start(dst[:, :, :, d, :], x_rows[:, half * (BATCH // 2):(half + 1) * (BATCH // 2)]).then_inc(x_loaded[half], 16)
            sp.dma_start(wq[:, :, :, :, :].rearrange("p j a k d -> p j (a k d)").bitcast(F32),
                         w_qkv.rearrange("(j p) l -> p j l", p=P)).then_inc(wq_loaded, 16)
            sp.dma_start(wp[:, :, :, :, :].rearrange("p j h a d -> p j (h a d)").bitcast(F32),
                         w_proj.rearrange("(j p) e -> p j e", p=P)).then_inc(wp_loaded, 16)
            sp.dma_start(r_in[:, :], r_weight).then_inc(r_loaded, 16)
            sp.dma_start(eb[:, :], e_bias).then_inc(r_loaded, 16)
            sp.dma_start(rb[:, :], r_bias.rearrange("(o h) -> o h", o=1).broadcast_to([P, EXPERTS])).then_inc(r_loaded, 16)
            h_blocks = h_dram.rearrange("(c h) (a b) -> a c h b", c=BATCH, a=NA)
            for g in range(SEQ // STORE_H):
                sp.wait_ge(a_free, GT + STORE_H // BANK_H * (g + 1))
                for a in range(NA):
                    sp.dma_start(h_blocks[a][:, STORE_H * g:STORE_H * (g + 1), :],
                                 ht[a * BATCH:(a + 1) * BATCH, g % 2, :, :]).then_inc(ht_stored[g % 2], 16)

            def load_h(w, q):
                sp.dma_start(H[:, :, :], h_dram[bass.ds(q * PT, PT), :].rearrange("(t p) l -> p t l", p=P)).then_inc(h_in.sem, 16)

            def lead(w):
                for i in range(2):
                    sp.wait_ge(ht_stored[i], 16 * NA * (SEQ // STORE_H // 2))
                load_h(w, 0)

            def body(w):
                if w.next:
                    await_(sp, xn_ready, w, 0)
                    load_h(w, w.p + 1)
                if w.prev:
                    await_(sp, acc_free, w, TT)
                sp.dma_start(Hr[:, :, :], h_dram[bass.ds(w.p * PT, PT), :].rearrange("(t p) l -> p t l", p=P)).then_inc(hr_in.sem, 16)
                if w.prev:
                    store_out(w, w.p - 1)

            def store_out(w, q):
                await_(sp, out_ready, w, 1)
                sp.dma_start(out_rows[bass.ds(q * PT, PT), :].rearrange("(t p) l -> p t l", p=P),
                             z[:, :, :]).then_inc(out_stored.sem, 16)

            def tail(w):
                store_out(w, PAIRS - 1)
                await_(sp, out_stored, w, 16)

            bodies(sp, lead, body, tail)

        @block.tensor
        def _(pe):
            pe.wait_ge(const_in, 16)
            na, nb = [0], [0]

            def bank_a():
                if na[0] >= len(results):
                    pe.wait_ge(a_free, na[0] - len(results) + 1)
                na[0] += 1
                return results[(na[0] - 1) % len(results)]

            def bank_b():
                if nb[0] >= len(weights):
                    pe.wait_ge(b_free, nb[0] - len(weights) + 1)
                nb[0] += 1
                return weights[(nb[0] - 1) % len(weights)]

            pe.wait_ge(par_loaded, 16 * 7)
            for i in range(2):
                b = bank_a()
                for k in range(2):
                    for s in range(2):
                        if i == 0:
                            src = par_in[:, s, k, :, :].rearrange("p d n -> p (d n)")
                        else:
                            src = b_in[:, s, :, :].rearrange("p d n -> p (d n)")[:, k::2]
                        mm = pe.transpose(b[:, (2 * k + s) * HHALF:(2 * k + s + 1) * HHALF], src, ident[0:HHALF, 0:HHALF])
                mm.then_inc(a_full, 1)
            for c in range(0, BATCH, 2):
                xs, c0 = (x_a, 0) if c < BATCH // 2 else (x_b, BATCH // 2)
                if c == c0:
                    pe.wait_ge(x_loaded[bool(c0)], 32)
                for r in range(2):
                    b = bank_a()
                    for k in range(2):
                        for s in range(2):
                            src = xs[:, c - c0 + k, s, :, :].rearrange("p d m -> p (d m)")[:, r::2]
                            mm = pe.transpose(b[:, (2 * k + s) * HHALF:(2 * k + s + 1) * HHALF], src, ident[0:HHALF, 0:HHALF])
                    mm.then_inc(a_full, 1)
            for c in range(NCH):
                pe.wait_ge(qb_made, c + 1)
                pe.wait_ge(cp_made, c + 1)
                for h0 in range(0, CH, BANK_H):
                    b = bank_a()
                    for h in range(h0, h0 + BANK_H):
                        for i, q in enumerate((QA, QB)):
                            mm = pe.matmul(b[0:NA * BATCH, P * (h - h0):P * (h - h0 + 1)], CP[:, c % 2, h].rearrange("p a c -> p (a c)"),
                                           q[:, c % 2, h].rearrange("p j k -> p (j k)"), start=(i == 0), stop=(i == 1))
                    mm.then_inc(a_full, 1)
                for t in w_tasks(c):
                    task = W_TASKS[t]
                    if t == 0:
                        pe.wait_ge(wq_loaded, 16)
                    if task[0] == "p" and W_TASKS[t - 1][0] == "q":
                        pe.wait_ge(wp_loaded, 16)
                    b = bank_b()
                    if task[0] == "q":
                        src = wq[:, task[1]].rearrange("p a k d -> p (a k d)").bitcast(F32)
                    else:
                        src = wp[:, task[1], task[2]:task[2] + 4].rearrange("p h a d -> p (h a d)").bitcast(F32)
                    for k in range(4):
                        mm = pe.transpose(b[:, k * P:(k + 1) * P], src[:, k * P:(k + 1) * P], ident)
                    mm.then_inc(b_full, 1)
            pe.wait_ge(r_loaded, 48)
            b = bank_b()
            for k in range(KT):
                mm = pe.transpose(b[:, k * EXPERTS:(k + 1) * EXPERTS], r_in[:, k * P:(k + 1) * P], ident[0:EXPERTS, 0:EXPERTS])
            mm.then_inc(b_full, 1)
            pe.wait_ge(a_free, GT + NCH * (CH // BANK_H))
            pe.wait_ge(b_free, len(W_TASKS) + 1)

            def take(w, task):
                i = INDEX[w.seg][task]
                await_(pe, free, w, i + 1 - RING)
                return ring_bank[(ring_start(w) + i) % RING]

            def ready(w, task):
                await_(pe, free, w, INDEX[w.seg][task] + 1)

            def split_product(b, pairs_, rhs_of, lhs_of, last=True):
                n = len(pairs_)
                for i, t in enumerate(pairs_):
                    for c, (l, r) in enumerate(((0, 0), (0, 1), (1, 0))):
                        mm = pe.matmul(b, lhs_of(t, l), rhs_of(t, r), start=(i == 0 and c == 0),
                                       stop=(last and i == n - 1 and c == 2))
                return mm

            def xx(w):
                for j in range(TT):
                    await_(pe, xn_ready, w, j + 1)
                    b = take(w, ("XX", j))
                    for k in range(KT):
                        mm = pe.transpose(b[:, k * P:(k + 1) * P], xn[:, j, k * P:(k + 1) * P], ident)
                    mm.then_inc(full.sem, 1)

            def project(w, u, x_task):
                if x_task is not None:
                    ready(*x_task)
                for j in range(QPG + 1):
                    b = take(w, ("A", u, j))
                    row = GROUP * (u % NKV) + j
                    split_product(b[:, 0:PT], range(KT), lambda t, r: xT[:, r, t, :],
                                  lambda t, l: wq[:, row, l, t, :]).then_inc(full.sem, 1)

            def values(w):
                for t in range(TT):
                    b = take(w, ("V", t))
                    split_product(b[:, :], range(KT), lambda k, r: wq[:, QPG + 1::GROUP, r, k, :],
                                  lambda k, l: xT[:, l, k, t * P:(t + 1) * P]).then_inc(full.sem, 1)

            def turn_probs(w, g):
                for b2 in range(2):
                    await_(pe, probs, w, 2 * g + b2 + 1)
                    b = take(w, ("T", g, b2))
                    for h in range(QPG):
                        mm = pe.transpose(b[:, h * P:(h + 1) * P], P0[:, b2, h, :], ident)
                    mm.then_inc(full.sem, 1)
                b = take(w, ("T", g, 2))
                for b2 in range(2):
                    for r2 in range(2):
                        mm = pe.transpose(b[:, (2 * b2 + r2) * P:(2 * b2 + r2 + 1) * P], P1[:, r2, b2, 0:S0], ident)
                mm.then_inc(full.sem, 1)
                b = take(w, ("T", g, 3))
                for r2 in range(2):
                    mm = pe.transpose(b[:, r2 * P:(r2 + 1) * P], P2[:, r2, :, :].rearrange("p b s -> p (b s)"), ident)
                mm.then_inc(full.sem, 1)

            def attend(w, g):
                ready(w, ("T", g, 3))
                if g == 0:
                    ready(w, ("V", TT - 1))
                for b2 in range(2):
                    for r2 in range(2):
                        b = take(w, ("D", g, b2, r2))
                        split_product(b[:, 0:PT], range(1), lambda t, r: PT0[:, r, b2, 2 * r2:2 * r2 + 2, :],
                                      lambda t, l: V[:, l, b2, g * D:(g + 1) * D], last=False)
                        tail_rows = b[:, 0:PT].rearrange("p (h s) -> p h s", h=2)[:, :, S0:SEQ]
                        half = slice(b2 * S1, (b2 + 1) * S1)
                        for c, (l, r) in enumerate(((0, 0), (0, 1), (1, 0))):
                            mm = pe.matmul(tail_rows, V[half, l, 2, g * D:(g + 1) * D], PT1[half, r, 2 * r2:2 * r2 + 2, :],
                                           start=False, stop=(c == 2))
                        mm.then_inc(full.sem, banks_of(w, g, b2, r2))

            def turn_z(w):
                for j in range(TT):
                    await_(pe, z_ready, w, j + 1)
                    b = take(w, ("Z", j))
                    for k in range(KT):
                        mm = pe.transpose(b[:, k * P:(k + 1) * P], z[:, j, k * P:(k + 1) * P], ident)
                    mm.then_inc(full.sem, 1)

            def logits(w):
                ready(w, ("Z", TT - 1))
                b = take(w, ("LG",))
                for j in range(TT):
                    for k in range(KT):
                        mm = pe.matmul(b[:, j * EXPERTS:(j + 1) * EXPERTS], zT[:, j, k, :], rwT[:, k, :],
                                       start=(k == 0), stop=(k == KT - 1))
                mm.then_inc(full.sem, 1)

            def turn_weights(w):
                b = take(w, ("WT",))
                await_apart(pe, w_ready, w, 1, pe_passed)
                for j in range(TT):
                    mm = pe.transpose(b[0:EXPERTS, j * P:(j + 1) * P], lg[:, 0, j, :], ident)
                mm.then_inc(full.sem, 1)

            def experts(w):
                ready(w, ("WT",))
                for j in range(TT):
                    b = take(w, ("EB", j))
                    pe.matmul(b[:, :], wT[:, j, :], eb[:, :], start=True, stop=True).then_inc(full.sem, 1)

            def lead(w):
                xx(w)
                project(w, 0, (w, ("XX", TT - 1)))

            def body(w):
                for g in range(NKV):
                    if g == 0:
                        if w.seg == "first":
                            await_(pe, free, LEAD, INDEX["lead"][("A", 0, QPG)] + 1)
                        elif w.seg == "mid":
                            await_(pe, free, w, INDEX["mid"][("A", NKV, QPG)] + 1 - len(TASKS["mid"]))
                        else:
                            await_(pe, free, w, INDEX["mid"][("A", NKV, QPG)] + 1 - len(TASKS["mid"]))
                    else:
                        ready(w, ("A", g, QPG))
                    scores_only(w, g)
                    if g < NKV - 1 or w.next:
                        project(w, g + 1, (w, ("XX", TT - 1)) if g == NKV - 1 else None)
                    if g == 0:
                        values(w)
                    if g == 0 and w.prev:
                        await_(pe, free, w, INDEX["mid"][("D", NKV - 1, 1, 1)] + 1 - len(TASKS["mid"]))
                    if g > 0 or w.prev:
                        output_group(w, (g - 1) % NKV, (0, 1) if g > 0 else (0,))
                    turn_probs(w, g)
                    if g > 0 or w.prev:
                        output_group(w, (g - 1) % NKV, (2,) if g > 0 else (1, 2))
                    if g == 2 and w.prev:
                        turn_z(w)
                    if g == 3 and w.prev:
                        turn_weights(w)
                    attend(w, g)
                    if g == 2 and w.prev:
                        logits(w)
                    if g == 2 and w.next:
                        xx(w)
                    if g == 3 and w.prev:
                        experts(w)

            def scores_only(w, g):
                for b2 in range(2):
                    b = take(w, ("S", g, b2, 0))
                    for h in range(QPG):
                        mm = split_product(b[:, h * S0:(h + 1) * S0], range(1),
                                           lambda t, r: kT[:, r, b2, 0:S0],
                                           lambda t, l: qT[:, l, b2, h * S0:(h + 1) * S0])
                    mm.then_inc(full.sem, 1)
                    b = take(w, ("S", g, b2, 1))
                    for r2 in range(2):
                        mm = split_product(b[:, r2 * SEQ:(r2 + 1) * SEQ], range(1),
                                           lambda t, r: kT[:, r, b2, :],
                                           lambda t, l: qT[:, l, b2, QPG * S0 + r2 * P:QPG * S0 + (r2 + 1) * P])
                    mm.then_inc(full.sem, 1)

            def output_group(w, g, tiles):
                if g < NKV - 1:
                    ready(w, ("D", g, 1, 1))
                for j in tiles:
                    if g == 0 and w.prev:
                        await_(pe, acc_free, w, j + 1)
                    for h in range(QPG):
                        for c, (l, r) in enumerate(((0, 0), (0, 1), (1, 0))):
                            mm = pe.matmul(acc[j][:, :], oT[:, l, h, j * P:(j + 1) * P], wp[:, :, g * QPG + h, r, :],
                                           start=(g == 0 and h == 0 and c == 0), stop=(g == NKV - 1 and h == QPG - 1 and c == 2))
                    if g == NKV - 1:
                        mm.then_inc(acc_full.sem, 1)

            def tail(w):
                await_(pe, free, LAST, INDEX["last"][("D", NKV - 1, 1, 1)] + 1)
                output_group(w, NKV - 1, range(TT))
                turn_z(w)
                logits(w)
                turn_weights(w)
                experts(w)

            bodies(pe, lead, body, tail)

        @block.scalar
        def _(act):
            na = [0]

            def bank_a():
                na[0] += 1
                act.wait_ge(a_full, na[0])
                return results[(na[0] - 1) % len(results)]

            def cp(out_, in_):
                return act.activation(out_, in_, ACT.Copy)

            b = bank_a()
            cp(pw[:, 0, :], b[:, 0:SEQ])
            cp(el[:, 1, :], b[:, SEQ:2 * SEQ]).then_inc(a_free, 1)
            b = bank_a()
            cp(pw[:, 1:3, :], b[:, 0:2 * SEQ].rearrange("p (k h) -> p k h", k=2)).then_inc(a_free, 1)
            def table(g):
                i = g % 2
                act.wait_ge(decay_arg, g + 1)
                act.activation(decay_t[:, :, :], decay_t[:, :, :], ACT.Exp).then_inc(decay, 1)
                if g >= 2:
                    act.wait_ge(qb_made, CPG * (g - 1))
                    act.wait_ge(cp_made, CPG * (g - 1))
                act.wait_ge(phase, g + 1)
                act.activation(cos_t[:, i], phase_t[:, :, :], ACT.Sin, scale=TWO_PI / 2).then_inc(act1, 1)
                act.activation(sin_t[:, i, :, 0:NKA], phase_t[:, :, 0:NKA], ACT.Sin, scale=TWO_PI)
                act.activation(sin_t[:, i, :, NKA:], phase_t[:, :, NKA:], ACT.Sin, scale=-TWO_PI).then_inc(sines, 1)
                act.wait_ge(act1, 2 * g + 1)
                act.activation(cos_t[:, i], cos_t[:, i], ACT.Square).then_inc(act1, 1)
                act.wait_ge(act1, 2 * g + 2)
                act.activation(cos_t[:, i], cos_t[:, i], ACT.Identity, scale=-2.0, bias=cst[:, C_ONE:C_ONE + 1]).then_inc(cosines, 1)

            act.wait_ge(const_in, 16)
            act.wait_ge(trig_in, 1)
            act.activation(pw[:, 6, :], re[:, :], ACT.Tanh, scale=0.5).then_inc(trig, 1)
            act.activation(pw[:, 7, :], pw[:, 5, :], ACT.Sin, scale=TWO_PI).then_inc(trig, 1)
            act.activation(pw[:, 8, :], pw[:, 5, :], ACT.Sin, scale=TWO_PI / 2).then_inc(trig, 1)
            table(0)
            for c in range(0, BATCH, 2):
                for r in range(2):
                    b = bank_a()
                    cp(G[:, r, c:c + 2, :], b[:, 0:2 * SEQ].rearrange("p (c h) -> p c h", c=2)).then_inc(a_free, 1)

            wq_flat = wq[:, :, :, :, :].rearrange("p j a k d -> p (j a k d)").bitcast(F32)
            wp_flat = wp[:, :, :, :, :].rearrange("p j h a d -> p (j h a d)").bitcast(F32)
            n_sq = [0]

            def square(n):
                for i in range(n_sq[0], n_sq[0] + n):
                    if i == 0:
                        act.wait_ge(wq_loaded, 16)
                    if i == 12:
                        act.wait_ge(wp_loaded, 16)
                    src = wq_flat[:, i * 1024:(i + 1) * 1024] if i < 12 else wp_flat[:, (i - 12) * 1024:(i - 11) * 1024]
                    if i:
                        act.wait_ge(squares, i)
                    act.activation(junk[:, :], src, ACT.Square, scale=2.0 ** -7, accum_out=sq[:, i:i + 1]).then_inc(squares, 1)
                n_sq[0] += n

            for c in range(NCH):
                if c % CPG == 0 and c // CPG + 1 < NG:
                    table(c // CPG + 1)
                if c < 4:
                    square(5)
                if c == 4:
                    act.wait_ge(norms, 1)
                    act.activation(wsc[:, 2:4], wsc[:, 0:2], ACT.Sqrt, scale=2.0 ** 14).then_inc(roots, 1)
                store, h0 = divmod(CH * c, STORE_H)
                if h0 == 0 and store >= 2:
                    act.wait_ge(ht_stored[store % 2], 16 * NA * (store // 2))
                for h in range(h0, h0 + CH, BANK_H):
                    b = bank_a()
                    cp(ht[0:NA * BATCH, store % 2, h:h + BANK_H, :],
                       b[0:NA * BATCH, :].rearrange("p (h b) -> p h b", h=BANK_H)).then_inc(a_free, 1)
                for t in w_tasks(c):
                    if t == 0:
                        act.wait_ge(scales, 1)
                    act.wait_ge(b_full, t + 1)
                    src = weights[t % len(weights)][:, :].rearrange("p (k d) -> p k d", k=4)
                    if W_TASKS[t][0] == "q":
                        hi = wq[:, W_TASKS[t][1], 0, :, :]
                    else:
                        hi = wp[:, W_TASKS[t][1], W_TASKS[t][2]:W_TASKS[t][2] + 4, 0, :]
                    act.activation(hi, src, ACT.Copy, scale=s_q if W_TASKS[t][0] == "q" else s_p).then_inc(b_hi, 1)

            act.preload_act_table(ACT.Exp)

            def copy_part(w, task, pieces, scale=1.0):
                i = INDEX[w.seg][task]
                await_(act, full, w, i + 1)
                b = ring_bank[(ring_start(w) + i) % RING]
                for out_, in_of in pieces:
                    ins = act.activation(out_, in_of(b), ACT.Copy, scale=scale)
                ins.then_inc(part_hi.sem, 1)

            def project(w, u):
                for j in range(QPG + 1):
                    copy_part(w, ("A", u, j), head_pieces(0, j), QKV_EVAC)

            def xx(w):
                for j in range(TT):
                    copy_part(w, ("XX", j), token_pieces(0, j), X_SCALE)

            def lead(w):
                xx(w)
                project(w, 0)

            def router_exp(w):
                await_(act, lg_in, w, 1)
                act.activation(lg[:, 1], lg[:, 0], ACT.Exp).then_inc(lg_exp.sem, 1)

            def body(w):
                for g in range(NKV):
                    for b2 in range(2):
                        await_(act, neg_max, w, 2 * g + b2 + 1)
                        for i in range(6):
                            t = P0[:, b2, i, :] if i < QPG else P1[:, i - QPG, b2, :]
                            e = act.activation(t, t, ACT.Exp, bias=nmx[:, b2, i:i + 1], scale=alpha,
                                               accum_out=sums[:, b2, i:i + 1])
                        e.then_inc(exps.sem, 1)
                    if g < NKV - 1 or w.next:
                        project(w, g + 1)
                    if g == 0:
                        for t in range(TT):
                            copy_part(w, ("V", t), [(V[:, 0, t, :], lambda b: b[:, :])], QKV_EVAC)
                    for i in range(4):
                        copy_part(w, ("T", g, i), [(probs_out(0, i), lambda b: probs_in(b, i))], P_SCALE)
                    for b2 in range(2):
                        for r2 in range(2):
                            copy_part(w, ("D", g, b2, r2), [(oT[:, 0, 2 * r2:2 * r2 + 2, b2 * SEQ:(b2 + 1) * SEQ],
                                      lambda b: b[:, 0:PT].rearrange("p (h s) -> p h s", h=2))], OUT_EVAC)
                    if g == 2 and w.prev:
                        router_exp(w)
                    if g == 2 and w.next:
                        xx(w)

            bodies(act, lead, body, router_exp)

        @block.gpsimd
        def _(pool):
            npool = [0]

            def own(ins):
                npool[0] += 1
                ins.then_inc(pool1, 1)
                pool.wait_ge(pool1, npool[0])

            def decay_args(g):
                if g:
                    pool.wait_ge(sin_made, g)
                    pool.wait_ge(cos_made, g)
                pool.tensor_tensor(decay_t[:, :, :], by_channel(re, g, NTAB), by_column(C_L), ALU.mult).then_inc(decay_arg, 1)

            def table(g):
                i = g % 2
                pool.wait_ge(decay, g + 1)
                pool.wait_ge(sines, g + 1)
                own(pool.tensor_tensor(sin_t[:, i], sin_t[:, i], decay_t[:, :, :], ALU.mult))
                pool.tensor_tensor(pg[:, 2], sin_t[:, i, :, NK_:NKA], by_channel(fr, g, NA), ALU.mult).then_inc(sin_made, 1)
                pool.wait_ge(cos_made, g + 1)
                own(pool.tensor_tensor(pg[:, 3], cos_t[:, i, :, NK_:NKA], by_channel(fi, g, NA), ALU.mult))
                pool.wait_ge(sin_made, g + 1)
                own(pool.tensor_tensor(pf_i[:, i], pg[:, 2], pg[:, 3], ALU.add))

            pool.wait_ge(const_in, 16)
            pool.wait_ge(trig_in, 1)
            decay_args(0)
            pool.wait_ge(b_made, 1)
            table(0)
            for c in range(NCH):
                g = c // CPG
                if c % CPG == 0 and g + 1 < NG:
                    decay_args(g + 1)
                if c % CPG == 2 and g + 1 < NG:
                    table(g + 1)
                if c == 5:
                    pool.wait_ge(roots, 1)
                    pool.partition_all_reduce(wsc[:, 4:6], wsc[:, 2:4], P, RMAX).then_inc(norm_max, 1)
                i, hs = in_table(c)
                if c == 0:
                    pool.wait_ge(a_free, GT)
                if c >= 2:
                    pool.wait_ge(cp_made, c - 1)
                    pool.wait_ge(a_full, GT + CH // BANK_H * (c - 1))
                pool.tensor_tensor(CB[:, c % 2], g_of(1, c), a_of(pf_i[:, i, hs]), ALU.mult).then_inc(cb_made, 1)
                pool.tensor_tensor(QB[:, c % 2], j_of(sin_t[:, i, hs, NKA:]), k_of(sin_t[:, i, hs, 0:NK_]), ALU.mult).then_inc(qb_made, 1)

            def normalise(w, g):
                for b2 in range(2):
                    await_(pool, recips, w, 2 * g + b2 + 1)
                    pool.tensor_tensor(P0[:, b2], P0[:, b2], rec[:, b2, 0:QPG].unsqueeze(2).broadcast_to([P, QPG, S0]), ALU.mult)
                    r1 = rec[:, b2, QPG:6].unsqueeze(2)
                    pool.tensor_tensor(P1[:, :, b2, 0:S0], P1[:, :, b2, 0:S0], r1.broadcast_to([P, 2, S0]), ALU.mult)
                    pool.tensor_tensor(P2[:, :, b2], P1[:, :, b2, S0:SEQ], r1.broadcast_to([P, 2, S1]), ALU.mult).then_inc(probs.sem, 1)

            def root(w, which, var, done):
                await_(pool, var, w, 1)
                pool.tensor_tensor(rstd[:, which, 1], rstd[:, which, 0], cst[:, C_HALF:C_HALF + TT], ALU.pow).then_inc(done.sem, 1)

            def body(w):
                for g in range(NKV):
                    normalise(w, g)
                    if g == 1 and w.prev:
                        root(w, 1, f_var, f_rstd)
                    if g == 1 and w.next:
                        root(w, 0, x_var, x_rstd)

            bodies(pool, lambda w: root(w, 0, x_var, x_rstd), body, lambda w: root(w, 1, f_var, f_rstd))

        @block.vector
        def _(dve):
            nd = [0]

            def own(ins):
                nd[0] += 1
                ins.then_inc(dve1, 1)
                dve.wait_ge(dve1, nd[0])

            def tt(o, a, b, op):
                own(dve.tensor_tensor(o, a, b, op))

            def ts(o, a, s1, s2, op0, op1):
                own(dve.tensor_scalar(o, a, s1, s2, op0, op1))

            def stt(o, a, s, b, op0, op1):
                own(dve.scalar_tensor_tensor(out=o, in0=a, scalar=s, in1=b, op0=op0, op1=op1))

            def low_weights(t):
                dve.wait_ge(b_hi, t + 1)
                task = W_TASKS[t]
                src = weights[t % len(weights)][:, :].rearrange("p (k d) -> p k d", k=4)
                if task[0] == "q":
                    hi, lo = wq[:, task[1], 0, :, :], wq[:, task[1], 1, :, :]
                else:
                    hi, lo = (wp[:, task[1], task[2]:task[2] + 4, i, :] for i in range(2))
                dve.scalar_tensor_tensor(out=lo, in0=src, scalar=s_q if task[0] == "q" else s_p, in1=hi,
                                         op0=ALU.mult, op1=ALU.subtract).then_inc(b_free, 1)

            dve.wait_ge(par_loaded, 16 * 7)
            dve.wait_ge(a_free, 2)
            elf = el[:, :, :].rearrange("p i h -> p (i h)")
            e0, e1, e2, e3 = (ev[:, i].rearrange("p i h -> p (i h)") for i in range(4))
            ts(e0, elf, LOG2E, ROUND, ALU.mult, ALU.add)
            ts(e0, e0, -ROUND, None, ALU.add, ALU.bypass)
            stt(e1, e0, -LN2_HI, elf, ALU.mult, ALU.add)
            stt(e1, e0, -LN2_LO, e1, ALU.mult, ALU.add)
            ts(e2, e1, 1.0 / 5040, None, ALU.mult, ALU.bypass)
            for c in (1.0 / 720, 1.0 / 120, 1.0 / 24, 1.0 / 6, 0.5, 1.0):
                stt(e2, e2, c, e1, ALU.add, ALU.mult)
            ts(e0, e0, 127.0 + 2.0 ** 23, None, ALU.add, ALU.bypass)
            own(dve.tensor_scalar(e3.bitcast(I32), e0.bitcast(I32), 23, None, ALU.logical_shift_left, ALU.bypass))
            stt(e2, e2, 1.0, e3, ALU.add, ALU.mult)
            dt, a = ev[:, 2, 0, :], ev[:, 2, 1, :]
            aim, br, bi = (pw[:, i, :] for i in range(3))
            r = lambda i: pw[:, i, :]
            stt(re[:, :], a, -1.0, dt, ALU.mult, ALU.mult)
            tt(r(3), aim, dt, ALU.mult)
            ts(r(3), r(3), INV_2PI, None, ALU.mult, ALU.bypass)
            ts(r(4), r(3), ROUND, -ROUND, ALU.add, ALU.add)
            tt(ur[:, :], r(3), r(4), ALU.subtract)
            ts(r(5), r(3), 0.5, None, ALU.mult, ALU.bypass)
            ts(r(4), r(5), ROUND, -ROUND, ALU.add, ALU.add)
            own(dve.tensor_tensor(r(5), r(5), r(4), ALU.subtract))
            dve.tensor_copy(r(4), r(5)).then_inc(trig_in, 1)

            def phases(g):
                if g:
                    dve.wait_ge(cosines, g)
                if g >= 2:
                    dve.wait_ge(cp_made, CPG * (g - 1))
                    dve.wait_ge(qb_made, CPG * (g - 1))
                tt(phase_t[:, :, :], by_channel(ur, g, NTAB), by_column(C_L), ALU.mult)
                tt(phase_t[:, :, :], phase_t[:, :, :], by_column(C_OFF), ALU.add)
                ts(cos_t[:, g % 2], phase_t[:, :, :], ROUND, -ROUND, ALU.add, ALU.add)
                dve.tensor_tensor(phase_t[:, :, :], phase_t[:, :, :], cos_t[:, g % 2], ALU.subtract).then_inc(phase, 1)

            def table(g):
                i = g % 2
                dve.wait_ge(decay, g + 1)
                dve.wait_ge(cosines, g + 1)
                own(dve.tensor_tensor(cos_t[:, i, :, 0:NKA], cos_t[:, i, :, 0:NKA], decay_t[:, :, 0:NKA], ALU.mult))
                dve.tensor_tensor(cos_j[:, i], cos_t[:, i, :, NKA:], decay_t[:, :, NKA:], ALU.mult).then_inc(cos_made, 1)
                tt(pg[:, 0], cos_t[:, i, :, NK_:NKA], by_channel(fr, g, NA), ALU.mult)
                dve.wait_ge(sin_made, g + 1)
                tt(pg[:, 1], sin_t[:, i, :, NK_:NKA], by_channel(fi, g, NA), ALU.mult)
                tt(pf_r[:, i], pg[:, 0], pg[:, 1], ALU.subtract)

            phases(0)
            dve.wait_ge(trig, 3)
            t_, sy, qy = r(6), r(7), r(8)
            ts(r(9), t_, -1.0, 1.0, ALU.mult, ALU.add)
            own(dve.reciprocal(r(10), r(9)))
            stt(r(9), t_, 2.0, r(10), ALU.mult, ALU.mult)
            tt(r(10), qy, qy, ALU.mult)
            ts(r(10), r(10), -2.0, 1.0, ALU.mult, ALU.add)
            stt(r(11), sy, 2.0, r(10), ALU.mult, ALU.mult)
            stt(r(12), sy, 2.0, sy, ALU.mult, ALU.mult)
            ts(r(13), r(12), -1.0, 1.0, ALU.mult, ALU.add)
            tt(r(13), r(13), r(9), ALU.mult)
            tt(r(13), r(13), r(12), ALU.subtract)
            stt(r(14), r(9), 1.0, r(11), ALU.add, ALU.mult)
            tt(r(9), a, a, ALU.mult)
            tt(r(10), aim, aim, ALU.mult)
            tt(r(9), r(9), r(10), ALU.add)
            own(dve.reciprocal(r(10), r(9)))
            tt(r(9), r(14), aim, ALU.mult)
            tt(r(11), r(13), a, ALU.mult)
            tt(r(9), r(9), r(11), ALU.subtract)
            tt(r(12), r(13), aim, ALU.mult)
            tt(r(11), r(14), a, ALU.mult)
            stt(r(12), r(12), -1.0, r(11), ALU.mult, ALU.subtract)
            stt(r(9), r(9), 2.0, r(10), ALU.mult, ALU.mult)
            stt(r(12), r(12), 2.0, r(10), ALU.mult, ALU.mult)
            tt(r(10), br, r(9), ALU.mult)
            tt(r(11), bi, r(12), ALU.mult)
            tt(fr[:, :], r(10), r(11), ALU.subtract)
            tt(r(10), br, r(12), ALU.mult)
            tt(r(11), bi, r(9), ALU.mult)
            dve.tensor_tensor(fi[:, :], r(10), r(11), ALU.add).then_inc(b_made, 1)
            dve.wait_ge(b_made, 1)
            table(0)

            for c in range(NCH):
                g = c // CPG
                i, hs = in_table(c)
                if c % CPG == 0 and g + 1 < NG:
                    phases(g + 1)
                if c % CPG == 2 and g + 1 < NG:
                    table(g + 1)
                if c == 4:
                    dve.wait_ge(squares, 20)
                    own(dve.tensor_reduce(wsc[:, 0:1], sq[:, 0:12], AX_X, ALU.add))
                    own(dve.tensor_reduce(wsc[:, 1:2], sq[:, 12:20], AX_X, ALU.add))
                    dve.tensor_scalar(wsc[:, 0:2], wsc[:, 0:2], NORM_FLOOR, None, ALU.max, ALU.bypass).then_inc(norms, 1)
                if c == W_FROM:
                    dve.wait_ge(norm_max, 1)
                    own(dve.tensor_scalar(wsc[:, 12:14].bitcast(I32), wsc[:, 4:6].bitcast(I32), 0x7F800000, None,
                                          ALU.bitwise_and, ALU.bypass))
                    own(dve.reciprocal(wsc[:, 14:16], wsc[:, 12:14]))
                    ts(wsc[:, 6:8], wsc[:, 14:16], W_SCALE, None, ALU.mult, ALU.bypass)
                    stt(alpha, wsc[:, 12:13], float(D) ** -0.5 / QKV_STORE ** 2, wsc[:, 12:13], ALU.mult, ALU.mult)
                    own(dve.tensor_scalar(wsc[:, 9:10], alpha, -1.0, None, ALU.mult, ALU.bypass))
                    dve.scalar_tensor_tensor(out=beta, in0=wsc[:, 12:13], scalar=1.0 / (QKV_STORE * W_SCALE), in1=wsc[:, 13:14],
                                             op0=ALU.mult, op1=ALU.mult).then_inc(scales, 1)
                if c == 0:
                    dve.wait_ge(a_free, GT)
                if c >= 2:
                    dve.wait_ge(a_full, GT + CH // BANK_H * (c - 1))
                if c:
                    dve.wait_ge(cp_made, c)
                own(dve.tensor_tensor(CA, g_of(0, c), a_of(pf_r[:, i, hs]), ALU.mult))
                dve.tensor_tensor(QA[:, c % 2], j_of(cos_j[:, i, hs]), k_of(cos_t[:, i, hs, 0:NK_]), ALU.mult)
                dve.wait_ge(cb_made, c + 1)
                dve.tensor_tensor(CP[:, c % 2], CA, CB[:, c % 2], ALU.subtract).then_inc(cp_made, 1)
                for t in w_tasks(c - 1) if c else ():
                    low_weights(t)
            for t in w_tasks(NCH - 1):
                low_weights(t)
            t = len(W_TASKS)
            dve.wait_ge(b_full, t + 1)
            dve.tensor_copy(rwT[:, :, :], weights[t % len(weights)][:, 0:KT * EXPERTS].rearrange("p (k e) -> p k e", k=KT)).then_inc(b_free, 1)

            steps = [0]

            def step(w, ins, apart=False):
                steps[0] += 1
                ins.then_inc(vec.sem, 1)
                if apart:
                    await_apart(dve, vec, w, steps[0], dve_passed)
                else:
                    await_(dve, vec, w, steps[0])

            def of(w, task):
                i = INDEX[w.seg][task]
                return ring_bank[(ring_start(w) + i) % RING]

            def low_part(w, task, pieces, hi_pieces, scale, banks=1):
                await_(dve, part_hi, w, SCALAR_INDEX[w.seg][task] + 1)
                for (lo, in_of), (hi, _) in zip(pieces, hi_pieces):
                    ins = dve.scalar_tensor_tensor(out=lo, in0=in_of(of(w, task)), scalar=scale, in1=hi,
                                                   op0=ALU.mult, op1=ALU.subtract)
                ins.then_inc(free.sem, banks)

            def h_stats(w):
                await_apart(dve, h_in, w, 16, dve_passed)
                for j in range(TT):
                    ins = dve.bn_stats(stat[:, 0, j, 0:6], H[:, j, :])
                step(w, ins, apart=True)
                normal(w, 0, x_var, vec, steps[0])

            def normal(w, which, var, signal, k):
                await_apart(dve, signal, w, k, dve_passed)
                for j in range(TT):
                    ins = dve.bn_aggr(mv[:, which, j, :], stat[:, which, j, 0:6])
                step(w, ins)
                dve.tensor_scalar(rstd[:, which, 0], mv[:, which, :, 1], EPS, None, ALU.add, ALU.bypass).then_inc(var.sem, 1)

            def x_norm(w):
                await_(dve, x_rstd, w, 1)
                for j in range(TT):
                    dve.tensor_scalar(xn[:, j, :], H[:, j, :], mv[:, 0, j, 0:1], rstd[:, 0, 1, j:j + 1],
                                      ALU.subtract, ALU.mult).then_inc(xn_ready.sem, 1)

            def xx(w):
                for j in range(TT):
                    low_part(w, ("XX", j), token_pieces(1, j), token_pieces(0, j), X_SCALE)

            def project(w, u, j):
                low_part(w, ("A", u, j), head_pieces(1, j), head_pieces(0, j), QKV_EVAC)

            def mask_max(w, g, b2):
                for r2 in range(2):
                    await_apart(dve, full, w, INDEX[w.seg][("S", g, b2, r2)] + 1, dve_passed)
                    b = of(w, ("S", g, b2, r2))
                    for i in range(QPG if r2 == 0 else 2):
                        if r2 == 0:
                            o, s, m, c = P0[:, b2, i, :], b[:, i * S0:(i + 1) * S0], mask0, i
                        else:
                            o, s, m, c = P1[:, i, b2, :], b[:, i * SEQ:(i + 1) * SEQ], mask1, QPG + i
                        ins = dve.tensor_tensor_reduce(o, s, m, 1.0, -3e38, ALU.add, ALU.max, mx[:, b2, c:c + 1])
                    ins.then_inc(free.sem, 1)
                await_(dve, free, w, INDEX[w.seg][("S", g, b2, 1)] + 1)
                dve.tensor_scalar(nmx[:, b2, :], mx[:, b2, :], wsc[:, 9:10], None, ALU.mult, ALU.bypass).then_inc(neg_max.sem, 1)

            def reciprocals(w, g, b2):
                await_(dve, exps, w, 2 * g + b2 + 1)
                dve.reciprocal(rec[:, b2, :], sums[:, b2, :]).then_inc(recips.sem, 1)

            def residual(w):
                await_(dve, hr_in, w, 0)
                await_(dve, out_ready, w, 0)
                for j in range(TT):
                    await_(dve, acc_full, w, j + 1)
                    dve.scalar_tensor_tensor(out=h2[:, j, :], in0=acc[j][:, :], scalar=beta, in1=Hr[:, j, :],
                                             op0=ALU.mult, op1=ALU.add).then_inc(acc_free.sem, 1)
                for j in range(TT):
                    await_(dve, acc_free, w, j + 1)
                    ins = dve.bn_stats(stat[:, 1, j, 0:6], h2[:, j, :])
                step(w, ins, apart=True)
                normal(w, 1, f_var, vec, steps[0])

            def z_norm(w):
                await_(dve, f_rstd, w, 1)
                await_(dve, out_stored, w, 0)
                for j in range(TT):
                    dve.tensor_scalar(z[:, j, :], h2[:, j, :], mv[:, 1, j, 0:1], rstd[:, 1, 1, j:j + 1],
                                      ALU.subtract, ALU.mult).then_inc(z_ready.sem, 1)

            def z_turned(w):
                for j in range(TT):
                    await_(dve, full, w, INDEX[w.seg][("Z", j)] + 1)
                    dve.tensor_copy(zT[:, j], of(w, ("Z", j))[:, :].rearrange("p (k s) -> p k s", k=KT)).then_inc(free.sem, 1)

            def router_in(w):
                await_(dve, full, w, INDEX[w.seg][("LG",)] + 1)
                dve.tensor_tensor(lg[:, 0], of(w, ("LG",))[:, 0:TT * EXPERTS].rearrange("p (t e) -> p t e", t=TT),
                                  rb[:, :].unsqueeze(1).broadcast_to([P, TT, EXPERTS]), ALU.add).then_inc(free.sem, 1)
                await_(dve, free, w, INDEX[w.seg][("LG",)] + 1)
                step(w, dve.tensor_reduce(small[:, 0, :], lg[:, 0], AX_X, ALU.max))
                dve.tensor_tensor(lg[:, 0], lg[:, 0], small[:, 0, :].unsqueeze(2).broadcast_to([P, TT, EXPERTS]),
                                  ALU.subtract).then_inc(lg_in.sem, 1)

            def router_out(w):
                await_(dve, lg_exp, w, 1)
                step(w, dve.tensor_reduce(small[:, 1, :], lg[:, 1], AX_X, ALU.add))
                step(w, dve.reciprocal(small[:, 2, :], small[:, 1, :]))
                step(w, dve.tensor_tensor(lg[:, 2], lg[:, 1], small[:, 2, :].unsqueeze(2).broadcast_to([P, TT, EXPERTS]), ALU.mult), apart=True)
                for j in range(TT):
                    ins = dve.max(out=top[:, j, :], in_=lg[:, 2, j, :])
                step(w, ins, apart=True)
                for j in range(TT):
                    ins = dve.match_replace(out=lg[:, 3, j, :], in_to_replace=top[:, j, :], in_values=lg[:, 2, j, :], imm_value=-1.0)
                step(w, ins)
                step(w, dve.tensor_scalar(lg[:, 3], lg[:, 3], 0.0, None, ALU.max, ALU.bypass))
                dve.tensor_tensor(lg[:, 0], lg[:, 2], lg[:, 3], ALU.subtract).then_inc(w_ready.sem, 1)
                await_(dve, w_ready, w, 1)
                step(w, dve.tensor_reduce(small[:, 3, :], lg[:, 0], AX_X, ALU.add))
                for j in range(TT):
                    ins = dve.scalar_tensor_tensor(out=h2[:, j, :], in0=z[:, j, :], scalar=small[:, 3, j:j + 1], in1=h2[:, j, :],
                                                   op0=ALU.mult, op1=ALU.add)
                step(w, ins)

            def weights_turned(w):
                await_(dve, full, w, INDEX[w.seg][("WT",)] + 1)
                dve.tensor_copy(wT[:, :, :], of(w, ("WT",))[0:EXPERTS, 0:TT * P].rearrange("p (t s) -> p t s", t=TT)).then_inc(free.sem, 1)

            def finish(w):
                for j in range(TT):
                    await_(dve, full, w, INDEX[w.seg][("EB", j)] + 1)
                    dve.tensor_tensor(z[:, j, :], of(w, ("EB", j))[:, :], h2[:, j, :], ALU.add).then_inc(free.sem, 1)
                await_(dve, free, w, INDEX[w.seg][("EB", TT - 1)] + 1)
                dve.tensor_copy(small[:, 0, :], small[:, 1, :]).then_inc(out_ready.sem, 1)

            def lead(w):
                steps[0] = 0
                h_stats(w)
                x_norm(w)
                xx(w)
                for j in range(QPG + 1):
                    project(w, 0, j)
                assert steps[0] == vec.n["lead"]

            def body(w):
                steps[0] = 0
                for g in range(NKV):
                    mask_max(w, g, 0)
                    mask_max(w, g, 1)
                    made = g < NKV - 1 or w.next
                    if made:
                        project(w, g + 1, 0)
                    reciprocals(w, g, 0)
                    if made:
                        project(w, g + 1, 1)
                    reciprocals(w, g, 1)
                    if g == 1 and w.prev:
                        residual(w)
                    if made:
                        for j in range(2, QPG + 1):
                            project(w, g + 1, j)
                    if g == 3 and w.prev:
                        router_out(w)
                    if g == 2 and w.next:
                        x_norm(w)
                    if g == 0:
                        for t in range(TT):
                            low_part(w, ("V", t), [(V[:, 1, t, :], lambda b: b[:, :])], [(V[:, 0, t, :], None)], QKV_EVAC)
                    for i in range(4):
                        low_part(w, ("T", g, i), [(probs_out(1, i), lambda b: probs_in(b, i))], [(probs_out(0, i), None)], P_SCALE)
                    if g == 1 and w.prev:
                        z_norm(w)
                    if g == 2 and w.prev:
                        z_turned(w)
                    if g == 3 and w.prev:
                        weights_turned(w)
                    for b2 in range(2):
                        for r2 in range(2):
                            o = [oT[:, i, 2 * r2:2 * r2 + 2, b2 * SEQ:(b2 + 1) * SEQ] for i in range(2)]
                            low_part(w, ("D", g, b2, r2), [(o[1], lambda b: b[:, 0:PT].rearrange("p (h s) -> p h s", h=2))],
                                     [(o[0], None)], OUT_EVAC, banks_of(w, g, b2, r2))
                    if g == 1 and w.next:
                        h_stats(w)
                    if g == 2 and w.prev:
                        router_in(w)
                    if g == 2 and w.next:
                        xx(w)
                    if g == 3 and w.prev:
                        finish(w)


            def tail(w):

                steps[0] = 0
                residual(w)
                z_norm(w)
                z_turned(w)
                router_in(w)
                router_out(w)
                weights_turned(w)
                finish(w)


            bodies(dve, lead, body, tail)


def ring_start(w):
    at, n = 0, {}
    for seg in SEGMENTS:
        n[seg] = at
        at = (at + len(TASKS[seg])) % RING
    assert len(TASKS["mid"]) % RING == 0
    return n[w.seg]


_INS = ["x", "L0_tok_log_dt", "L0_tok_B_ri", "L0_tok_inv_A_real", "L0_tok_A_imag", "L0_attn_weight_qkv",
        "L0_attn_weight_proj", "L0_ffn_router_weight", "L0_ffn_router_bias", "L0_ffn_expert_bias"]


def kernel(**inputs):
    import concourse.bacc as _bacc
    from concourse.bass_utils import run_bass_kernel_spmd as _run

    nc = _bacc.Bacc("TRN2", target_bir_lowering=False, num_devices=1)
    arrays, args = {}, []
    for name in _INS:
        a = np.ascontiguousarray(inputs[name])
        arrays[f"in_{name}"] = a
        args.append(nc.dram_tensor(f"in_{name}", a.shape, mybir.dt.from_np(a.dtype), kind="ExternalInput").ap())
    arrays["shape_constants"] = shape_constants()
    args.append(nc.dram_tensor("shape_constants", (P, NCONST), F32, kind="ExternalInput").ap())
    out = nc.dram_tensor("out", (BATCH, SEQ, HID), F32, kind="ExternalOutput").ap()
    vit_tower(nc, *args, out)
    r = _run(nc, [arrays], core_ids=[0])
    return r.results[0]["out"]
```

```python
from contextlib import ExitStack

import numpy as np

import concourse.bass as bass
from concourse import mybir

F32 = mybir.dt.float32
F16 = mybir.dt.float16
I32 = mybir.dt.int32
ALU = mybir.AluOpType
ACT = mybir.ActivationFunctionType
AX_X = mybir.AxisListType.X
RMAX = bass.bass_isa.ReduceOp.max

P = 128
BATCH, SEQ, MODES = 16, 192, 64
HID = 512
NKV, QPG, D = 4, 4, 128
NH = NKV * QPG
GROUP = QPG + 2
KT = HID // P
PAIRS = BATCH // 2
PT = 2 * SEQ
TT = PT // P
S0, S1 = P, SEQ - P
EXPERTS, TOP_K = 64, 8
EPS = 1e-5

NK_, NA, NJ = 16, HID // P, 8
NKA = NK_ + NA
NTAB = NKA + NJ
TAB_H = 32
CH = 8
CPG, NCH = TAB_H // CH, SEQ // CH
STORE_H = 16
BANK_H = 4
HHALF = SEQ // 2

X_SCALE = 2.0 ** 10
W_SCALE = 2.0 ** 14
QKV_STORE = 2.0 ** 9
P_SCALE = 2.0 ** 14
QKV_EVAC = QKV_STORE / (X_SCALE * W_SCALE)
OUT_EVAC = 1.0 / P_SCALE
NORM_FLOOR = 2.0 ** -60

MASKED = -1e30
ROUND = 1.5 * 2.0 ** 23
TWO_PI = 6.283185
LOG2E = 1.4426950408889634
LN2_HI, LN2_LO = 0.693145751953125, 1.4286068203094172e-06
INV_2PI = 0.15915494309189535

C_ID, C_M0, C_M1 = 0, P, 2 * P
C_L = C_M1 + SEQ
C_OFF = C_L + NTAB
C_HALF = C_OFF + NTAB
C_ONE = C_HALF + 3
NCONST = C_ONE + 1


def shape_constants():
    c = np.zeros((P, NCONST), np.float32)
    p, s = np.arange(P)[:, None], np.arange(SEQ)[None, :]
    c[:, C_ID:C_ID + P] = np.eye(P)
    c[:, C_M0:C_M0 + P] = np.where(s[:, :P] <= p, 0.0, MASKED)
    c[:, C_M1:C_M1 + SEQ] = np.where(s <= S0 + p % S1, 0.0, MASKED)
    c[:, C_L:C_L + NTAB] = [*range(NK_), *range(0, HID, P), *range(0, P, NK_)]
    imag = p >= MODES
    c[:, C_OFF:C_OFF + NK_] = np.where(imag, -0.25, 0.0)
    c[:, C_OFF + NK_:C_OFF + NKA] = np.where(imag, 0.25, 0.0)
    c[:, C_HALF:C_HALF + 3] = -0.5
    c[:, C_ONE] = 1.0
    return c


RING = 5


def padded(g, prev, nxt):
    return prev and nxt and g < NKV - 1


def slot_tasks(g, prev, nxt):
    out = [("S", g, b, r) for b in range(2) for r in range(2)]
    if g < NKV - 1 or nxt:
        out += [("A", g + 1, j) for j in range(QPG + 1)]
    if g == 0:
        out += [("V", t) for t in range(TT)]
    out += [("T", g, i) for i in range(4)]
    if g == 2 and prev:
        out += [("Z", j) for j in range(TT)]
    if g == 3 and prev:
        out += [("WT",)]
    out += [("D", g, b, r) for b in range(2) for r in range(2)]
    if padded(g, prev, nxt):
        out += [("PAD", g)]
    if g == 2 and prev:
        out += [("LG",)]
    if g == 2 and nxt:
        out += [("XX", j) for j in range(TT)]
    if g == 3 and prev:
        out += [("EB", j) for j in range(TT)]
    return out


def body_tasks(prev, nxt):
    return [t for g in range(NKV) for t in slot_tasks(g, prev, nxt)]


TASKS = {
    "lead": [("XX", j) for j in range(TT)] + [("A", 0, j) for j in range(QPG + 1)],
    "first": body_tasks(False, True),
    "mid": body_tasks(True, True),
    "last": body_tasks(True, False),
    "tail": [("Z", j) for j in range(TT)] + [("LG",), ("WT",)] + [("EB", j) for j in range(TT)],
}
SEGMENTS = list(TASKS)
ON_SCALAR = ("A", "V", "T", "D", "XX", "Z")
INDEX = {seg: {t: i for i, t in enumerate(ts)} for seg, ts in TASKS.items()}
SCALAR_INDEX = {seg: {t: i for i, t in enumerate([t for t in ts if t[0] in ON_SCALAR])} for seg, ts in TASKS.items()}


class Where:

    def __init__(self, seg, p):
        self.seg, self.p = seg, p
        self.prev = seg in ("mid", "last")
        self.next = seg in ("first", "mid")


class Signal:

    def __init__(self, sem, lead=0, first=0, mid=0, last=0, tail=0):
        self.sem = sem
        self.n = dict(lead=lead, first=first, mid=mid, last=last, tail=tail)

    def at(self, w, k):
        n, i = self.n, SEGMENTS.index(w.seg)
        before = sum(n[s] * (PAIRS - 2 if s == "mid" else 1) for s in SEGMENTS[:i])
        if w.seg != "mid":
            return before + k
        return w.p * n["mid"] + (before - n["mid"] + k)


def count(f):
    return {seg: f(seg) for seg in SEGMENTS}


def await_(eng, signal, w, k):
    v = signal.at(w, k)
    if not (isinstance(v, int) and v <= 0):
        eng.wait_ge(signal.sem, v)


def await_apart(eng, signal, w, k, spare):
    await_(eng, signal, w, k)
    if not isinstance(w.p, int):
        eng.sem_inc(spare, 1)


def vit_tower(nc, x, log_dt, b_ri, inv_a_real, a_imag, w_qkv, w_proj, r_weight, r_bias, e_bias, const, out):
    with ExitStack() as ctx:
        def sb(name, shape, dt=F32, c=ctx):
            return c.enter_context(nc.sbuf_tensor(name, shape, dt))

        def sem(name):
            return ctx.enter_context(nc.semaphore(name))

        h_dram = nc.dram_tensor("h_tokens", (BATCH * SEQ, HID), F32, kind="Internal").ap()
        out_rows = out.rearrange("c s l -> (c s) l")

        bank = [ctx.enter_context(nc.psum_tensor(f"bank{i}", [P, 512], F32)) for i in range(8)]
        ring_bank, acc = bank[:RING], bank[RING:]

        wq = sb("wq", [P, NKV * GROUP, 2, KT, P], F16)
        wp = sb("wp", [P, KT, NH, 2, P], F16)
        cst = sb("cst", [P, NCONST])
        ident = cst[:, C_ID:C_ID + P]
        mask0, mask1 = cst[:, C_M0:C_M0 + P], cst[:, C_M1:C_M1 + SEQ]
        rwT = sb("rwT", [P, KT, 2, EXPERTS], F16)
        eb_hi, eb_lo = sb("eb_hi", [2 * EXPERTS, HID], F16), sb("eb_lo", [EXPERTS, HID], F16)
        rb = sb("rb", [P, EXPERTS])
        sq = sb("sq", [P, 24])
        wsc = sb("wsc", [P, 32])
        w_sq, w_norm, w_max, w_pow, w_inv, w_scale = (wsc[:, 4 * i:4 * i + 4] for i in range(6))
        s_q, s_p, s_e, s_r = (w_scale[:, i:i + 1] for i in range(4))
        alpha, minus_alpha, beta, gamma, delta = (wsc[:, 24 + i:25 + i] for i in range(5))

        one = ExitStack()
        G = sb("G", [P, 2, BATCH, SEQ], c=one)
        ht = sb("ht", [P, 2, STORE_H, P], c=one)
        x_a = ht[0:HHALF, :, :, :].rearrange("p i h b -> p (i h b)").rearrange("p (c s d m) -> p c s d m", c=BATCH // 2, s=2, d=2)
        phase_t = sb("phase_t", [P, TAB_H, NTAB], c=one)
        whole = sb("whole", [P, TAB_H, NTAB], c=one)
        decay_t = sb("decay_t", [P, 2, TAB_H, NTAB], c=one)
        sin_t = sb("sin_t", [P, 2, TAB_H, NTAB], c=one)
        cos_t = sb("cos_t", [P, 2, TAB_H, NTAB], c=one)
        pf_i = sb("pf_i", [P, 2, TAB_H, NA], c=one)
        pg = sb("pg", [P, 4, TAB_H, NA], c=one)
        ur = sb("ur", [P, SEQ], c=one)
        re = sb("re", [P, SEQ], c=one)
        fr = sb("fr", [P, SEQ], c=one)
        fi = sb("fi", [P, SEQ], c=one)
        junk = sb("junk", [P, 1024], F16, c=one)
        r_in = sb("r_in", [EXPERTS, HID], c=one)
        eb = sb("eb", [2 * EXPERTS, HID], c=one)
        par = ExitStack()
        x_b = sb("x_b", [HHALF, BATCH // 2, 2, 2, 2 * MODES], c=par)
        par_in = sb("par_in", [HHALF, 2, 2, 2, MODES], c=par)
        b_in = sb("b_in", [HHALF, 2, 2, 2 * MODES], c=par)
        el = sb("el", [P, 2, SEQ], c=par)
        ev = sb("ev", [P, 4, 2, SEQ], c=par)
        pw = sb("pw", [P, 15, SEQ], c=par)
        ab_rows = sb("ab_rows", [P, 2, SEQ], c=par)
        bw = [ev[:, i, k, :] for i in (0, 1, 3) for k in range(2)] + [ab_rows[:, k, :] for k in range(2)]
        par.close()
        QA = sb("QA", [P, 2, CH, NJ, NK_], c=one)
        QB = sb("QB", [P, 2, CH, NJ, NK_], c=one)
        CP = sb("CP", [P, 2, CH, NA, BATCH], c=one)
        CB = sb("CB", [P, 2, CH, NA, BATCH], c=one)
        one.close()

        results, weights = bank[0:2], bank[2:5]
        cos_j = bank[5][:, :].rearrange("p (i h j) -> p i h j", i=2, h=TAB_H)
        pf_r = bank[6][:, 0:2 * TAB_H * NA].rearrange("p (i h a) -> p i h a", i=2, h=TAB_H)
        CA = bank[7][:, :].rearrange("p (h a c) -> p h a c", h=CH, a=NA)

        H = sb("H", [P, TT, HID])
        Hr = sb("Hr", [P, TT, HID])
        xn = sb("xn", [P, TT, HID])
        xT = sb("xT", [P, 2, KT, PT], F16)
        stat = sb("stat", [P, 2, TT, 8])
        mv = sb("mv", [P, 2, TT, 2])
        rstd = sb("rstd", [P, 2, 2, TT])
        qT = sb("qT", [P, 2, 2, QPG * SEQ], F16)
        kT = sb("kT", [P, 2, 2, SEQ], F16)
        V = sb("V", [P, 2, TT, NKV * D], F16)
        P0 = sb("P0", [P, 2, QPG, S0])
        P1 = sb("P1", [P, 2, 2, SEQ])
        P2 = sb("P2", [P, 2, 2, S1])
        mx = sb("mx", [P, 2, 6])
        nmx = sb("nmx", [P, 2, 6])
        sums = sb("sums", [P, 2, 6])
        rec = sb("rec", [P, 2, 6])
        PT0 = sb("PT0", [P, 2, 2, QPG, SEQ], F16)
        PT1 = sb("PT1", [P, 2, QPG, S1], F16)
        oT = sb("oT", [P, 2, QPG, PT], F16)
        h2 = sb("h2", [P, TT, HID])
        z = sb("z", [P, TT, HID])
        zT = sb("zT", [P, 2, TT, KT, P], F16)
        lg = sb("lg", [P, 4, TT, EXPERTS])
        small = sb("small", [P, 4, TT])
        top = sb("top", [P, TT, 8])
        w_hi = sb("w_hi", [P, TT, EXPERTS], F16)
        w_parts = sb("w_parts", [P, TT, 2, EXPERTS])
        wT = sb("wT", [2 * EXPERTS, TT, P], F16)

        const_in, par_loaded, x_loaded = sem("const_in"), sem("par_loaded"), [sem("x_a_loaded"), sem("x_b_loaded")]
        wq_loaded, wp_loaded, r_loaded = sem("wq_loaded"), sem("wp_loaded"), sem("r_loaded")
        a_full, a_free = sem("a_full"), sem("a_free")
        b_full, b_hi, b_free = sem("b_full"), sem("b_hi"), sem("b_free")
        dve1, pool1, act1 = sem("dve1"), sem("pool1"), sem("act1")
        trig_in, trig = sem("trig_in"), sem("trig")
        squares, norms, roots, norm_max, scales = (sem(s) for s in ("squares", "norms", "roots", "norm_max", "scales"))
        bias_hi = sem("bias_hi")
        exps_made, norm_in, a_inverse, b_over_a, exp_less_one = (
            sem(s) for s in ("exps_made", "norm_in", "a_inverse", "b_over_a", "exp_less_one"))
        b_made = sem("b_made")
        decay_arg, decay, phase = sem("decay_arg"), sem("decay"), sem("phase")
        sines, cosines, sin_made, cos_made = (sem(s) for s in ("sines", "cosines", "sin_made", "cos_made"))
        cb_made, qb_made, cp_made = sem("cb_made"), sem("qb_made"), sem("cp_made")
        ht_stored = [sem("ht_even_stored"), sem("ht_odd_stored")]

        ntask = count(lambda s: len(TASKS[s]))
        nscalar = count(lambda s: len(SCALAR_INDEX[s]))
        units = dict(first=8, mid=8, last=8)
        full = Signal(sem("full"), **ntask)
        free = Signal(sem("free"), **ntask)
        part_hi = Signal(sem("part_hi"), **nscalar)
        neg_max = Signal(sem("neg_max"), **units)
        exps = Signal(sem("exps"), **units)
        recips = Signal(sem("recips"), **units)
        probs = Signal(sem("probs"), **units)
        nx = dict(lead=1, first=1, mid=1)
        pv = dict(mid=1, last=1, tail=1)
        three = lambda d: {k: TT * v for k, v in d.items()}
        x_var, x_rstd = Signal(sem("x_var"), **nx), Signal(sem("x_rstd"), **nx)
        xn_ready = Signal(sem("xn_ready"), **three(nx))
        h_in = Signal(sem("h_in"), lead=16, first=16, mid=16)
        hr_in = Signal(sem("hr_in"), first=16, mid=16, last=16)
        acc_full = Signal(sem("acc_full"), **three(pv))
        acc_free = Signal(sem("acc_free"), **three(pv))
        pt = dict(mid=1, last=1, tail=TT)
        f_var, f_rstd = Signal(sem("f_var"), **pt), Signal(sem("f_rstd"), **pt)
        z_ready = Signal(sem("z_ready"), **three(pv))
        lg_in, lg_exp = Signal(sem("lg_in"), **pv), Signal(sem("lg_exp"), **pv)
        w_ready, out_ready = Signal(sem("w_ready"), **pv), Signal(sem("out_ready"), mid=1, last=1)
        out_stored = Signal(sem("out_stored"), mid=16, last=16, tail=16 * TT)
        x_steps, f_steps = 2, 14
        vec = Signal(sem("vec"), lead=x_steps, first=x_steps, mid=x_steps + f_steps, last=f_steps, tail=f_steps - 2 + 2 * TT)

        pe_passed, dve_passed = sem("pe_passed"), sem("dve_passed")

        block = ctx.enter_context(nc.Block())

        LEAD, FIRST, LAST, TAIL = Where("lead", 0), Where("first", 0), Where("last", PAIRS - 1), Where("tail", PAIRS)

        def banks_of(w, g, b2, r2):
            return 1 + (b2 == 1 and r2 == 1 and padded(g, w.prev, w.next))

        def bodies(eng, lead, body, tail):
            lead(LEAD)
            body(FIRST)
            with eng.Fori(1, PAIRS - 1) as p:
                body(Where("mid", p))
            body(LAST)
            tail(TAIL)

        NG = NCH // CPG
        GT = 2 + BATCH
        W_TASKS = [("q", j) for j in range(NKV * GROUP)] + [("p", j, e) for j in range(KT) for e in range(0, NH, 4)]
        SQ_FIRST, SQ_EACH, ROOTS = 5, 3, 6
        NORMS, NORM_MAX = ROOTS + 1, ROOTS + 2
        W_FROM, W_REST = ROOTS + 3, 7
        SQ_COLS = 1024
        SQ_Q, SQ_P = NKV * GROUP * HID // SQ_COLS, KT * NH * D // SQ_COLS
        SQUARES = SQ_Q + SQ_P + 2
        ARGS, PHASES, MODULI, SINES, SQUARED, POWERS = -2, -2, -2, -1, 0, 3

        def table_at(c, part):
            g, rest = divmod(c - part, CPG)
            return g + 1 if rest == 0 and 0 < g + 1 < NG else None

        def w_tasks(c):
            if c == NCH:
                return range(len(W_TASKS) - W_REST, len(W_TASKS))
            start, end = ((len(W_TASKS) - W_REST) * max(i - W_FROM, 0) // (NCH - W_FROM) for i in (c, c + 1))
            return range(start, end)

        def head_pieces(part, j):
            if j < QPG:
                first = qT[:, part, :, j * S0:(j + 1) * S0]
                rest = qT[:, part, :, QPG * S0 + j * S1:QPG * S0 + (j + 1) * S1]
            else:
                first, rest = kT[:, part, :, 0:S0], kT[:, part, :, S0:SEQ]
            return [(first, lambda b: b[:, 0:2 * S0].rearrange("p (b s) -> p b s", b=2)),
                    (rest, lambda b: b[:, 2 * S0:PT].rearrange("p (b s) -> p b s", b=2))]

        def token_pieces(part, j):
            def piece(at, start, n):
                return (xT[:, part, :, at:at + n], lambda b: b[:, :].rearrange("p (k s) -> p k s", k=KT)[:, :, start:start + n])
            if j == 0:
                return [piece(0, 0, P)]
            if j == 1:
                return [piece(2 * S0, 0, S1), piece(S0, S1, P - S1)]
            return [piece(S0 + P - S1, 0, S1), piece(2 * S0 + S1, S1, S1)]

        def probs_out(part, i):
            if i < 2:
                return PT0[:, part, i, :, 0:S0]
            if i == 2:
                return PT0[:, part].rearrange("p b h s -> p (b h) s")[:, :, S0:SEQ]
            return PT1[:, part, :, :]

        def probs_in(b, i):
            if i < 2:
                return b[:, :].rearrange("p (h s) -> p h s", h=QPG)
            if i == 2:
                return b[:, :].rearrange("p (h s) -> p h s", h=2 * QPG)
            return b[:, 0:2 * P].rearrange("p (h s) -> p h s", h=QPG)

        def in_table(c):
            return c // CPG % 2, slice(CH * (c % CPG), CH * (c % CPG + 1))

        def j_of(t):
            return t.unsqueeze(3).broadcast_to([P, CH, NJ, NK_])

        def k_of(t):
            return t.unsqueeze(2).broadcast_to([P, CH, NJ, NK_])

        def g_of(r, c):
            return G[:, r, :, CH * c:CH * (c + 1)].rearrange("p c h -> p h c").unsqueeze(2).broadcast_to([P, CH, NA, BATCH])

        def a_of(t):
            return t.unsqueeze(3).broadcast_to([P, CH, NA, BATCH])

        def by_channel(v, g, n):
            return v[:, TAB_H * g:TAB_H * (g + 1)].unsqueeze(2).broadcast_to([P, TAB_H, n])

        def by_column(c0):
            return cst[:, c0:c0 + NTAB].unsqueeze(1).broadcast_to([P, TAB_H, NTAB])

        @block.sync
        def _(sp):
            sp.dma_start(cst[:, :], const).then_inc(const_in, 16)
            for d in range(2):
                for i, src in enumerate((a_imag, inv_a_real)):
                    sp.dma_start(par_in[:, :, i, d, :], src.rearrange("(s p) n -> p s n", p=HHALF)).then_inc(par_loaded, 16)
                sp.dma_start(b_in[:, :, d, :], b_ri.rearrange("(s p) n r -> p s (n r)", p=HHALF)).then_inc(par_loaded, 16)
            sp.dma_start(el[:, 0, :], log_dt.rearrange("(o h) -> o h", o=1).broadcast_to([P, SEQ])).then_inc(par_loaded, 16)
            x_rows = x.rearrange("c (s p) n r -> p c s (n r)", p=HHALF)
            for half, dst in enumerate((x_a, x_b)):
                for d in range(2):
                    sp.dma_start(dst[:, :, :, d, :], x_rows[:, half * (BATCH // 2):(half + 1) * (BATCH // 2)]).then_inc(x_loaded[half], 16)
            sp.dma_start(wq[:, :, :, :, :].rearrange("p j a k d -> p j (a k d)").bitcast(F32),
                         w_qkv.rearrange("(j p) l -> p j l", p=P)).then_inc(wq_loaded, 16)
            sp.dma_start(wp[:, :, :, :, :].rearrange("p j h a d -> p j (h a d)").bitcast(F32),
                         w_proj.rearrange("(j p) e -> p j e", p=P)).then_inc(wp_loaded, 16)
            sp.dma_start(r_in[:, :], r_weight).then_inc(r_loaded, 16)
            for half in range(2):
                sp.dma_start(eb[half * EXPERTS:(half + 1) * EXPERTS, :], e_bias).then_inc(r_loaded, 16)
            sp.dma_start(rb[:, :], r_bias.rearrange("(o h) -> o h", o=1).broadcast_to([P, EXPERTS])).then_inc(r_loaded, 16)
            h_blocks = h_dram.rearrange("(c h) (a b) -> a c h b", c=BATCH, a=NA)
            for g in range(SEQ // STORE_H):
                sp.wait_ge(a_free, GT + STORE_H // BANK_H * (g + 1))
                for a in range(NA):
                    sp.dma_start(h_blocks[a][:, STORE_H * g:STORE_H * (g + 1), :],
                                 ht[a * BATCH:(a + 1) * BATCH, g % 2, :, :]).then_inc(ht_stored[g % 2], 16)

            def load_h(w, q):
                sp.dma_start(H[:, :, :], h_dram[bass.ds(q * PT, PT), :].rearrange("(t p) l -> p t l", p=P)).then_inc(h_in.sem, 16)

            def lead(w):
                for i in range(2):
                    sp.wait_ge(ht_stored[i], 16 * NA * (SEQ // STORE_H // 2))
                load_h(w, 0)

            def body(w):
                if w.next:
                    await_(sp, xn_ready, w, 0)
                    load_h(w, w.p + 1)
                if w.prev:
                    await_(sp, acc_free, w, TT)
                sp.dma_start(Hr[:, :, :], h_dram[bass.ds(w.p * PT, PT), :].rearrange("(t p) l -> p t l", p=P)).then_inc(hr_in.sem, 16)
                if w.prev:
                    store_out(w, w.p - 1)

            def store_out(w, q):
                await_(sp, out_ready, w, 1)
                sp.dma_start(out_rows[bass.ds(q * PT, PT), :].rearrange("(t p) l -> p t l", p=P),
                             z[:, :, :]).then_inc(out_stored.sem, 16)

            def tail(w):
                for j in range(TT):
                    await_(sp, free, w, INDEX["tail"][("EB", j)] + 1)
                    row = (PAIRS - 1) * PT + j * P
                    sp.dma_start(out_rows[row:row + P, :], z[:, j, :]).then_inc(out_stored.sem, 16)
                await_(sp, out_stored, w, 16 * TT)

            bodies(sp, lead, body, tail)

        @block.tensor
        def _(pe):
            pe.wait_ge(const_in, 16)
            na, nb = [0], [0]

            def bank_a():
                if na[0] >= len(results):
                    pe.wait_ge(a_free, na[0] - len(results) + 1)
                na[0] += 1
                return results[(na[0] - 1) % len(results)]

            def bank_b():
                if nb[0] >= len(weights):
                    pe.wait_ge(b_free, nb[0] - len(weights) + 1)
                nb[0] += 1
                return weights[(nb[0] - 1) % len(weights)]

            def turn_weights_tile(t):
                task = W_TASKS[t]
                if t == 0:
                    pe.wait_ge(wq_loaded, 16)
                if task[0] == "p" and W_TASKS[t - 1][0] == "q":
                    pe.wait_ge(wp_loaded, 16)
                b = bank_b()
                if task[0] == "q":
                    src = wq[:, task[1]].rearrange("p a k d -> p (a k d)").bitcast(F32)
                else:
                    src = wp[:, task[1], task[2]:task[2] + 4].rearrange("p h a d -> p (h a d)").bitcast(F32)
                for k in range(4):
                    mm = pe.transpose(b[:, k * P:(k + 1) * P], src[:, k * P:(k + 1) * P], ident)
                mm.then_inc(b_full, 1)

            pe.wait_ge(par_loaded, 16 * 7)
            for i in range(2):
                b = bank_a()
                for k in range(2):
                    for s in range(2):
                        if i == 0:
                            src = par_in[:, s, k, :, :].rearrange("p d n -> p (d n)")
                        else:
                            src = b_in[:, s, :, :].rearrange("p d n -> p (d n)")[:, k::2]
                        mm = pe.transpose(b[:, (2 * k + s) * HHALF:(2 * k + s + 1) * HHALF], src, ident[0:HHALF, 0:HHALF])
                mm.then_inc(a_full, 1)
            for c in range(0, BATCH, 2):
                xs, c0 = (x_a, 0) if c < BATCH // 2 else (x_b, BATCH // 2)
                if c == c0:
                    pe.wait_ge(x_loaded[bool(c0)], 32)
                for r in range(2):
                    b = bank_a()
                    for k in range(2):
                        for s in range(2):
                            src = xs[:, c - c0 + k, s, :, :].rearrange("p d m -> p (d m)")[:, r::2]
                            mm = pe.transpose(b[:, (2 * k + s) * HHALF:(2 * k + s + 1) * HHALF], src, ident[0:HHALF, 0:HHALF])
                    mm.then_inc(a_full, 1)
            for c in range(NCH):
                pe.wait_ge(qb_made, c + 1)
                pe.wait_ge(cp_made, c + 1)
                for half, h0 in enumerate(range(0, CH, BANK_H)):
                    b = bank_a()
                    for h in range(h0, h0 + BANK_H):
                        for i, q in enumerate((QA, QB)):
                            mm = pe.matmul(b[0:NA * BATCH, P * (h - h0):P * (h - h0 + 1)], CP[:, c % 2, h].rearrange("p a c -> p (a c)"),
                                           q[:, c % 2, h].rearrange("p j k -> p (j k)"), start=(i == 0), stop=(i == 1))
                    mm.then_inc(a_full, 1)
                    for t in w_tasks(c)[:1] if half == 0 else w_tasks(c)[1:]:
                        turn_weights_tile(t)
            for t in w_tasks(NCH):
                turn_weights_tile(t)
            pe.wait_ge(r_loaded, 64)
            b = bank_b()
            for k in range(KT):
                mm = pe.transpose(b[:, k * EXPERTS:(k + 1) * EXPERTS], r_in[:, k * P:(k + 1) * P], ident[0:EXPERTS, 0:EXPERTS])
            mm.then_inc(b_full, 1)
            pe.wait_ge(a_free, GT + NCH * (CH // BANK_H))
            pe.wait_ge(b_free, len(W_TASKS) + 1)

            def take(w, task):
                i = INDEX[w.seg][task]
                await_(pe, free, w, i + 1 - RING)
                return ring_bank[(ring_start(w) + i) % RING]

            def ready(w, task):
                await_(pe, free, w, INDEX[w.seg][task] + 1)

            def split_product(b, pairs_, rhs_of, lhs_of, last=True):
                n = len(pairs_)
                for i, t in enumerate(pairs_):
                    for c, (l, r) in enumerate(((0, 0), (0, 1), (1, 0))):
                        mm = pe.matmul(b, lhs_of(t, l), rhs_of(t, r), start=(i == 0 and c == 0),
                                       stop=(last and i == n - 1 and c == 2))
                return mm

            def xx(w):
                for j in range(TT):
                    await_(pe, xn_ready, w, j + 1)
                    b = take(w, ("XX", j))
                    for k in range(KT):
                        mm = pe.transpose(b[:, k * P:(k + 1) * P], xn[:, j, k * P:(k + 1) * P], ident)
                    mm.then_inc(full.sem, 1)

            def project(w, u, x_task):
                if x_task is not None:
                    ready(*x_task)
                for j in range(QPG + 1):
                    b = take(w, ("A", u, j))
                    row = GROUP * (u % NKV) + j
                    split_product(b[:, 0:PT], range(KT), lambda t, r: xT[:, r, t, :],
                                  lambda t, l: wq[:, row, l, t, :]).then_inc(full.sem, 1)

            def values(w):
                for t in range(TT):
                    b = take(w, ("V", t))
                    split_product(b[:, :], range(KT), lambda k, r: wq[:, QPG + 1::GROUP, r, k, :],
                                  lambda k, l: xT[:, l, k, t * P:(t + 1) * P]).then_inc(full.sem, 1)

            def turn_probs(w, g):
                for b2 in range(2):
                    await_(pe, probs, w, 2 * g + b2 + 1)
                    b = take(w, ("T", g, b2))
                    for h in range(QPG):
                        mm = pe.transpose(b[:, h * P:(h + 1) * P], P0[:, b2, h, :], ident)
                    mm.then_inc(full.sem, 1)
                b = take(w, ("T", g, 2))
                for b2 in range(2):
                    for r2 in range(2):
                        mm = pe.transpose(b[:, (2 * b2 + r2) * P:(2 * b2 + r2 + 1) * P], P1[:, r2, b2, 0:S0], ident)
                mm.then_inc(full.sem, 1)
                b = take(w, ("T", g, 3))
                for r2 in range(2):
                    mm = pe.transpose(b[:, r2 * P:(r2 + 1) * P], P2[:, r2, :, :].rearrange("p b s -> p (b s)"), ident)
                mm.then_inc(full.sem, 1)

            def attend(w, g):
                ready(w, ("T", g, 3))
                if g == 0:
                    ready(w, ("V", TT - 1))
                for b2 in range(2):
                    for r2 in range(2):
                        b = take(w, ("D", g, b2, r2))
                        split_product(b[:, 0:PT], range(1), lambda t, r: PT0[:, r, b2, 2 * r2:2 * r2 + 2, :],
                                      lambda t, l: V[:, l, b2, g * D:(g + 1) * D], last=False)
                        tail_rows = b[:, 0:PT].rearrange("p (h s) -> p h s", h=2)[:, :, S0:SEQ]
                        half = slice(b2 * S1, (b2 + 1) * S1)
                        for c, (l, r) in enumerate(((0, 0), (0, 1), (1, 0))):
                            mm = pe.matmul(tail_rows, V[half, l, 2, g * D:(g + 1) * D], PT1[half, r, 2 * r2:2 * r2 + 2, :],
                                           start=False, stop=(c == 2))
                        mm.then_inc(full.sem, banks_of(w, g, b2, r2))

            def turn_z(w, tiles=range(TT)):
                for j in tiles:
                    await_(pe, z_ready, w, j + 1)
                    b = take(w, ("Z", j))
                    for k in range(KT):
                        mm = pe.transpose(b[:, k * P:(k + 1) * P], z[:, j, k * P:(k + 1) * P], ident)
                    mm.then_inc(full.sem, 1)

            def logits(w, tiles=range(TT)):
                if w.seg != "tail":
                    ready(w, ("Z", TT - 1))
                b = take(w, ("LG",))
                for j in tiles:
                    if w.seg == "tail":
                        ready(w, ("Z", j))
                    at = 2 * EXPERTS * j
                    for k in range(KT):
                        pe.matmul(b[:, at:at + 2 * EXPERTS], zT[:, 0, j, k, :], rwT[:, k, :, :].rearrange("p i e -> p (i e)"),
                                  start=(k == 0), stop=False)
                    for k in range(KT):
                        mm = pe.matmul(b[:, at:at + EXPERTS], zT[:, 1, j, k, :], rwT[:, k, 0, :], start=False, stop=(k == KT - 1))
                if TT - 1 in tiles:
                    mm.then_inc(full.sem, 1)

            def turn_weights(w):
                b = take(w, ("WT",))
                await_apart(pe, w_ready, w, 1, pe_passed)
                for j in range(TT):
                    mm = pe.transpose(b[:, j * P:(j + 1) * P], w_parts[:, j, :, :].rearrange("p i e -> p (i e)"), ident)
                mm.then_inc(full.sem, 1)

            def experts(w):
                ready(w, ("WT",))
                for j in range(TT):
                    b = take(w, ("EB", j))
                    pe.matmul(b[:, :], wT[:, j, :], eb_hi[:, :], start=True, stop=False)
                    pe.matmul(b[:, :], wT[0:EXPERTS, j, :], eb_lo[:, :], start=False, stop=True).then_inc(full.sem, 1)

            def lead(w):
                xx(w)
                project(w, 0, (w, ("XX", TT - 1)))

            def body(w):
                for g in range(NKV):
                    if g == 0:
                        if w.seg == "first":
                            await_(pe, free, LEAD, INDEX["lead"][("A", 0, QPG)] + 1)
                        else:
                            await_(pe, free, w, INDEX["mid"][("A", NKV, QPG)] + 1 - len(TASKS["mid"]))
                    else:
                        ready(w, ("A", g, QPG))
                    scores_only(w, g)
                    if g < NKV - 1 or w.next:
                        project(w, g + 1, (w, ("XX", TT - 1)) if g == NKV - 1 else None)
                    if g == 0:
                        values(w)
                    if g == 0 and w.prev:
                        await_(pe, free, w, INDEX["mid"][("D", NKV - 1, 1, 1)] + 1 - len(TASKS["mid"]))
                    if g > 0 or w.prev:
                        output_group(w, (g - 1) % NKV, (0, 1) if g > 0 else (0,))
                    turn_probs(w, g)
                    if g > 0 or w.prev:
                        output_group(w, (g - 1) % NKV, (2,) if g > 0 else (1, 2))
                    if g == 2 and w.prev:
                        turn_z(w)
                    if g == 3 and w.prev:
                        turn_weights(w)
                    attend(w, g)
                    if g == 2 and w.prev:
                        logits(w)
                    if g == 2 and w.next:
                        xx(w)
                    if g == 3 and w.prev:
                        experts(w)

            def scores_only(w, g):
                for b2 in range(2):
                    b = take(w, ("S", g, b2, 0))
                    for h in range(QPG):
                        mm = split_product(b[:, h * S0:(h + 1) * S0], range(1),
                                           lambda t, r: kT[:, r, b2, 0:S0],
                                           lambda t, l: qT[:, l, b2, h * S0:(h + 1) * S0])
                    mm.then_inc(full.sem, 1)
                    b = take(w, ("S", g, b2, 1))
                    for r2 in range(2):
                        mm = split_product(b[:, r2 * SEQ:(r2 + 1) * SEQ], range(1),
                                           lambda t, r: kT[:, r, b2, :],
                                           lambda t, l: qT[:, l, b2, QPG * S0 + r2 * P:QPG * S0 + (r2 + 1) * P])
                    mm.then_inc(full.sem, 1)

            def output_group(w, g, tiles):
                if g < NKV - 1:
                    ready(w, ("D", g, 1, 1))
                for j in tiles:
                    if g == 0 and w.prev:
                        await_(pe, acc_free, w, j + 1)
                    for h in range(QPG):
                        for c, (l, r) in enumerate(((0, 0), (0, 1), (1, 0))):
                            mm = pe.matmul(acc[j][:, :], oT[:, l, h, j * P:(j + 1) * P], wp[:, :, g * QPG + h, r, :],
                                           start=(g == 0 and h == 0 and c == 0), stop=(g == NKV - 1 and h == QPG - 1 and c == 2))
                    if g == NKV - 1:
                        mm.then_inc(acc_full.sem, 1)

            def tail(w):
                await_(pe, free, LAST, INDEX["last"][("D", NKV - 1, 1, 1)] + 1)
                output_group(w, NKV - 1, range(TT))
                turn_z(w, (0, 1))
                logits(w, (0, 1))
                turn_z(w, (2,))
                logits(w, (2,))
                turn_weights(w)
                experts(w)

            bodies(pe, lead, body, tail)

        @block.scalar
        def _(act):
            na = [0]

            def bank_a():
                na[0] += 1
                act.wait_ge(a_full, na[0])
                return results[(na[0] - 1) % len(results)]

            def cp(out_, in_):
                return act.activation(out_, in_, ACT.Copy)

            b = bank_a()
            cp(pw[:, 0, :], b[:, 0:SEQ])
            cp(el[:, 1, :], b[:, SEQ:2 * SEQ]).then_inc(a_free, 1)
            b = bank_a()
            cp(pw[:, 1:3, :], b[:, 0:2 * SEQ].rearrange("p (k h) -> p k h", k=2)).then_inc(a_free, 1)

            def moduli(g):
                act.wait_ge(decay_arg, g + 1)
                act.activation(decay_t[:, g % 2], decay_t[:, g % 2], ACT.Exp).then_inc(decay, 1)

            def sine_values(g):
                i = g % 2
                if g >= 2:
                    act.wait_ge(qb_made, CPG * (g - 1))
                    act.wait_ge(cp_made, CPG * (g - 1))
                act.wait_ge(phase, g + 1)
                act.activation(cos_t[:, i], phase_t[:, :, :], ACT.Sin, scale=TWO_PI / 2).then_inc(act1, 1)
                act.activation(sin_t[:, i, :, 0:NKA], phase_t[:, :, 0:NKA], ACT.Sin, scale=TWO_PI)
                act.activation(sin_t[:, i, :, NKA:], phase_t[:, :, NKA:], ACT.Sin, scale=-TWO_PI).then_inc(sines, 1)

            def cosine_values(g):
                i = g % 2
                act.wait_ge(act1, 2 * g + 1)
                act.activation(cos_t[:, i], cos_t[:, i], ACT.Square).then_inc(act1, 1)
                act.wait_ge(act1, 2 * g + 2)
                act.activation(cos_t[:, i], cos_t[:, i], ACT.Identity, scale=-2.0, bias=cst[:, C_ONE:C_ONE + 1]).then_inc(cosines, 1)

            for c in range(0, BATCH, 2):
                for r in range(2):
                    b = bank_a()
                    cp(G[:, r, c:c + 2, :], b[:, 0:2 * SEQ].rearrange("p (c h) -> p c h", c=2)).then_inc(a_free, 1)

            act.wait_ge(const_in, 16)
            act.activation(sq[EXPERTS:, SQUARES - 1:SQUARES], cst[EXPERTS:, C_ONE:C_ONE + 1], ACT.Copy, scale=0.0)

            act.wait_ge(trig_in, 1)
            act.activation(pw[:, 6, :], re[:, :], ACT.Tanh, scale=0.5).then_inc(trig, 1)
            act.activation(pw[:, 7, :], pw[:, 5, :], ACT.Sin, scale=TWO_PI).then_inc(trig, 1)
            act.activation(pw[:, 8, :], pw[:, 5, :], ACT.Sin, scale=TWO_PI / 2).then_inc(trig, 1)
            moduli(0)
            sine_values(0)
            cosine_values(0)

            wq_flat = wq[:, :, :, :, :].rearrange("p j a k d -> p (j a k d)").bitcast(F32)
            wp_flat = wp[:, :, :, :, :].rearrange("p j h a d -> p (j h a d)").bitcast(F32)
            n_sq = [0]

            def square(n):
                for i in range(n_sq[0], min(SQUARES, n_sq[0] + n)):
                    if i == 0:
                        act.wait_ge(wq_loaded, 16)
                    if i == SQ_Q:
                        act.wait_ge(wp_loaded, 16)
                    if i >= SQ_Q + SQ_P:
                        act.wait_ge(r_loaded, 64)
                        src = eb[:, :] if i == SQ_Q + SQ_P else r_in[:, :]
                    else:
                        flat, at = (wq_flat, i * SQ_COLS) if i < SQ_Q else (wp_flat, (i - SQ_Q) * SQ_COLS)
                        src = flat[:, at:at + SQ_COLS]
                    if i:
                        act.wait_ge(squares, i)
                    n_p, n_c = src.shape[0], src.shape[-1]
                    act.activation(junk[0:n_p, 0:n_c], src, ACT.Square, scale=2.0 ** -7, accum_out=sq[0:n_p, i:i + 1]).then_inc(squares, 1)
                n_sq[0] += n

            def table_parts(c):
                for part, make in ((MODULI, moduli), (SINES, sine_values), (SQUARED, cosine_values)):
                    if table_at(c, part):
                        make(table_at(c, part))

            square(SQ_FIRST)
            for c in range(-CPG, 0):
                table_parts(c)

            def high_weights(t):
                if t == 0:
                    act.wait_ge(scales, 1)
                    act.activation(eb_hi[:, :], eb[:, :], ACT.Copy, scale=s_e).then_inc(bias_hi, 1)
                act.wait_ge(b_full, t + 1)
                src = weights[t % len(weights)][:, :].rearrange("p (k d) -> p k d", k=4)
                if W_TASKS[t][0] == "q":
                    hi = wq[:, W_TASKS[t][1], 0, :, :]
                else:
                    hi = wp[:, W_TASKS[t][1], W_TASKS[t][2]:W_TASKS[t][2] + 4, 0, :]
                act.activation(hi, src, ACT.Copy, scale=s_q if W_TASKS[t][0] == "q" else s_p).then_inc(b_hi, 1)

            for c in range(NCH):
                table_parts(c)
                if c < ROOTS:
                    square(SQ_EACH)
                if c == ROOTS:
                    act.wait_ge(norms, 1)
                    act.activation(w_norm, w_sq, ACT.Sqrt, scale=2.0 ** 14).then_inc(roots, 1)
                store, h0 = divmod(CH * c, STORE_H)
                if h0 == 0 and store >= 2:
                    act.wait_ge(ht_stored[store % 2], 16 * NA * (store // 2))
                for h in range(h0, h0 + CH, BANK_H):
                    b = bank_a()
                    cp(ht[0:NA * BATCH, store % 2, h:h + BANK_H, :],
                       b[0:NA * BATCH, :].rearrange("p (h b) -> p h b", h=BANK_H)).then_inc(a_free, 1)
                    for t in w_tasks(c)[:1] if h == h0 else w_tasks(c)[1:]:
                        high_weights(t)
            for t in w_tasks(NCH):
                high_weights(t)
            t = len(W_TASKS)
            act.wait_ge(b_full, t + 1)
            act.activation(rwT[:, :, 0, :], weights[t % len(weights)][:, 0:KT * EXPERTS].rearrange("p (k e) -> p k e", k=KT),
                           ACT.Copy, scale=s_r).then_inc(b_hi, 1)

            act.preload_act_table(ACT.Exp)

            def copy_part(w, task, pieces, scale=1.0):
                i = INDEX[w.seg][task]
                await_(act, full, w, i + 1)
                b = ring_bank[(ring_start(w) + i) % RING]
                for out_, in_of in pieces:
                    ins = act.activation(out_, in_of(b), ACT.Copy, scale=scale)
                ins.then_inc(part_hi.sem, 1)

            def project(w, u):
                for j in range(QPG + 1):
                    copy_part(w, ("A", u, j), head_pieces(0, j), QKV_EVAC)

            def xx(w):
                for j in range(TT):
                    copy_part(w, ("XX", j), token_pieces(0, j), X_SCALE)

            def lead(w):
                xx(w)
                project(w, 0)

            def z_turned(w):
                for j in range(TT):
                    copy_part(w, ("Z", j), [(zT[:, 0, j], lambda b: b[:, :].rearrange("p (k s) -> p k s", k=KT))], X_SCALE)

            def router_exp(w):
                await_(act, lg_in, w, 1)
                act.activation(lg[:, 1], lg[:, 0], ACT.Exp).then_inc(lg_exp.sem, 1)

            def body(w):
                for g in range(NKV):
                    for b2 in range(2):
                        await_(act, neg_max, w, 2 * g + b2 + 1)
                        for i in range(6):
                            t = P0[:, b2, i, :] if i < QPG else P1[:, i - QPG, b2, :]
                            e = act.activation(t, t, ACT.Exp, bias=nmx[:, b2, i:i + 1], scale=alpha,
                                               accum_out=sums[:, b2, i:i + 1])
                        e.then_inc(exps.sem, 1)
                    if g < NKV - 1 or w.next:
                        project(w, g + 1)
                    if g == 0:
                        for t in range(TT):
                            copy_part(w, ("V", t), [(V[:, 0, t, :], lambda b: b[:, :])], QKV_EVAC)
                    for i in range(4):
                        copy_part(w, ("T", g, i), [(probs_out(0, i), lambda b: probs_in(b, i))], P_SCALE)
                    if g == 2 and w.prev:
                        z_turned(w)
                    for b2 in range(2):
                        for r2 in range(2):
                            copy_part(w, ("D", g, b2, r2), [(oT[:, 0, 2 * r2:2 * r2 + 2, b2 * SEQ:(b2 + 1) * SEQ],
                                      lambda b: b[:, 0:PT].rearrange("p (h s) -> p h s", h=2))], OUT_EVAC)
                    if g == 2 and w.prev:
                        router_exp(w)
                    if g == 2 and w.next:
                        xx(w)

            def tail(w):
                z_turned(w)
                router_exp(w)

            bodies(act, lead, body, tail)

        @block.gpsimd
        def _(pool):
            npool = [0]

            def own(ins):
                npool[0] += 1
                ins.then_inc(pool1, 1)
                pool.wait_ge(pool1, npool[0])

            def decay_args(g):
                if g >= 2:
                    pool.wait_ge(sin_made, g - 1)
                    pool.wait_ge(cos_made, g - 1)
                pool.tensor_tensor(decay_t[:, g % 2], by_channel(re, g, NTAB), by_column(C_L), ALU.mult).then_inc(decay_arg, 1)

            def table(g):
                i = g % 2
                pool.wait_ge(decay, g + 1)
                pool.wait_ge(sines, g + 1)
                own(pool.tensor_tensor(sin_t[:, i], sin_t[:, i], decay_t[:, i], ALU.mult))
                pool.tensor_tensor(pg[:, 2], sin_t[:, i, :, NK_:NKA], by_channel(fr, g, NA), ALU.mult).then_inc(sin_made, 1)
                pool.wait_ge(cos_made, g + 1)
                own(pool.tensor_tensor(pg[:, 3], cos_t[:, i, :, NK_:NKA], by_channel(fi, g, NA), ALU.mult))
                pool.wait_ge(sin_made, g + 1)
                own(pool.tensor_tensor(pf_i[:, i], pg[:, 2], pg[:, 3], ALU.add))

            pool.wait_ge(const_in, 16)
            pool.wait_ge(exps_made, 1)
            pool.wait_ge(a_free, 2)
            a_im, b_re, b_im = (pw[:, i, :] for i in range(3))
            a_re = ev[:, 2, 1, :]
            pool.tensor_tensor(bw[4], a_re, a_re, ALU.mult)
            own(pool.tensor_tensor(bw[5], a_im, a_im, ALU.mult))
            pool.tensor_tensor(bw[0], bw[4], bw[5], ALU.add).then_inc(norm_in, 1)
            pool.tensor_tensor(bw[2], b_im, a_im, ALU.mult)
            own(pool.tensor_tensor(bw[3], b_re, a_re, ALU.mult))
            own(pool.tensor_tensor(bw[6], bw[2], bw[3], ALU.subtract))
            pool.tensor_tensor(bw[4], b_re, a_im, ALU.mult)
            own(pool.tensor_tensor(bw[5], b_im, a_re, ALU.mult))
            own(pool.tensor_tensor(bw[7], bw[4], bw[5], ALU.add))
            pool.wait_ge(trig_in, 1)
            decay_args(0)
            pool.wait_ge(a_inverse, 1)
            pool.tensor_tensor(bw[2], bw[6], bw[1], ALU.mult)
            own(pool.tensor_tensor(bw[3], bw[7], bw[1], ALU.mult))
            pool.sem_inc(b_over_a, 1)
            pool.wait_ge(exp_less_one, 1)
            pool.tensor_tensor(bw[4], pw[:, 14, :], bw[2], ALU.mult)
            own(pool.tensor_tensor(bw[5], pw[:, 13, :], bw[3], ALU.mult))
            pool.tensor_tensor(fi[:, :], bw[4], bw[5], ALU.subtract).then_inc(b_made, 1)
            pool.wait_ge(b_made, 2)
            table(0)

            def table_parts(c):
                for part, make in ((ARGS, decay_args), (POWERS, table)):
                    if table_at(c, part):
                        make(table_at(c, part))

            for c in range(-CPG, 0):
                table_parts(c)
            for c in range(NCH):
                g = c // CPG
                table_parts(c)
                if c == NORM_MAX:
                    pool.wait_ge(roots, 1)
                    pool.partition_all_reduce(w_max, w_norm, P, RMAX).then_inc(norm_max, 1)
                i, hs = in_table(c)
                if c == 0:
                    pool.wait_ge(a_free, GT)
                if c >= 2:
                    pool.wait_ge(cp_made, c - 1)
                    pool.wait_ge(a_full, GT + CH // BANK_H * (c - 1))
                pool.tensor_tensor(CB[:, c % 2], g_of(1, c), a_of(pf_i[:, i, hs]), ALU.mult).then_inc(cb_made, 1)
                pool.tensor_tensor(QB[:, c % 2], j_of(sin_t[:, i, hs, NKA:]), k_of(sin_t[:, i, hs, 0:NK_]), ALU.mult).then_inc(qb_made, 1)

            def normalise(w, g):
                for b2 in range(2):
                    await_(pool, recips, w, 2 * g + b2 + 1)
                    pool.tensor_tensor(P0[:, b2], P0[:, b2], rec[:, b2, 0:QPG].unsqueeze(2).broadcast_to([P, QPG, S0]), ALU.mult)
                    r1 = rec[:, b2, QPG:6].unsqueeze(2)
                    pool.tensor_tensor(P1[:, :, b2, 0:S0], P1[:, :, b2, 0:S0], r1.broadcast_to([P, 2, S0]), ALU.mult)
                    pool.tensor_tensor(P2[:, :, b2], P1[:, :, b2, S0:SEQ], r1.broadcast_to([P, 2, S1]), ALU.mult).then_inc(probs.sem, 1)

            def root(w, which, var, done):
                await_(pool, var, w, 1)
                pool.tensor_tensor(rstd[:, which, 1], rstd[:, which, 0], cst[:, C_HALF:C_HALF + TT], ALU.pow).then_inc(done.sem, 1)

            def body(w):
                for g in range(NKV):
                    normalise(w, g)
                    if g == 1 and w.prev:
                        root(w, 1, f_var, f_rstd)
                    if g == 1 and w.next:
                        root(w, 0, x_var, x_rstd)

            def tail(w):
                for j in range(TT):
                    await_(pool, f_var, w, j + 1)
                    pool.tensor_tensor(rstd[:, 1, 1, j:j + 1], rstd[:, 1, 0, j:j + 1], cst[:, C_HALF:C_HALF + 1],
                                       ALU.pow).then_inc(f_rstd.sem, 1)

            bodies(pool, lambda w: root(w, 0, x_var, x_rstd), body, tail)

        @block.vector
        def _(dve):
            nd = [0]

            def own(ins):
                nd[0] += 1
                ins.then_inc(dve1, 1)
                dve.wait_ge(dve1, nd[0])

            def tt(o, a, b, op):
                own(dve.tensor_tensor(o, a, b, op))

            def ts(o, a, s1, s2, op0, op1):
                own(dve.tensor_scalar(o, a, s1, s2, op0, op1))

            def stt(o, a, s, b, op0, op1):
                own(dve.scalar_tensor_tensor(out=o, in0=a, scalar=s, in1=b, op0=op0, op1=op1))

            def low_weights(t):
                dve.wait_ge(b_hi, t + 1)
                task = W_TASKS[t]
                src = weights[t % len(weights)][:, :].rearrange("p (k d) -> p k d", k=4)
                if task[0] == "q":
                    hi, lo = wq[:, task[1], 0, :, :], wq[:, task[1], 1, :, :]
                else:
                    hi, lo = (wp[:, task[1], task[2]:task[2] + 4, i, :] for i in range(2))
                dve.scalar_tensor_tensor(out=lo, in0=src, scalar=s_q if task[0] == "q" else s_p, in1=hi,
                                         op0=ALU.mult, op1=ALU.subtract).then_inc(b_free, 1)

            dve.wait_ge(par_loaded, 16 * 7)
            dve.wait_ge(a_free, 2)
            elf = el[:, :, :].rearrange("p i h -> p (i h)")
            e0, e1, e2, e3 = (ev[:, i].rearrange("p i h -> p (i h)") for i in range(4))
            ts(e0, elf, LOG2E, ROUND, ALU.mult, ALU.add)
            ts(e0, e0, -ROUND, None, ALU.add, ALU.bypass)
            stt(e1, e0, -LN2_HI, elf, ALU.mult, ALU.add)
            stt(e1, e0, -LN2_LO, e1, ALU.mult, ALU.add)
            ts(e2, e1, 1.0 / 5040, None, ALU.mult, ALU.bypass)
            for c in (1.0 / 720, 1.0 / 120, 1.0 / 24, 1.0 / 6, 0.5, 1.0):
                stt(e2, e2, c, e1, ALU.add, ALU.mult)
            ts(e0, e0, 127.0 + 2.0 ** 23, None, ALU.add, ALU.bypass)
            own(dve.tensor_scalar(e3.bitcast(I32), e0.bitcast(I32), 23, None, ALU.logical_shift_left, ALU.bypass))
            dve.scalar_tensor_tensor(out=e2, in0=e2, scalar=1.0, in1=e3, op0=ALU.add, op1=ALU.mult).then_inc(exps_made, 1)
            dve.wait_ge(exps_made, 1)
            dt, a = ev[:, 2, 0, :], ev[:, 2, 1, :]
            aim, br, bi = (pw[:, i, :] for i in range(3))
            r = lambda i: pw[:, i, :]
            stt(re[:, :], a, -1.0, dt, ALU.mult, ALU.mult)
            tt(r(3), aim, dt, ALU.mult)
            ts(r(3), r(3), INV_2PI, None, ALU.mult, ALU.bypass)
            ts(r(4), r(3), ROUND, -ROUND, ALU.add, ALU.add)
            tt(ur[:, :], r(3), r(4), ALU.subtract)
            ts(r(5), r(3), 0.5, None, ALU.mult, ALU.bypass)
            ts(r(4), r(5), ROUND, -ROUND, ALU.add, ALU.add)
            own(dve.tensor_tensor(r(5), r(5), r(4), ALU.subtract))
            dve.tensor_copy(r(4), r(5)).then_inc(trig_in, 1)

            def phases(g):
                if g:
                    dve.wait_ge(sines, g)
                tt(phase_t[:, :, :], by_channel(ur, g, NTAB), by_column(C_L), ALU.mult)
                tt(phase_t[:, :, :], phase_t[:, :, :], by_column(C_OFF), ALU.add)
                ts(whole[:, :, :], phase_t[:, :, :], ROUND, -ROUND, ALU.add, ALU.add)
                dve.tensor_tensor(phase_t[:, :, :], phase_t[:, :, :], whole[:, :, :], ALU.subtract).then_inc(phase, 1)

            def table(g):
                i = g % 2
                dve.wait_ge(decay, g + 1)
                dve.wait_ge(cosines, g + 1)
                own(dve.tensor_tensor(cos_t[:, i, :, 0:NKA], cos_t[:, i, :, 0:NKA], decay_t[:, i, :, 0:NKA], ALU.mult))
                dve.tensor_tensor(cos_j[:, i], cos_t[:, i, :, NKA:], decay_t[:, i, :, NKA:], ALU.mult).then_inc(cos_made, 1)
                tt(pg[:, 0], cos_t[:, i, :, NK_:NKA], by_channel(fr, g, NA), ALU.mult)
                dve.wait_ge(sin_made, g + 1)
                tt(pg[:, 1], sin_t[:, i, :, NK_:NKA], by_channel(fi, g, NA), ALU.mult)
                tt(pf_r[:, i], pg[:, 0], pg[:, 1], ALU.subtract)

            phases(0)
            dve.wait_ge(norm_in, 1)
            ts(bw[0], bw[0], 0.5, None, ALU.mult, ALU.bypass)
            dve.reciprocal(bw[1], bw[0]).then_inc(a_inverse, 1)
            dve.wait_ge(trig, 3)
            t_, sy, qy = r(6), r(7), r(8)
            ts(r(9), t_, -1.0, 1.0, ALU.mult, ALU.add)
            own(dve.reciprocal(r(10), r(9)))
            stt(r(9), t_, 2.0, r(10), ALU.mult, ALU.mult)
            tt(r(10), qy, qy, ALU.mult)
            ts(r(10), r(10), -2.0, 1.0, ALU.mult, ALU.add)
            stt(r(11), sy, 2.0, r(10), ALU.mult, ALU.mult)
            stt(r(12), sy, 2.0, sy, ALU.mult, ALU.mult)
            ts(r(13), r(12), -1.0, 1.0, ALU.mult, ALU.add)
            stt(r(14), r(9), 1.0, r(11), ALU.add, ALU.mult)
            tt(r(13), r(13), r(9), ALU.mult)
            dve.tensor_tensor(r(13), r(13), r(12), ALU.subtract).then_inc(exp_less_one, 1)
            dve.wait_ge(exp_less_one, 1)
            dve.wait_ge(b_over_a, 1)
            tt(r(10), r(13), bw[2], ALU.mult)
            tt(r(11), r(14), bw[3], ALU.mult)
            dve.tensor_tensor(fr[:, :], r(10), r(11), ALU.add).then_inc(b_made, 1)
            dve.wait_ge(b_made, 2)
            table(0)

            def table_parts(c):
                for part, make in ((PHASES, phases), (POWERS, table)):
                    if table_at(c, part):
                        make(table_at(c, part))

            for c in range(-CPG, 0):
                table_parts(c)
            for c in range(NCH):
                g = c // CPG
                i, hs = in_table(c)
                for t in w_tasks(c - 2)[1:] if c >= 2 else ():
                    low_weights(t)
                table_parts(c)
                if c == NORMS:
                    dve.wait_ge(squares, SQUARES)
                    own(dve.tensor_reduce(w_sq[:, 0:1], sq[:, 0:SQ_Q], AX_X, ALU.add))
                    own(dve.tensor_reduce(w_sq[:, 1:2], sq[:, SQ_Q:SQ_Q + SQ_P], AX_X, ALU.add))
                    own(dve.tensor_copy(w_sq[:, 2:4], sq[:, SQ_Q + SQ_P:SQUARES]))
                    dve.tensor_scalar(w_sq, w_sq, NORM_FLOOR, None, ALU.max, ALU.bypass).then_inc(norms, 1)
                if c == W_FROM:
                    dve.wait_ge(norm_max, 1)
                    own(dve.tensor_scalar(w_pow.bitcast(I32), w_max.bitcast(I32), 0x7F800000, None,
                                          ALU.bitwise_and, ALU.bypass))
                    own(dve.reciprocal(w_inv, w_pow))
                    ts(w_scale, w_inv, W_SCALE, None, ALU.mult, ALU.bypass)
                    stt(alpha, w_pow[:, 0:1], float(D) ** -0.5 / QKV_STORE ** 2, w_pow[:, 0:1], ALU.mult, ALU.mult)
                    own(dve.tensor_scalar(minus_alpha, alpha, -1.0, None, ALU.mult, ALU.bypass))
                    ts(delta, w_pow[:, 3:4], 1.0 / (X_SCALE * W_SCALE), None, ALU.mult, ALU.bypass)
                    ts(gamma, w_pow[:, 2:3], 1.0 / (P_SCALE * W_SCALE), None, ALU.mult, ALU.bypass)
                    dve.scalar_tensor_tensor(out=beta, in0=w_pow[:, 0:1], scalar=1.0 / (QKV_STORE * W_SCALE), in1=w_pow[:, 1:2],
                                             op0=ALU.mult, op1=ALU.mult).then_inc(scales, 1)
                if c == NCH - 1:
                    dve.wait_ge(bias_hi, 1)
                    own(dve.scalar_tensor_tensor(out=eb_lo[:, :], in0=eb[0:EXPERTS, :], scalar=s_e[0:EXPERTS], in1=eb_hi[0:EXPERTS, :],
                                                 op0=ALU.mult, op1=ALU.subtract))
                if c == 0:
                    dve.wait_ge(a_free, GT)
                if c >= 2:
                    dve.wait_ge(a_full, GT + CH // BANK_H * (c - 1))
                if c:
                    dve.wait_ge(cp_made, c)
                own(dve.tensor_tensor(CA, g_of(0, c), a_of(pf_r[:, i, hs]), ALU.mult))
                dve.tensor_tensor(QA[:, c % 2], j_of(cos_j[:, i, hs]), k_of(cos_t[:, i, hs, 0:NK_]), ALU.mult)
                for t in w_tasks(c - 1)[:1] if c else ():
                    low_weights(t)
                dve.wait_ge(cb_made, c + 1)
                dve.tensor_tensor(CP[:, c % 2], CA, CB[:, c % 2], ALU.subtract).then_inc(cp_made, 1)
            for t in (*w_tasks(NCH - 2)[1:], *w_tasks(NCH - 1), *w_tasks(NCH)):
                low_weights(t)
            t = len(W_TASKS)
            dve.wait_ge(b_hi, t + 1)
            dve.scalar_tensor_tensor(out=rwT[:, :, 1, :], in0=weights[t % len(weights)][:, 0:KT * EXPERTS].rearrange("p (k e) -> p k e", k=KT),
                                     scalar=s_r, in1=rwT[:, :, 0, :], op0=ALU.mult, op1=ALU.subtract).then_inc(b_free, 1)

            steps = [0]

            def step(w, ins, apart=False):
                steps[0] += 1
                ins.then_inc(vec.sem, 1)
                if apart:
                    await_apart(dve, vec, w, steps[0], dve_passed)
                else:
                    await_(dve, vec, w, steps[0])

            def of(w, task):
                i = INDEX[w.seg][task]
                return ring_bank[(ring_start(w) + i) % RING]

            def low_part(w, task, pieces, hi_pieces, scale, banks=1):
                await_(dve, part_hi, w, SCALAR_INDEX[w.seg][task] + 1)
                for (lo, in_of), (hi, _) in zip(pieces, hi_pieces):
                    ins = dve.scalar_tensor_tensor(out=lo, in0=in_of(of(w, task)), scalar=scale, in1=hi,
                                                   op0=ALU.mult, op1=ALU.subtract)
                ins.then_inc(free.sem, banks)

            def h_stats(w):
                await_apart(dve, h_in, w, 16, dve_passed)
                for j in range(TT):
                    ins = dve.bn_stats(stat[:, 0, j, 0:6], H[:, j, :])
                step(w, ins, apart=True)
                normal(w, 0, x_var, vec, steps[0])

            def normal(w, which, var, signal, k):
                await_apart(dve, signal, w, k, dve_passed)
                for j in range(TT):
                    ins = dve.bn_aggr(mv[:, which, j, :], stat[:, which, j, 0:6])
                step(w, ins)
                dve.tensor_scalar(rstd[:, which, 0], mv[:, which, :, 1], EPS, None, ALU.add, ALU.bypass).then_inc(var.sem, 1)

            def x_norm(w):
                await_(dve, x_rstd, w, 1)
                for j in range(TT):
                    dve.tensor_scalar(xn[:, j, :], H[:, j, :], mv[:, 0, j, 0:1], rstd[:, 0, 1, j:j + 1],
                                      ALU.subtract, ALU.mult).then_inc(xn_ready.sem, 1)

            def xx(w):
                for j in range(TT):
                    low_part(w, ("XX", j), token_pieces(1, j), token_pieces(0, j), X_SCALE)

            def project(w, u, j):
                low_part(w, ("A", u, j), head_pieces(1, j), head_pieces(0, j), QKV_EVAC)

            def mask_max(w, g, b2):
                for r2 in range(2):
                    await_apart(dve, full, w, INDEX[w.seg][("S", g, b2, r2)] + 1, dve_passed)
                    b = of(w, ("S", g, b2, r2))
                    for i in range(QPG if r2 == 0 else 2):
                        if r2 == 0:
                            o, s, m, c = P0[:, b2, i, :], b[:, i * S0:(i + 1) * S0], mask0, i
                        else:
                            o, s, m, c = P1[:, i, b2, :], b[:, i * SEQ:(i + 1) * SEQ], mask1, QPG + i
                        ins = dve.tensor_tensor_reduce(o, s, m, 1.0, -3e38, ALU.add, ALU.max, mx[:, b2, c:c + 1])
                    ins.then_inc(free.sem, 1)
                await_(dve, free, w, INDEX[w.seg][("S", g, b2, 1)] + 1)
                dve.tensor_scalar(nmx[:, b2, :], mx[:, b2, :], minus_alpha, None, ALU.mult, ALU.bypass).then_inc(neg_max.sem, 1)

            def reciprocals(w, g, b2):
                await_(dve, exps, w, 2 * g + b2 + 1)
                dve.reciprocal(rec[:, b2, :], sums[:, b2, :]).then_inc(recips.sem, 1)

            def residual(w):
                await_(dve, hr_in, w, 0)
                await_(dve, out_ready, w, 0)
                for j in range(TT):
                    await_(dve, acc_full, w, j + 1)
                    dve.scalar_tensor_tensor(out=h2[:, j, :], in0=acc[j][:, :], scalar=beta, in1=Hr[:, j, :],
                                             op0=ALU.mult, op1=ALU.add).then_inc(acc_free.sem, 1)
                    await_(dve, acc_free, w, j + 1)
                    ins = dve.bn_stats(stat[:, 1, j, 0:6], h2[:, j, :])
                step(w, ins, apart=True)
                normal(w, 1, f_var, vec, steps[0])

            def add_tile(w, j):
                await_(dve, acc_full, w, j + 1)
                dve.scalar_tensor_tensor(out=h2[:, j, :], in0=acc[j][:, :], scalar=beta, in1=Hr[:, j, :],
                                         op0=ALU.mult, op1=ALU.add).then_inc(acc_free.sem, 1)
                await_(dve, acc_free, w, j + 1)
                step(w, dve.bn_stats(stat[:, 1, j, 0:6], h2[:, j, :]))
                step(w, dve.bn_aggr(mv[:, 1, j, :], stat[:, 1, j, 0:6]))
                dve.tensor_scalar(rstd[:, 1, 0, j:j + 1], mv[:, 1, j, 1:2], EPS, None, ALU.add, ALU.bypass).then_inc(f_var.sem, 1)

            def norm_tile(w, j):
                await_(dve, f_rstd, w, j + 1)
                dve.tensor_scalar(z[:, j, :], h2[:, j, :], mv[:, 1, j, 0:1], rstd[:, 1, 1, j:j + 1],
                                  ALU.subtract, ALU.mult).then_inc(z_ready.sem, 1)

            def z_norm(w):
                await_(dve, f_rstd, w, 1)
                await_(dve, out_stored, w, 0)
                for j in range(TT):
                    dve.tensor_scalar(z[:, j, :], h2[:, j, :], mv[:, 1, j, 0:1], rstd[:, 1, 1, j:j + 1],
                                      ALU.subtract, ALU.mult).then_inc(z_ready.sem, 1)

            def z_turned(w, tiles=range(TT)):
                for j in tiles:
                    low_part(w, ("Z", j), [(zT[:, 1, j], lambda b: b[:, :].rearrange("p (k s) -> p k s", k=KT))],
                             [(zT[:, 0, j], None)], X_SCALE)

            def router_in(w):
                await_(dve, full, w, INDEX[w.seg][("LG",)] + 1)
                parts = of(w, ("LG",))[:, 0:TT * 2 * EXPERTS].rearrange("p (t i e) -> p t i e", t=TT, i=2)
                step(w, dve.scalar_tensor_tensor(out=lg[:, 0], in0=parts[:, :, 0, :], scalar=delta,
                                                 in1=rb[:, :].unsqueeze(1).broadcast_to([P, TT, EXPERTS]), op0=ALU.mult, op1=ALU.add))
                dve.scalar_tensor_tensor(out=lg[:, 0], in0=parts[:, :, 1, :], scalar=delta, in1=lg[:, 0],
                                         op0=ALU.mult, op1=ALU.add).then_inc(free.sem, 1)
                await_(dve, free, w, INDEX[w.seg][("LG",)] + 1)
                step(w, dve.tensor_reduce(small[:, 0, :], lg[:, 0], AX_X, ALU.max))
                dve.tensor_tensor(lg[:, 0], lg[:, 0], small[:, 0, :].unsqueeze(2).broadcast_to([P, TT, EXPERTS]),
                                  ALU.subtract).then_inc(lg_in.sem, 1)

            def router_out(w):
                await_(dve, lg_exp, w, 1)
                step(w, dve.tensor_reduce(small[:, 1, :], lg[:, 1], AX_X, ALU.add))
                step(w, dve.reciprocal(small[:, 2, :], small[:, 1, :]))
                step(w, dve.tensor_tensor(lg[:, 2], lg[:, 1], small[:, 2, :].unsqueeze(2).broadcast_to([P, TT, EXPERTS]), ALU.mult), apart=True)
                for j in range(TT):
                    ins = dve.max(out=top[:, j, :], in_=lg[:, 2, j, :])
                step(w, ins, apart=True)
                for j in range(TT):
                    ins = dve.match_replace(out=lg[:, 3, j, :], in_to_replace=top[:, j, :], in_values=lg[:, 2, j, :], imm_value=-1.0)
                step(w, ins)
                step(w, dve.tensor_scalar(lg[:, 3], lg[:, 3], 0.0, None, ALU.max, ALU.bypass))
                step(w, dve.tensor_tensor(lg[:, 0], lg[:, 2], lg[:, 3], ALU.subtract))
                step(w, dve.tensor_scalar(w_hi[:, :, :], lg[:, 0], P_SCALE, None, ALU.mult, ALU.bypass))
                dve.tensor_copy(w_parts[:, :, 0, :], w_hi[:, :, :])
                dve.scalar_tensor_tensor(out=w_parts[:, :, 1, :], in0=lg[:, 0], scalar=P_SCALE, in1=w_hi[:, :, :],
                                         op0=ALU.mult, op1=ALU.subtract).then_inc(w_ready.sem, 1)
                step(w, dve.tensor_reduce(small[:, 3, :], lg[:, 0], AX_X, ALU.add))
                for j in range(TT):
                    ins = dve.scalar_tensor_tensor(out=h2[:, j, :], in0=z[:, j, :], scalar=small[:, 3, j:j + 1], in1=h2[:, j, :],
                                                   op0=ALU.mult, op1=ALU.add)
                step(w, ins)

            def weights_turned(w):
                await_(dve, full, w, INDEX[w.seg][("WT",)] + 1)
                dve.tensor_copy(wT[:, :, :], of(w, ("WT",))[:, 0:TT * P].rearrange("p (t s) -> p t s", t=TT)).then_inc(free.sem, 1)

            def finish(w):
                for j in range(TT):
                    await_(dve, full, w, INDEX[w.seg][("EB", j)] + 1)
                    dve.scalar_tensor_tensor(out=z[:, j, :], in0=of(w, ("EB", j))[:, :], scalar=gamma, in1=h2[:, j, :],
                                             op0=ALU.mult, op1=ALU.add).then_inc(free.sem, 1)
                if w.seg == "tail":
                    return
                await_(dve, free, w, INDEX[w.seg][("EB", TT - 1)] + 1)
                dve.tensor_copy(small[:, 0, :], small[:, 1, :]).then_inc(out_ready.sem, 1)

            def lead(w):
                steps[0] = 0
                h_stats(w)
                x_norm(w)
                xx(w)
                for j in range(QPG + 1):
                    project(w, 0, j)
                assert steps[0] == vec.n["lead"]

            def body(w):
                steps[0] = 0
                for g in range(NKV):
                    mask_max(w, g, 0)
                    mask_max(w, g, 1)
                    made = g < NKV - 1 or w.next
                    if made:
                        project(w, g + 1, 0)
                    reciprocals(w, g, 0)
                    if made:
                        project(w, g + 1, 1)
                    reciprocals(w, g, 1)
                    if g == 1 and w.prev:
                        residual(w)
                    if made:
                        for j in range(2, QPG + 1):
                            project(w, g + 1, j)
                    if g == 3 and w.prev:
                        router_out(w)
                    if g == 2 and w.next:
                        x_norm(w)
                    if g == 0:
                        for t in range(TT):
                            low_part(w, ("V", t), [(V[:, 1, t, :], lambda b: b[:, :])], [(V[:, 0, t, :], None)], QKV_EVAC)
                    for i in range(4):
                        low_part(w, ("T", g, i), [(probs_out(1, i), lambda b: probs_in(b, i))], [(probs_out(0, i), None)], P_SCALE)
                    if g == 1 and w.prev:
                        z_norm(w)
                    if g == 2 and w.prev:
                        z_turned(w)
                    if g == 3 and w.prev:
                        weights_turned(w)
                    for b2 in range(2):
                        for r2 in range(2):
                            o = [oT[:, i, 2 * r2:2 * r2 + 2, b2 * SEQ:(b2 + 1) * SEQ] for i in range(2)]
                            low_part(w, ("D", g, b2, r2), [(o[1], lambda b: b[:, 0:PT].rearrange("p (h s) -> p h s", h=2))],
                                     [(o[0], None)], OUT_EVAC, banks_of(w, g, b2, r2))
                    if g == 1 and w.next:
                        h_stats(w)
                    if g == 2 and w.prev:
                        router_in(w)
                    if g == 2 and w.next:
                        xx(w)
                    if g == 3 and w.prev:
                        finish(w)

            def tail(w):
                steps[0] = 0
                await_(dve, hr_in, w, 0)
                await_(dve, out_ready, w, 0)
                add_tile(w, 0)
                add_tile(w, 1)
                await_(dve, out_stored, w, 0)
                norm_tile(w, 0)
                norm_tile(w, 1)
                add_tile(w, 2)
                z_turned(w, (0, 1))
                norm_tile(w, 2)
                z_turned(w, (2,))
                router_in(w)
                router_out(w)
                weights_turned(w)
                finish(w)
                assert steps[0] == vec.n["tail"]

            bodies(dve, lead, body, tail)


def ring_start(w):
    at, n = 0, {}
    for seg in SEGMENTS:
        n[seg] = at
        at = (at + len(TASKS[seg])) % RING
    assert len(TASKS["mid"]) % RING == 0
    return n[w.seg]


_INS = ["x", "L0_tok_log_dt", "L0_tok_B_ri", "L0_tok_inv_A_real", "L0_tok_A_imag", "L0_attn_weight_qkv",
        "L0_attn_weight_proj", "L0_ffn_router_weight", "L0_ffn_router_bias", "L0_ffn_expert_bias"]


def kernel(**inputs):
    import concourse.bacc as _bacc
    from concourse.bass_utils import run_bass_kernel_spmd as _run

    nc = _bacc.Bacc("TRN2", target_bir_lowering=False, num_devices=1)
    arrays, args = {}, []
    for name in _INS:
        a = np.ascontiguousarray(inputs[name])
        arrays[f"in_{name}"] = a
        args.append(nc.dram_tensor(f"in_{name}", a.shape, mybir.dt.from_np(a.dtype), kind="ExternalInput").ap())
    arrays["shape_constants"] = shape_constants()
    args.append(nc.dram_tensor("shape_constants", (P, NCONST), F32, kind="ExternalInput").ap())
    out = nc.dram_tensor("out", (BATCH, SEQ, HID), F32, kind="ExternalOutput").ap()
    vit_tower(nc, *args, out)
    r = _run(nc, [arrays], core_ids=[0])
    return r.results[0]["out"]
```
